# Optimizing a Trainium2 kernel written in Bass

```python
import numpy as np
import jax
import jax.numpy as jnp

def _softmax(x, axis=-1):
    return jax.nn.softmax(x, axis=axis)

def _gelu(x):
    return jax.nn.gelu(x, approximate=True)

def _silu(x):
    return jax.nn.silu(x)

def _sigmoid(x):
    return jax.nn.sigmoid(x)

def _layernorm(x, axis=-1, eps=1e-05):
    m = jnp.mean(x, axis=axis, keepdims=True)
    v = jnp.var(x, axis=axis, keepdims=True)
    return (x - m) / jnp.sqrt(v + eps)

def _scatter_add(tgt, idx, src, axis=0):
    return tgt.at[idx].add(src)

def _segment_sum(src, seg, n):
    return jax.ops.segment_sum(src, seg, n)
kernel_name = 'mk_gnn_preln_d2_gnn_r8_34df1c'

def setup_inputs(seed: int=0):
    np.random.seed(seed)
    _w = jnp.asarray

    def _rec_inputs():
        import jax
        import jax.numpy as jnp
        _gk = jax.random.key(seed)
        x = -0.0003713 + 1 * jax.random.normal(jax.random.fold_in(_gk, 1), (12500, 128), jnp.float32)
        src = jax.random.randint(jax.random.fold_in(_gk, 2), (200000,), 0, 12500, jnp.int32)
        dst = jnp.minimum((12500 * jax.random.uniform(jax.random.fold_in(_gk, 3), (200000,)) ** 2.0).astype(jnp.int32), 99999)
        _o = jnp.argsort(dst, stable=True)
        src = src[_o]
        dst = dst[_o]
        edge_attr_128 = 0.00013283 + 1.0001 * jax.random.normal(jax.random.fold_in(_gk, 12), (200000, 128), jnp.float32)
        edge_weight1 = jax.random.uniform(jax.random.fold_in(_gk, 14), (200000, 1), jnp.float32, 0.0, 0.999998)
        return (x, src, dst, edge_attr_128, edge_weight1)
    x, src, dst, edge_attr_128, edge_weight1 = _rec_inputs()

    def _L0_gnn_setup():
        import jax, jax.numpy as jnp
        import numpy as np
        N_NODES = 12500
        N_EDGES = 200000
        D = 128
        key = jax.random.key(seed)
        ks = jax.random.split(key, 6)
        feat = jax.random.normal(ks[0], (N_NODES, D), dtype=jnp.float32)
        src = jax.random.randint(ks[1], (N_EDGES,), 0, N_NODES, dtype=jnp.int32)
        dst = jax.random.randint(ks[2], (N_EDGES,), 0, N_NODES, dtype=jnp.int32)
        eps = jnp.zeros((1,), dtype=jnp.float32)
        scale = 1.0 / np.sqrt(D)
        W1 = jax.random.normal(ks[3], (D, D), dtype=jnp.float32) * scale
        b1 = jnp.zeros((D,), dtype=jnp.float32)
        W2 = jax.random.normal(ks[4], (D, D), dtype=jnp.float32) * scale
        b2 = jnp.zeros((D,), dtype=jnp.float32)
        return {'feat': feat, 'src': src, 'dst': dst, 'eps': eps, 'W1': W1, 'b1': b1, 'W2': W2, 'b2': b2}
    _L0_gnn_all = _L0_gnn_setup()
    _L0_gnn_in = {k: v for k, v in _L0_gnn_all.items() if k in ('eps', 'W1', 'b1', 'W2', 'b2')}
    del _L0_gnn_all

    def _L1_gnn_setup():
        import jax, jax.numpy as jnp
        import numpy as np
        N_NODES = 12500
        N_EDGES = 75000
        D = 128
        DE = 128
        EPS_LN = 1e-05
        EPS_SM = 1e-16
        key = jax.random.key(seed)
        ks = jax.random.split(key, 12)
        x = jax.random.normal(ks[0], (N_NODES, D), jnp.float32)
        edge_index = jax.random.randint(ks[1], (2, N_EDGES), 0, N_NODES, dtype=jnp.int64)
        edge_type = jax.random.uniform(ks[2], (N_EDGES, 1), jnp.float32)
        edge_vector = jax.random.normal(ks[3], (N_EDGES, DE), jnp.float32)
        s_t = 1.0 / np.sqrt(D + DE)
        s = 1.0 / np.sqrt(D)
        Wt = jax.random.normal(ks[4], (D + DE, D), jnp.float32) * s_t
        bt = jnp.zeros((D,), jnp.float32)
        Wq = jax.random.normal(ks[5], (D, D), jnp.float32) * s
        bq = jnp.zeros((D,), jnp.float32)
        Wk = jax.random.normal(ks[6], (D, D), jnp.float32) * s
        bk = jnp.zeros((D,), jnp.float32)
        Wv = jax.random.normal(ks[7], (D, D), jnp.float32) * s
        bv = jnp.zeros((D,), jnp.float32)
        gamma = jnp.ones((D,), jnp.float32)
        beta = jnp.zeros((D,), jnp.float32)
        return {'x': x, 'edge_index': edge_index, 'edge_type': edge_type, 'edge_vector': edge_vector, 'gamma': gamma, 'beta': beta, 'Wt': Wt, 'bt': bt, 'Wq': Wq, 'bq': bq, 'Wk': Wk, 'bk': bk, 'Wv': Wv, 'bv': bv}
    _L1_gnn_all = _L1_gnn_setup()
    _L1_gnn_in = {k: v for k, v in _L1_gnn_all.items() if k in ('gamma', 'beta', 'Wt', 'bt', 'Wq', 'bq', 'Wk', 'bk', 'Wv', 'bv')}
    del _L1_gnn_all
    return {'x': x, 'src': src, 'dst': dst, 'edge_attr_128': edge_attr_128, 'edge_weight1': edge_weight1, 'L0_gnn_eps': _L0_gnn_in['eps'], 'L0_gnn_W1': _L0_gnn_in['W1'], 'L0_gnn_b1': _L0_gnn_in['b1'], 'L0_gnn_W2': _L0_gnn_in['W2'], 'L0_gnn_b2': _L0_gnn_in['b2'], 'L1_gnn_gamma': _L1_gnn_in['gamma'], 'L1_gnn_beta': _L1_gnn_in['beta'], 'L1_gnn_Wt': _L1_gnn_in['Wt'], 'L1_gnn_bt': _L1_gnn_in['bt'], 'L1_gnn_Wq': _L1_gnn_in['Wq'], 'L1_gnn_bq': _L1_gnn_in['bq'], 'L1_gnn_Wk': _L1_gnn_in['Wk'], 'L1_gnn_bk': _L1_gnn_in['bk'], 'L1_gnn_Wv': _L1_gnn_in['Wv'], 'L1_gnn_bv': _L1_gnn_in['bv']}

def reference(x, src, dst, edge_attr_128, edge_weight1, L0_gnn_eps, L0_gnn_W1, L0_gnn_b1, L0_gnn_W2, L0_gnn_b2, L1_gnn_gamma, L1_gnn_beta, L1_gnn_Wt, L1_gnn_bt, L1_gnn_Wq, L1_gnn_bq, L1_gnn_Wk, L1_gnn_bk, L1_gnn_Wv, L1_gnn_bv):
    import jax
    import jax.numpy as jnp

    def _L0_gnn_ref(feat, src, dst, eps, W1, b1, W2, b2):
        import jax, jax.numpy as jnp
        import numpy as np
        N_NODES = 12500
        N_EDGES = 200000
        D = 128
        msgs = feat[src]
        neigh = jax.ops.segment_sum(msgs, dst, num_segments=N_NODES)
        rst = (1.0 + eps[0]) * feat + neigh
        h = jax.nn.relu(rst @ W1 + b1)
        h = h @ W2 + b2
        return jax.nn.relu(h)

    def _L1_gnn_ref(x, edge_index, edge_type, edge_vector, gamma, beta, Wt, bt, Wq, bq, Wk, bk, Wv, bv):
        import jax, jax.numpy as jnp
        import numpy as np
        N_NODES = 12500
        N_EDGES = 75000
        D = 128
        DE = 128
        EPS_LN = 1e-05
        EPS_SM = 1e-16
        d_sqrt = jnp.sqrt(jnp.asarray(D, x.dtype))
        residual = x
        mu = jnp.mean(x, axis=-1, keepdims=True)
        var = jnp.var(x, axis=-1, keepdims=True)
        h = (x - mu) / jnp.sqrt(var + EPS_LN) * gamma + beta
        src, dst = (edge_index[0], edge_index[1])
        x_j = h[src]
        x_i = h[dst]
        t = jax.nn.gelu(jnp.concatenate([x_j, edge_vector], axis=1) @ Wt + bt, approximate=False)
        q = x_i @ Wq + bq
        k = t @ Wk + bk
        attn = jnp.sum(k * q, axis=-1, keepdims=True)
        attn = attn * edge_type / d_sqrt
        m = jax.ops.segment_max(attn, dst, num_segments=N_NODES)
        e = jnp.exp(attn - m[dst])
        s = jax.ops.segment_sum(e, dst, num_segments=N_NODES)
        a = e / (s[dst] + EPS_SM)
        msg = a * (t @ Wv + bv)
        aggr = jax.ops.segment_sum(msg, dst, num_segments=N_NODES)
        return residual + jax.nn.gelu(aggr, approximate=False)
    edge_index = jnp.stack([src, dst])
    h = jnp.maximum(_layernorm(x, axis=-1), 0.0)
    x = x + _L0_gnn_ref(h, src, dst, L0_gnn_eps, L0_gnn_W1, L0_gnn_b1, L0_gnn_W2, L0_gnn_b2)
    h = jnp.maximum(_layernorm(x, axis=-1), 0.0)
    x = x + _L1_gnn_ref(h, edge_index, edge_weight1, edge_attr_128, L1_gnn_gamma, L1_gnn_beta, L1_gnn_Wt, L1_gnn_bt, L1_gnn_Wq, L1_gnn_bq, L1_gnn_Wk, L1_gnn_bk, L1_gnn_Wv, L1_gnn_bv)
    return x

_drawn_inputs = setup_inputs


def setup_inputs(seed=0):
    import zlib

    import numpy as np

    out = dict(_drawn_inputs(seed))
    spreads = {'L0_gnn_b1': (0.0, 0.8),
     'L0_gnn_b2': (0.0, 0.609),
     'L1_gnn_gamma': (1.0, 0.6),
     'L1_gnn_beta': (0.0, 0.8),
     'L1_gnn_bt': (0.0, 0.8),
     'L1_gnn_bq': (0.0, 0.8),
     'L1_gnn_bk': (0.0, 2.0),
     'L1_gnn_bv': (0.0, 0.8)}
    factors = {'edge_attr_128': 4.338, 'edge_weight1': 8.0, 'L1_gnn_Wq': 8.0, 'L1_gnn_Wk': 8.0}
    for name, (base, spread) in spreads.items():
        noise = np.random.default_rng([zlib.crc32(name.encode()), seed]).standard_normal(out[name].shape)
        drawn = base * np.exp(spread * noise) if base else spread * noise
        out[name] = jnp.asarray(drawn.astype(out[name].dtype))
    for name, factor in factors.items():
        out[name] = (out[name] * factor).astype(out[name].dtype)
    return out
```

```python
from contextlib import ExitStack

import numpy as np

import concourse.bass as bass
from concourse import mybir
from concourse.alu_op_type import AluOpType as ALU

F32 = mybir.dt.float32
I32 = mybir.dt.int32
ACT = mybir.ActivationFunctionType
AX = mybir.AxisListType

P = 128
D = 128
N = 12500
E = 200000
WIN = 40
SUB = 2
BLOCK = P * SUB
BPC = 8
CHUNK = BPC * BLOCK
COLS = BPC * SUB
NCH = -(-E // CHUNK)
NBLK = NCH * BPC
QUADS = COLS // 4
CW = BPC * WIN
BIG = 1e30
TILES = -(-(N + WIN) // P)
NP = TILES * P
GT = 7
GROUPS = TILES // GT
GN = GT * P
HALF = GN // 2
PB = 112
KB = NBLK // PB
LN_EPS = 1e-5
SM_EPS = 1e-16
TAIL = E - (NCH - 1) * CHUNK
TAIL_BLOCKS = TAIL // BLOCK
TAIL_PARTS = (TAIL - TAIL_BLOCKS * BLOCK) // SUB
assert TILES % (2 * GT) == 0 and NBLK % PB == 0 and NCH % 2 == 0 and TAIL % SUB == 0 and HALF <= 512


def wait(eng, sem, value):
    if isinstance(value, int) and value <= 0:
        return
    eng.wait_ge(sem, value)


def over_chunks(eng, step):
    step((0, 0, 0), None)
    step((1, 0, 1), (0, 0, 0))
    with eng.Fori(0, (NCH - 2) // 2) as i:
        step((2 * i + 2, i + 1, 0), (2 * i + 1, i, 1))
        step((2 * i + 3, i + 1, 1), (2 * i + 2, i + 1, 0))
    step(None, (NCH - 1, (NCH - 2) // 2, 1))


def bcast_mid(ap, shape):
    return ap.unsqueeze(2).to_broadcast(shape)


def build_gnn(nc, a):
    with ExitStack() as ctx:
        def sb(name, shape, dt=F32):
            return ctx.enter_context(nc.sbuf_tensor(name, shape, dt))

        h0 = nc.dram_tensor("h0_rows", [NP, D], F32, kind="Internal").ap()
        res = nc.dram_tensor("residual_rows", [NP, D], F32, kind="Internal").ap()
        arow = nc.dram_tensor("source_rows", [NP, D], F32, kind="Internal").ap()
        qk = nc.dram_tensor("qk_cols", [D, NP], F32, kind="Internal").ap()
        ck = nc.dram_tensor("qk_bias_cols", [1, NP], F32, kind="Internal").ap()

        low = nc.dram_tensor("low_row", [1, NBLK], F32, kind="Internal").ap()

        g = {
            "acc": sb("acc", [P, NP]),
            "ident": sb("ident", [P, P]),
            "ones": sb("ones", [P, P]),
            "iota": sb("iota", [P, WIN]),
            "dst": sb("dst", [P, NBLK, SUB]),
            "rel": sb("rel", [P, NBLK, SUB]),
            "start": sb("start", [1, NBLK]),
            "capped": sb("capped", [1, NBLK]),
            "base": sb("base", [1, NBLK], I32),
            "span": sb("span", [1, 1], I32),
            "eps1": sb("eps1", [P, 1]),
            "spare": sb("spare", [1, 1]),
        }
        constants(nc, a, g)
        node_norm(nc, a, g, h0)
        edge_tables(nc, a, g, low)
        span = nc.values_load(g["span"][0:1, 0:1], min_val=0, max_val=N)
        gin_sweeps(nc, a, g, h0, low, span)
        node_mid(nc, a, g, res, arow, qk, ck)
        with nc.sbuf_tensor("rows", [33, NP], F32) as rows:
            g["rows"] = rows
            attention_sweeps(nc, a, g, arow, qk, ck, low, span)
            node_end(nc, a, g, res)


class Stage:

    def __init__(self, nc, ctx, name):
        self.nc, self.ctx, self.name, self.sems = nc, ctx, name, []

    def sb(self, name, shape, dt=F32):
        return self.ctx.enter_context(self.nc.sbuf_tensor(f"{self.name}_{name}", shape, dt))

    def two(self, name, shape, dt=F32):
        return [self.sb(f"{name}{j}", shape, dt) for j in range(2)]

    def ps(self, name, shape=(P, 512)):
        return self.ctx.enter_context(self.nc.psum_tensor(f"{self.name}_{name}", list(shape), F32))

    def sem(self, name):
        s = self.ctx.enter_context(self.nc.semaphore(f"{self.name}_{name}"))
        self.sems.append(s)
        return s

    def sem2(self, name):
        return [self.sem(f"{name}_{j}") for j in range(2)]

    def clear(self):
        self.nc.all_engine_barrier()
        for s in self.sems:
            self.nc.sync.sem_clear(s)
        self.nc.all_engine_barrier()


def constants(nc, a, g):
    with ExitStack() as ctx:
        st = Stage(nc, ctx, "constants")
        iota_i = st.sb("iota_i", [P, WIN], I32)
        zeroed, identity_ready, iota_ready = st.sem("zeroed"), st.sem("identity_ready"), st.sem("iota_ready")
        eps_in, ones_ready, float_ready = st.sem("eps_in"), st.sem("ones_ready"), st.sem("float_ready")
        block = ctx.enter_context(nc.Block())

        @block.sync
        def _(sp):
            sp.dma_start(g["eps1"][:, :], a["eps"].to_broadcast([P, 1])).then_inc(eps_in, 16)

        @block.gpsimd
        def _(gp):
            gp.memset(g["ident"][:, :], 0.0).then_inc(zeroed, 1)
            gp.iota(iota_i[:, :], pattern=[[1, WIN]], base=0, channel_multiplier=0).then_inc(iota_ready, 1)
            gp.wait_ge(zeroed, 1)
            gp.affine_select(out=g["ident"][:, :], in_=g["ident"][:, :], compare_op=ALU.not_equal, fill=1.0,
                             base=0, pattern=[[-1, P]], channel_multiplier=1).then_inc(identity_ready, 1)
            gp.wait_ge(identity_ready, 1)

        @block.vector
        def _(v):
            v.memset(g["ones"][:, :], 1.0).then_inc(ones_ready, 1)
            v.wait_ge(iota_ready, 1)
            v.tensor_copy(g["iota"][:, :], iota_i[:, :]).then_inc(float_ready, 1)
            v.wait_ge(eps_in, 16)
            v.tensor_scalar(g["eps1"][:, :], g["eps1"][:, :], 1.0, None, ALU.add).then_inc(float_ready, 1)
            v.wait_ge(float_ready, 2)
            v.wait_ge(ones_ready, 1)


NORM_STEPS = ("stats", "held", "means", "var", "std", "rstd", "shift")


def norm_steps(st, name):
    return {**{k: st.sem(f"{name}_{k}") for k in NORM_STEPS}, "spare": st.sb(name + "_spare", [1, 1])}


def norm_moments(v, x, m, s, G):
    for t in range(GT):
        v.bn_stats(m["stats"][:, t, :], x[:, t, :]).then_inc(s["stats"], 1)
    wait(v, s["stats"], (G + 1) * GT)
    wait(v, s["held"], G)
    v.tensor_tensor(s["spare"][:, :], m["eps"][0:1, 0:1], m["eps"][0:1, 0:1], ALU.mult).then_inc(s["held"], 1)
    for t in range(GT):
        v.bn_aggr(m["mv"][:, t, :], m["stats"][:, t, :]).then_inc(s["means"], 1)
    wait(v, s["means"], (G + 1) * GT)
    v.tensor_scalar(m["var"][:, :], m["mv"][:, :, 1], LN_EPS, None, ALU.add).then_inc(s["var"], 1)


def norm_root(act, m, s, G):
    wait(act, s["var"], G + 1)
    wait(act, s["rstd"], G - 1)
    act.activation(m["std"][:, :], m["var"][:, :], ACT.Sqrt).then_inc(s["std"], 1)


def norm_scales(v, m, s, G):
    wait(v, s["std"], G + 1)
    v.reciprocal(m["rstd"][:, :], m["std"][:, :]).then_inc(s["rstd"], 1)
    wait(v, s["rstd"], G + 1)
    v.scalar_tensor_tensor(out=m["shift"][:, :], in0=m["mv"][:, :, 0], scalar=-1.0, in1=m["rstd"][:, :],
                           op0=ALU.mult, op1=ALU.mult).then_inc(s["shift"], 1)


def norm_buffers(st, g):
    return [{"stats": st.sb(f"stats{u}", [P, GT, 6]), "mv": st.sb(f"mv{u}", [P, GT, 2]), "eps": g["eps1"],
             **{k: st.sb(f"{k}{u}", [P, GT]) for k in ("var", "std", "rstd", "shift")}} for u in range(2)]


def node_norm(nc, a, g, h0):
    with ExitStack() as ctx:
        st = Stage(nc, ctx, "node_norm")
        x, h = st.two("x", [P, GT, D]), st.two("h", [P, GT, D])
        m = norm_buffers(st, g)
        hT = [st.ps(f"hT{u}", (P, 1024)) for u in range(2)]
        x_in, h_out = st.sem2("x_in"), st.sem2("h_out")
        s = norm_steps(st, "n")
        h_ready, hT_ready, acc_ready = st.sem("h_ready"), st.sem("hT_ready"), st.sem("acc_ready")
        x_rows = a["x"].rearrange("(g t p) d -> g p t d", t=GT, p=P)
        h_rows = h0.rearrange("(g t p) d -> g p t d", t=GT, p=P)
        st.clear()
        block = ctx.enter_context(nc.Block())

        def pairs(eng, step):
            for u in range(2):
                step(u, 0, u)
            with eng.Fori(1, GROUPS // 2) as i:
                for u in range(2):
                    step(2 * i + u, i, u)

        @block.sync
        def _(sp):
            def step(G, i, u):
                wait(sp, h_ready, (G - 1) * GT)
                sp.dma_start(x[u][:, :, :], x_rows[bass.ds(G, 1)].rearrange("a p t d -> p (a t) d")).then_inc(x_in[u], 16)
            pairs(sp, step)

        @block.vector
        def _(v):
            def moments(G, i, u):
                wait(v, x_in[u], 16 * (i + 1))
                norm_moments(v, x[u], m[u], s, G)

            def scales(G, i, u):
                wait(v, h_ready, (G - 1) * GT)
                norm_scales(v, m[u], s, G)
            for f in (moments, scales):
                for u in range(2):
                    f(u, 0, u)
            with v.Fori(1, GROUPS // 2) as i:
                for f in (moments, scales):
                    for u in range(2):
                        f(2 * i + u, i, u)

        @block.scalar
        def _(act):
            def root(G, i, u):
                norm_root(act, m[u], s, G)

            def scale(G, i, u):
                wait(act, s["shift"], G + 1)
                wait(act, h_out[u], 16 * i)
                wait(act, hT_ready, G - 1)
                for t in range(GT):
                    act.activation(h[u][:, t, :], x[u][:, t, :], ACT.Relu, bias=m[u]["shift"][:, t:t + 1],
                                   scale=m[u]["rstd"][:, t:t + 1]).then_inc(h_ready, 1)

            def keep(G, i, u):
                wait(act, h_ready, (G + 1) * GT)
                act.dma_start(h_rows[bass.ds(G, 1)].rearrange("a p t d -> p (a t) d"), h[u][:, :, :]).then_inc(h_out[u], 16)
                wait(act, hT_ready, G + 1)
                act.activation(g["acc"][:, bass.ds(G * GN, GN)], hT[u][:, 0:GN], ACT.Copy,
                               scale=g["eps1"][:, 0:1]).then_inc(acc_ready, 1)
            def both(i, first):
                for f in (root, scale, keep):
                    for u in range(2):
                        f(2 * i + u if not first else u, i, u)
            both(0, True)
            with act.Fori(1, GROUPS // 2) as i:
                both(i, False)
            for u in range(2):
                act.wait_ge(h_out[u], 16 * (GROUPS // 2))
            act.wait_ge(acc_ready, GROUPS)

        @block.tensor
        def _(pe):
            def step(G, i, u):
                wait(pe, h_ready, (G + 1) * GT)
                wait(pe, acc_ready, G - 1)
                for t in range(GT):
                    mm = pe.transpose(hT[u][:, t * P:(t + 1) * P], h[u][:, t, :], g["ident"][:, :])
                mm.then_inc(hT_ready, 1)
            pairs(pe, step)


def edge_tables(nc, a, g, low_row):
    with ExitStack() as ctx:
        st = Stage(nc, ctx, "edge")
        by_block = st.sb("by_block", [PB, KB, BLOCK], I32)
        by_edge = st.sb("by_edge", [P, NBLK, SUB], I32)
        low, high = st.sb("low_p", [PB, KB]), st.sb("high_p", [PB, KB])
        wide, widest = st.sb("wide", [PB, KB]), st.sb("widest", [PB, 1])
        low_sb = st.sb("low_sb", [1, NBLK])
        lowT, wideT = st.ps("lowT", (P, 1024)), st.ps("wideT")
        dst_in, blocks_in = st.sem("dst_in"), st.sem("blocks_in")
        ends_ready, wide_ready, widest_ready = st.sem("ends_ready"), st.sem("wide_ready"), st.sem("widest_ready")
        rows_ready, tables_ready, low_out = st.sem("rows_ready"), st.sem("tables_ready"), st.sem("low_out")
        st.clear()
        block = ctx.enter_context(nc.Block())

        @block.sync
        def _(sp):
            sp.dma_start(by_block[:, :, :], a["dst_blocks"].rearrange("(k p) e -> p k e", p=PB)).then_inc(blocks_in, 16)
            sp.dma_start(by_edge[:, :, :], a["dst_cols"].rearrange("p (b s) -> p b s", s=SUB)).then_inc(dst_in, 16)
            sp.wait_ge(tables_ready, 4)
            sp.dma_start(low_row, low_sb[:, :]).then_inc(low_out, 16)
            sp.wait_ge(low_out, 16)

        @block.vector
        def _(v):
            v.wait_ge(blocks_in, 16)
            v.tensor_reduce(low[:, :], by_block[:, :, :], AX.X, ALU.min).then_inc(ends_ready, 1)
            v.tensor_reduce(high[:, :], by_block[:, :, :], AX.X, ALU.max).then_inc(ends_ready, 1)
            v.wait_ge(ends_ready, 2)
            v.tensor_tensor(wide[:, :], high[:, :], low[:, :], ALU.subtract).then_inc(wide_ready, 1)
            v.wait_ge(wide_ready, 1)
            v.tensor_reduce(widest[:, :], wide[:, :], AX.X, ALU.max).then_inc(widest_ready, 1)
            v.wait_ge(dst_in, 16)
            v.tensor_copy(g["dst"][:, :, :], by_edge[:, :, :]).then_inc(tables_ready, 1)
            v.wait_ge(rows_ready, 1)
            for half in range(2):
                n = min(KB - 4 * half, 4) * PB
                v.tensor_copy(low_sb[0:1, 4 * PB * half:4 * PB * half + n],
                              lowT[0:1, 512 * half:512 * half + n]).then_inc(tables_ready, 1)
            v.tensor_reduce(g["span"][0:1, 0:1], wideT[0:1, 0:PB], AX.X, ALU.max).then_inc(tables_ready, 1)
            v.wait_ge(tables_ready, 4)

        @block.tensor
        def _(pe):
            pe.wait_ge(widest_ready, 1)
            for k in range(KB):
                at = 512 * (k // 4) + PB * (k % 4)
                pe.matmul(lowT[0:1, at:at + PB], low[:, k:k + 1], g["ident"][0:PB, 0:PB], start=True, stop=True)
            pe.matmul(wideT[0:1, 0:PB], widest[:, 0:1], g["ident"][0:PB, 0:PB],
                      start=True, stop=True).then_inc(rows_ready, 1)


def first_windows(nc, g, low_row, name):
    with nc.semaphore(name) as copied, nc.Block() as block:
        @block.sync
        def _(sp):
            sp.dma_start(g["start"][:, :], low_row).then_inc(copied, 16)
            sp.wait_ge(copied, 16)


def next_windows(nc, g, st, s):
    bank = s["bank"]
    half = NBLK // 2
    with nc.Block() as block:
        @block.vector
        def _(v):
            v.tensor_scalar(g["capped"][:, :], g["start"][:, :], float(N), None, ALU.min).then_inc(s["capped"], 1)
            v.wait_ge(s["capped"], 1)
            v.tensor_copy(g["base"][:, :], g["capped"][:, :]).then_inc(s["tables"], 1)
            v.tensor_scalar(g["start"][:, :], g["start"][:, :], float(WIN), None, ALU.add).then_inc(s["tables"], 1)
            v.wait_ge(s["spread"], 2)
            for k in range(2):
                v.tensor_tensor(g["rel"][:, k * half:(k + 1) * half, :], g["dst"][:, k * half:(k + 1) * half, :],
                                bank[k][:, 0:half].unsqueeze(2).to_broadcast([P, half, SUB]),
                                ALU.subtract).then_inc(s["tables"], 1)
            v.wait_ge(s["tables"], 4)

        @block.tensor
        def _(pe):
            pe.wait_ge(s["capped"], 1)
            for k in range(2):
                pe.matmul(bank[k][:, 0:half], g["ones"][0:1, :], g["capped"][0:1, k * half:(k + 1) * half],
                          start=True, stop=True).then_inc(s["spread"], 1)


def onehot_op(v, g, out, c):
    rel = g["rel"][:, bass.ds(c * BPC, BPC), :].rearrange("p b s -> p (b s)")
    return v.tensor_tensor(out[:, :, :], g["iota"][:, :].unsqueeze(1).to_broadcast([P, COLS, WIN]),
                           rel.unsqueeze(2).to_broadcast([P, COLS, WIN]), ALU.is_equal)


def load_bases(eng, regs, g, c):
    eng.load(regs, g["base"][0:1, bass.ds(c * BPC, BPC)])


def window(eng, reg):
    return eng.snap(reg, min_val=0, max_val=N)


def hold(gp, g, held, c):
    wait(gp, held, c)
    gp.tensor_tensor(g["spare"][0:1, 0:1], g["ones"][0:1, 0:1], g["ones"][0:1, 0:1], ALU.mult).then_inc(held, 1)


def gather_chunk(gp, idx, rows, out, done):
    for k in range(COLS):
        gp.indirect_dma_start(out=out[:, k, :], out_offset=None, in_=rows[:, :],
                              in_offset=bass.IndirectOffsetOnAxis(ap=idx[:, k:k + 1], axis=0)).then_inc(done, 16)


def gin_sweeps(nc, a, g, h0, low, span):
    with ExitStack() as ctx:
        st = Stage(nc, ctx, "gin")
        idx = st.two("idx", [P, COLS], I32)
        hs = st.two("hs", [P, COLS, D])
        hot = st.two("hot", [P, COLS, WIN])
        sums = [st.ps(f"sums{j}") for j in range(2)]
        held = st.sem("held")
        w = {"bank": [st.ps(f"wbank{j}") for j in range(2)],
             "capped": st.sem("w_capped"), "tables": st.sem("w_tables"), "spread": st.sem("w_spread")}
        idx_in, gathered = st.sem2("idx_in"), st.sem2("gathered")
        hot_ready, sums_ready, added = st.sem("hot_ready"), st.sem("sums_ready"), st.sem("added")
        src = a["src_chunks"]
        dve_regs = [nc.vector.alloc_register(f"gin_win{b}") for b in range(BPC)]
        first_windows(nc, g, low, "copied_gin")
        with nc.Fori(0, span + 1, WIN):
            st.clear()
            next_windows(nc, g, st, w)
            with nc.Block() as block:
                @block.sync
                def _(sp):
                    def step(front, back):
                        if front:
                            c, h, j = front
                            wait(sp, gathered[j], 16 * COLS * h)
                            sp.dma_start(idx[j][:, :], src[bass.ds(c, 1)].rearrange("a p k -> p (a k)")).then_inc(idx_in[j], 16)
                    over_chunks(sp, step)

                @block.gpsimd
                def _(gp):
                    def step(front, back):
                        if front:
                            c, h, j = front
                            wait(gp, idx_in[j], 16 * (h + 1))
                            wait(gp, sums_ready, c - 1)
                            hold(gp, g, held, c)
                            gather_chunk(gp, idx[j], h0, hs[j], gathered[j])
                    over_chunks(gp, step)

                @block.tensor
                def _(pe):
                    def step(front, back):
                        if front:
                            c, h, j = front
                            wait(pe, gathered[j], 16 * COLS * (h + 1))
                            wait(pe, hot_ready, c + 1)
                            wait(pe, added, (c - 1) * BPC)
                            for b in range(BPC):
                                for s in range(SUB):
                                    k = b * SUB + s
                                    mm = pe.matmul(sums[j][:, b * WIN:(b + 1) * WIN], hs[j][:, k, :], hot[j][:, k, :],
                                                   start=(s == 0), stop=(s == SUB - 1))
                            mm.then_inc(sums_ready, 1)
                    over_chunks(pe, step)

                @block.vector
                def _(v):
                    def step(front, back):
                        if front:
                            c, h, j = front
                            wait(v, sums_ready, c - 1)
                            onehot_op(v, g, hot[j], c).then_inc(hot_ready, 1)
                        if back:
                            c, h, j = back
                            load_bases(v, dve_regs, g, c)
                            for b in range(BPC):
                                at = window(v, dve_regs[b])
                                if b == 0:
                                    wait(v, sums_ready, c + 1)
                                wait(v, added, c * BPC + b)
                                v.tensor_tensor(g["acc"][:, bass.ds(at, WIN)], g["acc"][:, bass.ds(at, WIN)],
                                                sums[j][:, b * WIN:(b + 1) * WIN], ALU.add).then_inc(added, 1)
                    over_chunks(v, step)
                    v.wait_ge(added, NCH * BPC)


def node_mid(nc, a, g, res, arow, qk, ck):
    with ExitStack() as ctx:
        st = Stage(nc, ctx, "node_mid")
        W = {k: st.sb("w_" + k, [P, D]) for k in ("W1", "W2", "Wt", "Wq", "WkT", "b2", "bt")}
        col = {k: st.sb("c_" + k, [P, 1]) for k in ("b1", "bq", "bk", "gamma", "beta")}
        tiles = {k: st.two("m_" + k, [P, GT, D]) for k in ("x", "u", "y", "x1", "h2", "r", "hn", "hT", "A", "q", "qk")}
        cb = st.two("m_c", [1, GN])
        m = norm_buffers(st, g)
        pa = [st.ps(f"pa{u}", (P, 1024)) for u in range(2)]
        pb = [st.ps(f"pb{u}", (P, 1024)) for u in range(2)]
        weights_in = st.sem("weights_in")
        x_in, r_out, a_out, q_out = st.sem2("x_in"), st.sem2("r_out"), st.sem2("a_out"), st.sem2("q_out")
        s1 = norm_steps(st, "s1")
        s2 = norm_steps(st, "s2")
        names = ("u_ps", "u_sb", "y_ps", "y_sb", "x1", "h2", "r", "hn", "t_ps", "hT", "a_ps", "a_sb",
                 "q_ps", "q_sb", "k_ps", "c_ps", "k_sb", "c_sb")
        s = {k: st.sem("m_" + k) for k in names}
        st.clear()
        block = ctx.enter_context(nc.Block())
        x_rows = a["x"].rearrange("(g t p) d -> g p t d", t=GT, p=P)
        r_rows = res.rearrange("(g t p) d -> g p t d", t=GT, p=P)
        a_rows = arow.rearrange("(g t p) d -> g p t d", t=GT, p=P)
        n_weights = 12
        flat = lambda t: t[:, :, :].rearrange("p t d -> p (t d)")
        one = lambda rows, G: rows[bass.ds(G, 1)].rearrange("a p t d -> p (a t) d")

        def pairs(eng, steps):
            for f in steps:
                for u in range(2):
                    f(u, 0, u)
            with eng.Fori(1, GROUPS // 2) as i:
                for f in steps:
                    for u in range(2):
                        f(2 * i + u, i, u)

        @block.sync
        def _(sp):
            for k in ("W1", "W2", "Wq", "WkT"):
                sp.dma_start(W[k][:, :], a[k]).then_inc(weights_in, 16)
            sp.dma_start(W["Wt"][:, :], a["Wt"][0:D, :]).then_inc(weights_in, 16)
            for k in ("b2", "bt"):
                sp.dma_start(W[k][:, :], a[k].rearrange("(a d) -> a d", a=1).to_broadcast([P, D])).then_inc(weights_in, 16)
            for k in ("b1", "bq", "bk", "gamma", "beta"):
                sp.dma_start(col[k][:, :], a[k].rearrange("(d a) -> d a", a=1)).then_inc(weights_in, 16)

            def load(G, i, u):
                wait(sp, s["x1"], G - 1)
                sp.dma_start(tiles["x"][u][:, :, :], one(x_rows, G)).then_inc(x_in[u], 16)

            def store_r(G, i, u):
                wait(sp, s["r"], G + 1)
                sp.dma_start(one(r_rows, G), tiles["r"][u][:, :, :]).then_inc(r_out[u], 16)

            def store_a(G, i, u):
                wait(sp, s["a_sb"], G + 1)
                sp.dma_start(one(a_rows, G), tiles["A"][u][:, :, :]).then_inc(a_out[u], 16)

            def store_q(G, i, u):
                wait(sp, s["k_sb"], G + 1)
                sp.dma_start(qk[:, bass.ds(G * GN, GN)], flat(tiles["qk"][u])).then_inc(q_out[u], 16)
                wait(sp, s["c_sb"], G + 1)
                sp.dma_start(ck[:, bass.ds(G * GN, GN)], cb[u][:, :]).then_inc(q_out[u], 16)
            pairs(sp, [load, store_r, store_a, store_q])
            for u in range(2):
                sp.wait_ge(r_out[u], 16 * (GROUPS // 2))
                sp.wait_ge(a_out[u], 16 * (GROUPS // 2))
                sp.wait_ge(q_out[u], 32 * (GROUPS // 2))

        @block.tensor
        def _(pe):
            pe.wait_ge(weights_in, 16 * n_weights)

            def halves(out, u, lhsT, rhs, sem):
                for h in range(2):
                    mm = pe.matmul(out[0:lhsT.shape[1], 512 * h:512 * h + HALF], lhsT, rhs(h), start=True, stop=True)
                mm.then_inc(sem, 1)

            def by_tile(out, lhs, rhs, sem):
                for t in range(GT):
                    mm = pe.matmul(out[:, t * P:(t + 1) * P], lhs[:, t, :], rhs[:, :], start=True, stop=True)
                mm.then_inc(sem, 1)

            def first(G, i, u):
                wait(pe, s["c_sb"], G - 1)
                halves(pa[u], u, W["W1"][:, :], lambda h: g["acc"][:, bass.ds(G * GN + h * HALF, HALF)], s["u_ps"])

            def second(G, i, u):
                wait(pe, s["u_sb"], G + 1)
                wait(pe, s["k_sb"], G - 1)
                by_tile(pb[u], tiles["u"][u], W["W2"], s["y_ps"])

            def turn(G, i, u):
                wait(pe, s["hn"], (G + 1) * GT)
                for t in range(GT):
                    mm = pe.transpose(pa[u][:, t * P:(t + 1) * P], tiles["hn"][u][:, t, :], g["ident"][:, :])
                mm.then_inc(s["t_ps"], 1)

            def by_source(G, i, u):
                wait(pe, s["hT"], G + 1)
                by_tile(pb[u], tiles["hT"][u], W["Wt"], s["a_ps"])
                hT = flat(tiles["hT"][u])
                halves(pa[u], u, W["Wq"][:, :], lambda h: hT[:, h * HALF:(h + 1) * HALF], s["q_ps"])

            def by_target(G, i, u):
                wait(pe, s["q_sb"], G + 1)
                wait(pe, s["a_sb"], G + 1)
                q = flat(tiles["q"][u])
                halves(pb[u], u, W["WkT"][:, :], lambda h: q[:, h * HALF:(h + 1) * HALF], s["k_ps"])
                halves(pa[u], u, col["bk"][:, 0:1], lambda h: q[:, h * HALF:(h + 1) * HALF], s["c_ps"])
            pairs(pe, [first, second, turn, by_source, by_target])

        two = lambda ps, m=P: ps[0:m, :].rearrange("p (h n) -> p h n", h=2)[:, :, 0:HALF]
        twos = lambda t: t.rearrange("p (h n) -> p h n", h=2)

        @block.scalar
        def _(act):
            act.wait_ge(weights_in, 16 * n_weights)

            def relu1(G, i, u):
                wait(act, s["u_ps"], G + 1)
                act.activation(twos(flat(tiles["u"][u])), two(pa[u]), ACT.Relu,
                               bias=col["b1"][:, 0:1]).then_inc(s["u_sb"], 1)

            def root1(G, i, u):
                norm_root(act, m[u], s1, G)

            def root2(G, i, u):
                norm_root(act, m[u], s2, G)

            def norm1(G, i, u):
                wait(act, s1["shift"], G + 1)
                for t in range(GT):
                    act.activation(tiles["h2"][u][:, t, :], tiles["x1"][u][:, t, :], ACT.Relu,
                                   bias=m[u]["shift"][:, t:t + 1], scale=m[u]["rstd"][:, t:t + 1]).then_inc(s["h2"], 1)

            def norm2(G, i, u):
                wait(act, s2["shift"], G + 1)
                for t in range(GT):
                    act.activation(tiles["hn"][u][:, t, :], tiles["h2"][u][:, t, :], ACT.Identity,
                                   bias=m[u]["shift"][:, t:t + 1], scale=m[u]["rstd"][:, t:t + 1]).then_inc(s["hn"], 1)

            def affine(G, i, u):
                wait(act, s["t_ps"], G + 1)
                act.activation(flat(tiles["hT"][u]), pa[u][:, 0:GN], ACT.Identity,
                               bias=col["beta"][:, 0:1], scale=col["gamma"][:, 0:1]).then_inc(s["hT"], 1)

            def query(G, i, u):
                wait(act, s["q_ps"], G + 1)
                act.activation(twos(flat(tiles["q"][u])), two(pa[u]), ACT.Identity,
                               bias=col["bq"][:, 0:1]).then_inc(s["q_sb"], 1)

            def key(G, i, u):
                wait(act, q_out[u], 32 * i)
                wait(act, s["k_ps"], G + 1)
                act.activation(twos(flat(tiles["qk"][u])), two(pb[u]), ACT.Copy,
                               scale=float(D) ** -0.5).then_inc(s["k_sb"], 1)
                wait(act, s["c_ps"], G + 1)
                act.activation(twos(cb[u][:, :]), two(pa[u], 1), ACT.Copy,
                               scale=float(D) ** -0.5).then_inc(s["c_sb"], 1)
            pairs(act, [relu1, root1, norm1, root2, norm2, affine, query, key])

        @block.vector
        def _(v):
            v.wait_ge(weights_in, 16 * n_weights)

            def residual(G, i, u):
                wait(v, s["y_ps"], G + 1)
                v.tensor_tensor(tiles["y"][u][:, :, :], pb[u][:, 0:GN].rearrange("p (t d) -> p t d", t=GT),
                                W["b2"][:, :].unsqueeze(1).to_broadcast([P, GT, D]), ALU.add).then_inc(s["y_sb"], 1)
                wait(v, x_in[u], 16 * (i + 1))
                wait(v, s["y_sb"], G + 1)
                v.scalar_tensor_tensor(out=flat(tiles["x1"][u]), in0=flat(tiles["y"][u]), scalar=0.0,
                                       in1=flat(tiles["x"][u]), op0=ALU.max, op1=ALU.add).then_inc(s["x1"], 1)
                wait(v, s["x1"], G + 1)
                norm_moments(v, tiles["x1"][u], m[u], s1, G)

            def scales1(G, i, u):
                wait(v, s["hn"], (G - 1) * GT)
                norm_scales(v, m[u], s1, G)

            def scales2(G, i, u):
                norm_scales(v, m[u], s2, G)

            def renorm(G, i, u):
                wait(v, s["h2"], (G + 1) * GT)
                norm_moments(v, tiles["h2"][u], m[u], s2, G)
                wait(v, r_out[u], 16 * i)
                v.tensor_tensor(tiles["r"][u][:, :, :], tiles["x1"][u][:, :, :], tiles["h2"][u][:, :, :],
                                ALU.add).then_inc(s["r"], 1)

            def sources(G, i, u):
                wait(v, a_out[u], 16 * i)
                wait(v, s["a_ps"], G + 1)
                v.tensor_tensor(tiles["A"][u][:, :, :], pb[u][:, 0:GN].rearrange("p (t d) -> p t d", t=GT),
                                W["bt"][:, :].unsqueeze(1).to_broadcast([P, GT, D]), ALU.add).then_inc(s["a_sb"], 1)
            pairs(v, [residual, scales1, renorm, scales2, sources])


def attention_sweeps(nc, a, g, arow, qk, ck, low, span):
    with ExitStack() as ctx:
        st = Stage(nc, ctx, "attention")
        acc, rows = g["acc"], g["rows"]
        wt = st.sb("wt_edge", [P, D])
        wgt = st.sb("wgt", [P, NBLK * SUB])
        idx = st.two("idx", [P, COLS], I32)
        ev = st.two("ev", [P, COLS, D])
        ag = st.two("ag", [P, COLS, D])
        t = st.two("t", [P, COLS, D])
        evT, tT = st.two("evT", [P, 512]), st.two("tT", [P, 512])
        qw, cw = st.two("qw", [P, CW]), st.two("cw", [1, CW])
        hot, attn = st.two("hot", [P, COLS, WIN]), st.two("attn", [P, COLS])
        pen, prod = st.sb("pen", [P, COLS, WIN]), st.sb("prod", [P, COLS, WIN])
        xm = st.sb("xm", [P, CW])
        bm = st.sb("bm", [2 * WIN, BPC // 2])
        mold, mnew, mdiff = st.sb("mold", [1, CW]), st.sb("mnew", [1, CW]), st.sb("mdiff", [1, CW])
        fade = st.sb("fade", [P, CW])
        mx, z, pr = st.sb("mx", [P, COLS]), st.sb("z", [P, COLS]), st.sb("pr", [P, COLS])
        e_hot = st.sb("e_hot", [P, COLS, WIN])
        evT_ps, tT_ps = st.ps("evT_ps"), st.ps("tT_ps")
        pre_ps = [st.ps("pre_ps0"), st.ps("pre_ps1")]
        sc_ps = st.ps("sc_ps", (P, 1024))
        b0, b1 = st.ps("back0"), st.ps("back1")
        w = {"bank": [b0, b1],
             "capped": st.sem("w_capped"), "tables": st.sem("w_tables"), "spread": st.sem("w_spread")}
        setup, held = st.sem("setup"), st.sem("held")
        idx_in, gathered, ev_in, qw_in = st.sem2("idx_in"), st.sem2("gathered"), st.sem2("ev_in"), st.sem2("qw_in")
        names = ("evT_ps", "evT_sb", "pre_ps", "pre_sb", "t_sb", "tT_ps", "tT_sb", "sc_ps",
                 "hot", "pen", "prod", "score", "attn", "masked", "xm", "xm_ps", "bm", "bm_ps",
                 "mold", "mrow", "mnew", "mdiff", "mnew_ps", "mdiff_ps", "fade", "mprod", "mx", "z", "pr", "e_hot",
                 "sums_ps", "faded", "added", "sfaded", "sadded")
        s = {k: st.sem("a_" + k) for k in names}
        src = a["src_chunks"]
        regs = {e: [getattr_free(nc, e).alloc_register(f"att_{e}{b}") for b in range(BPC)] for e in ("vector", "sync")}
        half = COLS // 2
        HB = BPC // 2 * WIN * SUB

        with nc.Block() as block:
            @block.sync
            def _(sp):
                sp.dma_start(wt[:, :], a["Wt"][D:2 * D, :]).then_inc(setup, 16)
                sp.dma_start(wgt[:, :], a["wgt_cols"]).then_inc(setup, 16)
                sp.wait_ge(setup, 32)

            @block.vector
            def _(v):
                v.memset(acc[:, :], 0.0).then_inc(s["added"], 1)
                v.memset(rows[0:1, :], -BIG).then_inc(s["added"], 1)
                v.memset(rows[32:33, :], 0.0).then_inc(s["added"], 1)
                v.wait_ge(s["added"], 3)
        first_windows(nc, g, low, "copied_att")

        with nc.Fori(0, span + 1, WIN):
            st.clear()
            next_windows(nc, g, st, w)
            with nc.Block() as block:
                @block.sync
                def _(sp):
                    def step(front, back):
                        if not front:
                            return
                        c, h, j = front
                        wait(sp, gathered[j], 16 * COLS * h)
                        sp.dma_start(idx[j][:, :], src[bass.ds(c, 1)].rearrange("a p k -> p (a k)")).then_inc(idx_in[j], 16)
                        wait(sp, s["evT_ps"], QUADS * (c - 1))
                        sp.dma_start(ev[j][:, :, :].rearrange("p (b s) d -> p b s d", s=SUB),
                                     a["edge_attr"][bass.ds(c * CHUNK, CHUNK), :].rearrange(
                                         "(b p s) d -> p b s d", p=P, s=SUB)).then_inc(ev_in[j], 16)
                        load_windows(c, j)

                    def load_windows(c, j):
                        load_bases(sp, regs["sync"], g, c)
                        wait(sp, s["sc_ps"], 2 * (c - 1))
                        for b in range(BPC):
                            at = window(sp, regs["sync"][b])
                            sp.dma_start(qw[j][:, b * WIN:(b + 1) * WIN], qk[:, bass.ds(at, WIN)]).then_inc(qw_in[j], 16)
                            sp.dma_start(cw[j][:, b * WIN:(b + 1) * WIN], ck[:, bass.ds(at, WIN)]).then_inc(qw_in[j], 16)

                    def last(c, h, j):
                        sp.wait_ge(gathered[j], 16 * COLS * h)
                        sp.dma_start(idx[j][:, :], src[c]).then_inc(idx_in[j], 16)
                        sp.wait_ge(s["evT_ps"], QUADS * (c - 1))
                        full = a["edge_attr"][c * CHUNK:c * CHUNK + TAIL_BLOCKS * BLOCK, :]
                        sp.dma_start(ev[j][:, 0:TAIL_BLOCKS * SUB, :].rearrange("p (b s) d -> p b s d", s=SUB),
                                     full.rearrange("(b p s) d -> p b s d", p=P, s=SUB)).then_inc(ev_in[j], 16)
                        part = a["edge_attr"][c * CHUNK + TAIL_BLOCKS * BLOCK:E, :]
                        sp.dma_start(ev[j][0:TAIL_PARTS, TAIL_BLOCKS * SUB:(TAIL_BLOCKS + 1) * SUB, :],
                                     part.rearrange("(p s) d -> p s d", s=SUB)).then_inc(ev_in[j], 16)
                        load_windows(c, j)

                    step((0, 0, 0), None)
                    step((1, 0, 1), None)
                    with sp.Fori(0, (NCH - 4) // 2) as i:
                        step((2 * i + 2, i + 1, 0), None)
                        step((2 * i + 3, i + 1, 1), None)
                    step((NCH - 2, (NCH - 2) // 2, 0), None)
                    last(NCH - 1, (NCH - 2) // 2, 1)

                @block.gpsimd
                def _(gp):
                    def step(front, back):
                        if front:
                            c, h, j = front
                            wait(gp, idx_in[j], 16 * (h + 1))
                            wait(gp, s["pre_sb"], QUADS * (c - 1))
                            hold(gp, g, held, c)
                            gather_chunk(gp, idx[j], arow, ag[j], gathered[j])
                    over_chunks(gp, step)

                @block.tensor
                def _(pe):
                    def turn_edges(f, q):
                        c, h, j = f
                        if q == 0:
                            wait(pe, ev_in[j], 16 * (h + 1) + (16 if c is LAST else 0))
                        wait(pe, s["evT_sb"], QUADS * c + q)
                        for k in range(4):
                            mm = pe.transpose(evT_ps[:, k * P:(k + 1) * P], ev[j][:, 4 * q + k, :], g["ident"][:, :])
                        mm.then_inc(s["evT_ps"], 1)

                    def edge_product(f, q):
                        c, h, j = f
                        wait(pe, s["evT_sb"], QUADS * c + q + 1)
                        wait(pe, s["pre_sb"], QUADS * c + q - 1)
                        for k in range(4):
                            mm = pe.matmul(pre_ps[q % 2][:, k * P:(k + 1) * P], evT[q % 2][:, k * P:(k + 1) * P],
                                           wt[:, :], start=True, stop=True)
                        mm.then_inc(s["pre_ps"], 1)

                    def turn_gelu(f, q):
                        c, h, j = f
                        wait(pe, s["t_sb"], QUADS * c + q + 1)
                        wait(pe, s["tT_sb"], QUADS * c + q)
                        for k in range(4):
                            mm = pe.transpose(tT_ps[:, k * P:(k + 1) * P], t[j][:, 4 * q + k, :], g["ident"][:, :])
                        mm.then_inc(s["tT_ps"], 1)

                    def scores(f, q):
                        c, h, j = f
                        at = 512 * (q // 2)
                        if q == 0:
                            wait(pe, qw_in[j], 16 * 2 * BPC * (h + 1))
                            wait(pe, s["prod"], c)
                        wait(pe, s["tT_sb"], QUADS * c + q + 1)
                        if q % 2 == 0:
                            nb = BPC // 2
                            bias = cw[j][0:1, (q // 2) * nb * WIN:(q // 2 + 1) * nb * WIN].rearrange(
                                "p (b n) -> p b n", n=WIN)
                            pe.matmul(sc_ps[:, at:at + HB].rearrange("p (b s n) -> p b s n", s=SUB, n=WIN),
                                      g["ones"][0:1, :], bcast_mid(bias, [1, nb, SUB, WIN]), start=True, stop=True,
                                      skip_group_check=True)
                        for k in range(4):
                            n = 4 * q + k
                            o = at + (n % half) * WIN
                            mm = pe.matmul(sc_ps[:, o:o + WIN], tT[q % 2][:, k * P:(k + 1) * P],
                                           qw[j][:, (n // SUB) * WIN:(n // SUB + 1) * WIN], start=False,
                                           stop=True, skip_group_check=True)
                        if q % 2 == 1:
                            mm.then_inc(s["sc_ps"], 1)

                    def turn_scores(bk):
                        c, h, j = bk
                        wait(pe, s["xm"], c + 1)
                        wait(pe, s["added"], BPC * c)
                        wait(pe, s["sadded"], BPC * c)
                        for k in range(BPC // 2):
                            mm = pe.transpose(b0[0:2 * WIN, k * P:(k + 1) * P], xm[:, k * 2 * WIN:(k + 1) * 2 * WIN],
                                              g["ident"][:, :])
                        mm.then_inc(s["xm_ps"], 1)

                    def spread_maxima(bk):
                        c, h, j = bk
                        wait(pe, s["bm"], c + 1)
                        for k in range(BPC // 2):
                            mm = pe.matmul(b1[:, k * 2 * WIN:(k + 1) * 2 * WIN], bm[:, k:k + 1].to_broadcast([2 * WIN, P]),
                                           g["ident"][0:2 * WIN, 0:2 * WIN], start=True, stop=True)
                        mm.then_inc(s["bm_ps"], 1)

                    def spread_running(bk):
                        c, h, j = bk
                        wait(pe, s["mnew"], c + 1)
                        pe.matmul(b0[:, 0:CW], g["ones"][0:1, :], mnew[:, :], start=True, stop=True).then_inc(s["mnew_ps"], 1)
                        wait(pe, s["mdiff"], c + 1)
                        pe.matmul(b1[:, 0:CW], g["ones"][0:1, :], mdiff[:, :], start=True, stop=True).then_inc(s["mdiff_ps"], 1)

                    def sums(bk):
                        c, h, j = bk
                        wait(pe, s["fade"], c + 1)
                        wait(pe, s["e_hot"], c + 1)
                        for b in range(BPC):
                            for k in range(SUB):
                                pe.matmul(b0[:, b * WIN:(b + 1) * WIN], t[j][:, b * SUB + k, :], e_hot[:, b * SUB + k, :],
                                          start=(k == 0), stop=(k == SUB - 1))
                        e = e_hot[:, :, :].rearrange("p (b s) n -> p b s n", s=SUB)
                        for k in range(SUB):
                            mm = pe.matmul(b1[:, 0:CW].rearrange("p (b n) -> p b n", n=WIN), g["ones"][:, :], e[:, :, k, :],
                                           start=(k == 0), stop=(k == SUB - 1))
                        mm.then_inc(s["sums_ps"], 1)

                    def step(f, bk):
                        if f:
                            turn_edges(f, 0)
                        if bk:
                            turn_scores(bk)
                        if f:
                            turn_edges(f, 1)
                            edge_product(f, 0)
                        if bk:
                            spread_maxima(bk)
                        if f:
                            turn_edges(f, 2)
                            edge_product(f, 1)
                            turn_gelu(f, 0)
                            turn_edges(f, 3)
                            edge_product(f, 2)
                        if bk:
                            spread_running(bk)
                        if f:
                            turn_gelu(f, 1)
                            scores(f, 0)
                            edge_product(f, 3)
                            turn_gelu(f, 2)
                            scores(f, 1)
                            turn_gelu(f, 3)
                            scores(f, 2)
                        if bk:
                            sums(bk)
                        if f:
                            scores(f, 3)
                    walk(pe, step)

                @block.scalar
                def _(act):
                    def copy_evT(f, q):
                        c, h, j = f
                        wait(act, s["evT_ps"], QUADS * c + q + 1)
                        wait(act, s["pre_ps"], QUADS * c + q - 1)
                        act.activation(evT[q % 2][:, :], evT_ps[:, :], ACT.Copy).then_inc(s["evT_sb"], 1)

                    def gelu(f, q):
                        c, h, j = f
                        wait(act, s["pre_sb"], QUADS * c + q + 1)
                        x = t[j][:, 4 * q:4 * q + 4, :]
                        act.activation(x, x, ACT.Gelu).then_inc(s["t_sb"], 1)

                    def copy_tT(f, q):
                        c, h, j = f
                        wait(act, s["tT_ps"], QUADS * c + q + 1)
                        wait(act, s["sc_ps"], (QUADS * c + q - 1) // 2 if isinstance(c, int) else 2 * c + (q - 1) // 2)
                        act.activation(tT[q % 2][:, :], tT_ps[:, :], ACT.Copy).then_inc(s["tT_sb"], 1)

                    def exps(bk):
                        c, h, j = bk
                        wait(act, s["mdiff_ps"], c + 1)
                        wait(act, s["added"], BPC * c)
                        wait(act, s["sadded"], BPC * c)
                        act.activation(fade[:, :], b1[:, 0:CW], ACT.Exp).then_inc(s["fade"], 1)
                        wait(act, s["z"], c + 1)
                        act.activation(pr[:, :], z[:, :], ACT.Exp).then_inc(s["pr"], 1)

                    def step(f, bk):
                        if f:
                            copy_evT(f, 0)
                            copy_evT(f, 1)
                            gelu(f, 0)
                            copy_evT(f, 2)
                            copy_tT(f, 0)
                            gelu(f, 1)
                            copy_evT(f, 3)
                            copy_tT(f, 1)
                            gelu(f, 2)
                            copy_tT(f, 2)
                            gelu(f, 3)
                            copy_tT(f, 3)
                        if bk:
                            exps(bk)
                    walk(act, step)

                @block.vector
                def _(v):
                    r = regs["vector"]
                    by_b = lambda x: x.rearrange("p (b s) n -> p b s n", s=SUB)
                    win3 = lambda x: x.rearrange("p (b n) -> p b n", n=WIN)
                    along = lambda x: x.unsqueeze(2).to_broadcast([P, COLS, WIN])

                    def add_source(f, q):
                        c, h, j = f
                        if q == 0:
                            wait(v, gathered[j], 16 * COLS * (h + 1))
                            wait(v, s["sums_ps"], c - 1)
                        wait(v, s["pre_ps"], QUADS * c + q + 1)
                        v.tensor_tensor(t[j][:, 4 * q:4 * q + 4, :],
                                        pre_ps[q % 2][:, :].rearrange("p (k d) -> p k d", k=4),
                                        ag[j][:, 4 * q:4 * q + 4, :], ALU.add).then_inc(s["pre_sb"], 1)

                    def one_hot(f):
                        c, h, j = f
                        onehot_op(v, g, hot[j], c).then_inc(s["hot"], 1)
                        wait(v, s["hot"], c + 1)
                        v.tensor_scalar(pen[:, :, :], hot[j][:, :, :], BIG, -BIG, ALU.mult, ALU.add).then_inc(s["pen"], 1)

                    def score(f):
                        c, h, j = f
                        wait(v, s["sc_ps"], 2 * (c + 1))
                        v.tensor_tensor(prod[:, :, :].rearrange("p (a k) n -> p a (k n)", a=2),
                                        sc_ps[:, :].rearrange("p (a n) -> p a n", a=2)[:, :, 0:HB],
                                        hot[j][:, :, :].rearrange("p (a k) n -> p a (k n)", a=2),
                                        ALU.mult).then_inc(s["prod"], 1)
                        wait(v, s["prod"], c + 1)
                        v.tensor_reduce(attn[j][:, :], prod[:, :, :], AX.X, ALU.add).then_inc(s["score"], 1)
                        wait(v, s["score"], c + 1)
                        v.tensor_tensor(attn[j][:, :], attn[j][:, :], wgt[:, bass.ds(c * COLS, COLS)],
                                        ALU.mult).then_inc(s["attn"], 1)
                        wait(v, s["attn"], c + 1)
                        wait(v, s["pen"], c + 1)
                        v.tensor_tensor(pen[:, :, :], pen[:, :, :], along(attn[j][:, :]), ALU.add).then_inc(s["masked"], 1)
                        wait(v, s["masked"], c + 1)
                        wait(v, s["xm_ps"], c)
                        x = by_b(pen[:, :, :])
                        v.tensor_tensor(win3(xm[:, :]), x[:, :, 0, :], x[:, :, 1, :], ALU.max).then_inc(s["xm"], 1)

                    def block_maxima(bk):
                        c, h, j = bk
                        load_bases(v, r, g, c)
                        wait(v, s["xm_ps"], c + 1)
                        wait(v, s["bm_ps"], c)
                        v.tensor_reduce(bm[:, :], b0[0:2 * WIN, :].rearrange("p (k e) -> p k e", e=P), AX.X,
                                        ALU.max).then_inc(s["bm"], 1)

                    def running_maxima(bk):
                        c, h, j = bk
                        for b in range(BPC):
                            at = window(v, r[b])
                            if b == 0:
                                wait(v, s["bm_ps"], c + 1)
                            cols = slice(b * WIN, (b + 1) * WIN)
                            wait(v, s["mrow"], BPC * c + b)
                            v.tensor_copy(mold[0:1, cols], rows[0:1, bass.ds(at, WIN)]).then_inc(s["mold"], 1)
                            wait(v, s["mold"], BPC * c + b + 1)
                            v.tensor_tensor(rows[0:1, bass.ds(at, WIN)], mold[0:1, cols], b1[0:1, cols],
                                            ALU.max).then_inc(s["mrow"], 1)
                        wait(v, s["mnew_ps"], c)
                        wait(v, s["mdiff_ps"], c)
                        v.tensor_tensor(mnew[:, :], mold[:, :], b1[0:1, 0:CW], ALU.max).then_inc(s["mnew"], 1)
                        wait(v, s["mnew"], c + 1)
                        v.tensor_tensor(mdiff[:, :], mold[:, :], mnew[:, :], ALU.subtract).then_inc(s["mdiff"], 1)

                    def below_maximum(bk):
                        c, h, j = bk
                        wait(v, s["mnew_ps"], c + 1)
                        v.tensor_tensor(by_b(prod[:, :, :]), by_b(hot[j][:, :, :]),
                                        bcast_mid(win3(b0[:, 0:CW]), [P, BPC, SUB, WIN]), ALU.mult).then_inc(s["mprod"], 1)
                        wait(v, s["mprod"], c + 1)
                        v.tensor_reduce(mx[:, :], prod[:, :, :], AX.X, ALU.add).then_inc(s["mx"], 1)
                        wait(v, s["mx"], c + 1)
                        wait(v, s["pr"], c)
                        v.tensor_tensor(z[:, :], attn[j][:, :], mx[:, :], ALU.subtract).then_inc(s["z"], 1)

                    def spread_e(bk):
                        c, h, j = bk
                        wait(v, s["pr"], c + 1)
                        wait(v, s["sums_ps"], c)
                        v.tensor_tensor(e_hot[:, :, :], hot[j][:, :, :], along(pr[:, :]), ALU.mult).then_inc(s["e_hot"], 1)

                    def add_sums(bk):
                        c, h, j = bk
                        for b in range(BPC):
                            at = window(v, r[b])
                            if b == 0:
                                wait(v, s["sums_ps"], c + 1)
                                wait(v, s["fade"], c + 1)
                            cols = slice(b * WIN, (b + 1) * WIN)
                            n = BPC * c + b
                            nodes, total = acc[:, bass.ds(at, WIN)], rows[32:33, bass.ds(at, WIN)]
                            wait(v, s["added"], n)
                            v.tensor_tensor(nodes, nodes, fade[:, cols], ALU.mult).then_inc(s["faded"], 1)
                            wait(v, s["sadded"], n)
                            v.tensor_tensor(total, total, fade[32:33, cols], ALU.mult).then_inc(s["sfaded"], 1)
                            wait(v, s["faded"], n + 1)
                            v.tensor_tensor(nodes, nodes, b0[:, cols], ALU.add).then_inc(s["added"], 1)
                            wait(v, s["sfaded"], n + 1)
                            v.tensor_tensor(total, total, b1[32:33, cols], ALU.add).then_inc(s["sadded"], 1)

                    def step(f, bk):
                        if f:
                            add_source(f, 0)
                        if bk:
                            block_maxima(bk)
                        if f:
                            add_source(f, 1)
                        if bk:
                            running_maxima(bk)
                        if f:
                            add_source(f, 2)
                        if bk:
                            below_maximum(bk)
                        if f:
                            add_source(f, 3)
                            one_hot(f)
                        if bk:
                            spread_e(bk)
                            add_sums(bk)
                        if f:
                            score(f)
                    walk(v, step)
                    v.wait_ge(s["added"], NCH * BPC)
                    v.wait_ge(s["sadded"], NCH * BPC)


LAST = NCH - 1


def getattr_free(nc, name):
    return {"vector": nc.vector, "sync": nc.sync}[name]


def walk(eng, step):
    step((0, 0, 0), None)
    step((1, 0, 1), (0, 0, 0))
    with eng.Fori(0, (NCH - 4) // 2) as i:
        step((2 * i + 2, i + 1, 0), (2 * i + 1, i, 1))
        step((2 * i + 3, i + 1, 1), (2 * i + 2, i + 1, 0))
    m = (NCH - 2) // 2
    step((NCH - 2, m, 0), (NCH - 3, m - 1, 1))
    step((LAST, m, 1), (NCH - 2, m, 0))
    step(None, (LAST, m, 1))


def node_end(nc, a, g, res):
    with ExitStack() as ctx:
        st = Stage(nc, ctx, "node_end")
        wv, bv = st.sb("wv", [P, D]), st.sb("bv_row", [1, D])
        tc, gl, rr, oo = (st.two("e_" + k, [P, GT, D]) for k in ("tc", "gl", "rr", "oo"))
        sr = st.two("e_s", [1, GN])
        den, rden = st.two("e_den", [P, GT]), st.two("e_rden", [P, GT])
        pv = [st.ps(f"pv{u}", (P, 1024)) for u in range(2)]
        pd = [st.ps(f"pd{u}") for u in range(2)]
        names = ("tc", "sr", "pv", "den", "rden", "gl", "oo")
        s = {k: st.sem("e_" + k) for k in names}
        weights_in, r_in, o_out = st.sem("ew_in"), st.sem2("er_in"), st.sem2("eo_out")
        r_rows = res.rearrange("(g t p) d -> g p t d", t=GT, p=P)
        o_rows = a["out"].rearrange("(g t p) d -> g p t d", t=GT, p=P)
        one = lambda rows, G: rows[bass.ds(G, 1)].rearrange("a p t d -> p (a t) d")
        st.clear()
        block = ctx.enter_context(nc.Block())

        def pairs(eng, steps):
            for f in steps:
                for u in range(2):
                    f(u, 0, u)
            with eng.Fori(1, GROUPS // 2) as i:
                for f in steps:
                    for u in range(2):
                        f(2 * i + u, i, u)

        @block.sync
        def _(sp):
            sp.dma_start(wv[:, :], a["Wv"]).then_inc(weights_in, 16)
            sp.dma_start(bv[:, :], a["bv"].rearrange("(a d) -> a d", a=1)).then_inc(weights_in, 16)

            def load(G, i, u):
                wait(sp, s["oo"], G - 1)
                sp.dma_start(rr[u][:, :, :], one(r_rows, G)).then_inc(r_in[u], 16)

            def store(G, i, u):
                wait(sp, s["oo"], G + 1)
                sp.dma_start(one(o_rows, G), oo[u][:, :, :]).then_inc(o_out[u], 16)
            pairs(sp, [load, store])
            for u in range(2):
                sp.wait_ge(o_out[u], 16 * (GROUPS // 2))

        @block.scalar
        def _(act):
            def take(G, i, u):
                wait(act, s["pv"], G - 1)
                act.activation(tc[u][:, :, :].rearrange("p t d -> p (t d)"), g["acc"][:, bass.ds(G * GN, GN)],
                               ACT.Copy).then_inc(s["tc"], 1)
                act.activation(sr[u][0:1, :], g["rows"][32:33, bass.ds(G * GN, GN)], ACT.Copy).then_inc(s["sr"], 1)

            def gelu(G, i, u):
                wait(act, s["pv"], G + 1)
                wait(act, s["rden"], G + 1)
                wait(act, s["oo"], G - 1)
                for t in range(GT):
                    act.activation(gl[u][:, t, :], pv[u][:, t * P:(t + 1) * P], ACT.Gelu,
                                   scale=rden[u][:, t:t + 1]).then_inc(s["gl"], 1)
            pairs(act, [take, gelu])

        @block.tensor
        def _(pe):
            pe.wait_ge(weights_in, 32)

            def products(G, i, u):
                wait(pe, s["tc"], G + 1)
                wait(pe, s["sr"], G + 1)
                wait(pe, s["gl"], (G - 1) * GT)
                for t in range(GT):
                    out, sums = pv[u][:, t * P:(t + 1) * P], sr[u][0:1, t * P:(t + 1) * P]
                    pe.matmul(out, tc[u][:, t, :], wv[:, :], start=True, stop=False)
                    pe.matmul(out, sums, bv[:, :], start=False, stop=True)
                for t in range(GT):
                    mm = pe.matmul(pd[u][:, t:t + 1], sr[u][0:1, t * P:(t + 1) * P], g["ones"][0:1, 0:1],
                                   start=True, stop=True)
                mm.then_inc(s["pv"], 1)
            pairs(pe, [products])

        @block.vector
        def _(v):
            def inverse(G, i, u):
                wait(v, s["gl"], (G - 1) * GT)
                wait(v, s["pv"], G + 1)
                v.tensor_scalar(den[u][:, :], pd[u][:, 0:GT], SM_EPS, None, ALU.add).then_inc(s["den"], 1)
                wait(v, s["den"], G + 1)
                v.reciprocal(rden[u][:, :], den[u][:, :]).then_inc(s["rden"], 1)

            def finish(G, i, u):
                wait(v, s["gl"], (G + 1) * GT)
                wait(v, r_in[u], 16 * (i + 1))
                wait(v, o_out[u], 16 * i)
                v.tensor_tensor(oo[u][:, :, :], gl[u][:, :, :], rr[u][:, :, :], ALU.add).then_inc(s["oo"], 1)
            pairs(v, [inverse, finish])


def kernel(x, src, dst, edge_attr_128, edge_weight1, L0_gnn_eps, L0_gnn_W1, L0_gnn_b1, L0_gnn_W2, L0_gnn_b2,
           L1_gnn_gamma, L1_gnn_beta, L1_gnn_Wt, L1_gnn_bt, L1_gnn_Wq, L1_gnn_bq, L1_gnn_Wk, L1_gnn_bk,
           L1_gnn_Wv, L1_gnn_bv):
    import concourse.bacc as bacc
    from concourse.bass_utils import run_bass_kernel_spmd

    pad = NCH * CHUNK - E

    def chunked(v, fill):
        v = np.concatenate([np.asarray(v).reshape(-1), np.full(pad, fill, np.asarray(v).dtype)])
        return v.reshape(NCH, BPC, P, SUB).transpose(0, 2, 1, 3)

    dst_pad = np.concatenate([np.asarray(dst), np.full(pad, N, np.asarray(dst).dtype)])
    cols = lambda v: np.ascontiguousarray(v.transpose(1, 0, 2, 3).reshape(P, NBLK * SUB))
    arrays = {
        "x": np.pad(np.asarray(x), ((0, NP - N), (0, 0))),
        "src_chunks": np.ascontiguousarray(chunked(src, 0).reshape(NCH, P, COLS)),
        "dst_cols": cols(chunked(dst, N)),
        "dst_blocks": dst_pad.reshape(NBLK, BLOCK),
        "wgt_cols": cols(chunked(edge_weight1, 0)),
        "edge_attr": np.asarray(edge_attr_128),
        "eps": np.asarray(L0_gnn_eps).reshape(1, 1),
        "W1": L0_gnn_W1, "b1": L0_gnn_b1, "W2": L0_gnn_W2, "b2": L0_gnn_b2,
        "gamma": L1_gnn_gamma, "beta": L1_gnn_beta, "Wt": L1_gnn_Wt, "bt": L1_gnn_bt,
        "Wq": L1_gnn_Wq, "bq": L1_gnn_bq, "WkT": np.ascontiguousarray(np.asarray(L1_gnn_Wk).T), "bk": L1_gnn_bk,
        "Wv": L1_gnn_Wv, "bv": L1_gnn_bv,
    }
    arrays = {k: np.ascontiguousarray(v) for k, v in arrays.items()}
    nc = bacc.Bacc("TRN2", target_bir_lowering=False, num_devices=1)
    a = {k: nc.dram_tensor("in_" + k, list(v.shape), mybir.dt.from_np(v.dtype), kind="ExternalInput").ap()
         for k, v in arrays.items()}
    a["out"] = nc.dram_tensor("out_rows", [NP, D], F32, kind="ExternalOutput").ap()
    build_gnn(nc, a)
    r = run_bass_kernel_spmd(nc, [{"in_" + k: v for k, v in arrays.items()}], core_ids=[0])
    return r.results[0]["out_rows"][:N]
```

```python
from contextlib import ExitStack

import numpy as np

import concourse.bass as bass
from concourse import mybir
from concourse.alu_op_type import AluOpType as ALU

F32 = mybir.dt.float32
I32 = mybir.dt.int32
ACT = mybir.ActivationFunctionType
AX = mybir.AxisListType

P = 128
D = 128
N = 12500
E = 200000
WIN = 40
SUB = 2
BLOCK = P * SUB
BPC = 8
CHUNK = BPC * BLOCK
COLS = BPC * SUB
NCH = -(-E // CHUNK)
NBLK = NCH * BPC
QUADS = COLS // 4
CW = BPC * WIN
BIG = 1e30
TILES = -(-(N + WIN) // P)
NP = TILES * P
GT = 7
GROUPS = TILES // GT
GN = GT * P
HALF = GN // 2
PB = 112
KB = NBLK // PB
LN_EPS = 1e-5
SM_EPS = 1e-16
PEEL = 4
TAIL = E - (NCH - 1) * CHUNK
TAIL_BLOCKS = TAIL // BLOCK
TAIL_PARTS = (TAIL - TAIL_BLOCKS * BLOCK) // SUB
assert TILES % (2 * GT) == 0 and NBLK % PB == 0 and NCH % 4 == 2 and TAIL % SUB == 0 and HALF <= 512


def wait(eng, sem, value):
    if isinstance(value, int) and value <= 0:
        return
    eng.wait_ge(sem, value)


class Chunk:

    def __init__(self, base, n):
        self.j, self.k = n % 2, n % 4
        self.c = n if base is None else 4 * base + n
        self.h = n // 2 if base is None else 2 * base + n // 2
        self.g = n // 4 if base is None else base + n // 4
        self.last = base is None and n == NCH - 1
        self.two_before = (n - 2) % 4, (n - 2) // 4 + 1 if base is None else base + (n - 2) // 4 + 1


def over_chunks(eng, step):
    step(Chunk(None, 0), None)
    for n in range(1, PEEL):
        step(Chunk(None, n), Chunk(None, n - 1))
    with eng.Fori(0, (NCH - PEEL - 2) // 4) as i:
        for n in range(PEEL, PEEL + 4):
            step(Chunk(i, n), Chunk(i, n - 1))
    for n in range(NCH - 2, NCH):
        step(Chunk(None, n), Chunk(None, n - 1))
    step(None, Chunk(None, NCH - 1))


def over_stages(eng, step):
    def at(base, n):
        step(*(Chunk(base, n - k) if base is not None or 0 <= n - k < NCH else None for k in range(4)))

    for n in range(PEEL):
        at(None, n)
    with eng.Fori(0, (NCH - PEEL - 2) // 4) as i:
        for n in range(PEEL, PEEL + 4):
            at(i, n)
    for n in range(NCH - 2, NCH + 3):
        at(None, n)


def bcast_mid(ap, shape):
    return ap.unsqueeze(2).to_broadcast(shape)


def build_gnn(nc, a):
    with ExitStack() as ctx:
        def sb(name, shape, dt=F32):
            return ctx.enter_context(nc.sbuf_tensor(name, shape, dt))

        h0 = nc.dram_tensor("h0_rows", [NP, D], F32, kind="Internal").ap()
        res = nc.dram_tensor("residual_rows", [NP, D], F32, kind="Internal").ap()
        arow = nc.dram_tensor("source_rows", [NP, D], F32, kind="Internal").ap()
        qk = nc.dram_tensor("qk_cols", [D, NP], F32, kind="Internal").ap()
        ck = nc.dram_tensor("qk_bias_cols", [1, NP], F32, kind="Internal").ap()

        ew = nc.dram_tensor("edge_products", [NCH, P, COLS * D], F32, kind="Internal").ap()
        low = nc.dram_tensor("low_row", [1, NBLK], F32, kind="Internal").ap()

        g = {
            "acc": sb("acc", [P, NP]),
            "ident": sb("ident", [P, P]),
            "ones": sb("ones", [P, P]),
            "iota": sb("iota", [P, WIN]),
            "dst": sb("dst", [P, NBLK, SUB]),
            "rel": sb("rel", [P, NBLK, SUB]),
            "start": sb("start", [1, NBLK]),
            "capped": sb("capped", [1, NBLK]),
            "base": sb("base", [1, NBLK], I32),
            "span": sb("span", [1, 1], I32),
            "eps1": sb("eps1", [P, 1]),
            "spare": sb("spare", [1, 1]),
        }
        constants(nc, a, g)
        node_norm(nc, a, g, h0)
        edge_tables(nc, a, g, low)
        span = nc.values_load(g["span"][0:1, 0:1], min_val=0, max_val=N)
        gin_sweeps(nc, a, g, h0, ew, low, span)
        node_mid(nc, a, g, res, arow, qk, ck)
        with nc.sbuf_tensor("rows", [33, NP], F32) as rows:
            g["rows"] = rows
            attention_sweeps(nc, a, g, arow, ew, qk, ck, low, span)
            node_end(nc, a, g, res)


class Stage:

    def __init__(self, nc, ctx, name):
        self.nc, self.ctx, self.name, self.sems = nc, ctx, name, []

    def sb(self, name, shape, dt=F32):
        return self.ctx.enter_context(self.nc.sbuf_tensor(f"{self.name}_{name}", shape, dt))

    def two(self, name, shape, dt=F32):
        return [self.sb(f"{name}{j}", shape, dt) for j in range(2)]

    def ps(self, name, shape=(P, 512)):
        return self.ctx.enter_context(self.nc.psum_tensor(f"{self.name}_{name}", list(shape), F32))

    def sem(self, name):
        s = self.ctx.enter_context(self.nc.semaphore(f"{self.name}_{name}"))
        self.sems.append(s)
        return s

    def sem2(self, name):
        return [self.sem(f"{name}_{j}") for j in range(2)]

    def clear(self):
        self.nc.all_engine_barrier()
        for s in self.sems:
            self.nc.sync.sem_clear(s)
        self.nc.all_engine_barrier()


def constants(nc, a, g):
    with ExitStack() as ctx:
        st = Stage(nc, ctx, "constants")
        iota_i = st.sb("iota_i", [P, WIN], I32)
        zeroed, identity_ready, iota_ready = st.sem("zeroed"), st.sem("identity_ready"), st.sem("iota_ready")
        eps_in, ones_ready, float_ready = st.sem("eps_in"), st.sem("ones_ready"), st.sem("float_ready")
        block = ctx.enter_context(nc.Block())

        @block.sync
        def _(sp):
            sp.dma_start(g["eps1"][:, :], a["eps"].to_broadcast([P, 1])).then_inc(eps_in, 16)

        @block.gpsimd
        def _(gp):
            gp.memset(g["ident"][:, :], 0.0).then_inc(zeroed, 1)
            gp.iota(iota_i[:, :], pattern=[[1, WIN]], base=0, channel_multiplier=0).then_inc(iota_ready, 1)
            gp.wait_ge(zeroed, 1)
            gp.affine_select(out=g["ident"][:, :], in_=g["ident"][:, :], compare_op=ALU.not_equal, fill=1.0,
                             base=0, pattern=[[-1, P]], channel_multiplier=1).then_inc(identity_ready, 1)
            gp.wait_ge(identity_ready, 1)

        @block.vector
        def _(v):
            v.memset(g["ones"][:, :], 1.0).then_inc(ones_ready, 1)
            v.wait_ge(iota_ready, 1)
            v.tensor_copy(g["iota"][:, :], iota_i[:, :]).then_inc(float_ready, 1)
            v.wait_ge(eps_in, 16)
            v.tensor_scalar(g["eps1"][:, :], g["eps1"][:, :], 1.0, None, ALU.add).then_inc(float_ready, 1)
            v.wait_ge(float_ready, 2)
            v.wait_ge(ones_ready, 1)


NORM_STEPS = ("stats", "held", "means", "var", "std", "rstd", "shift")


def norm_steps(st, name):
    return {**{k: st.sem(f"{name}_{k}") for k in NORM_STEPS}, "spare": st.sb(name + "_spare", [1, 1])}


def norm_moments(v, x, m, s, G):
    for t in range(GT):
        v.bn_stats(m["stats"][:, t, :], x[:, t, :]).then_inc(s["stats"], 1)
    wait(v, s["stats"], (G + 1) * GT)
    wait(v, s["held"], G)
    v.tensor_tensor(s["spare"][:, :], m["eps"][0:1, 0:1], m["eps"][0:1, 0:1], ALU.mult).then_inc(s["held"], 1)
    for t in range(GT):
        v.bn_aggr(m["mv"][:, t, :], m["stats"][:, t, :]).then_inc(s["means"], 1)
    wait(v, s["means"], (G + 1) * GT)
    v.tensor_scalar(m["var"][:, :], m["mv"][:, :, 1], LN_EPS, None, ALU.add).then_inc(s["var"], 1)


def norm_root(act, m, s, G):
    wait(act, s["var"], G + 1)
    wait(act, s["rstd"], G - 1)
    act.activation(m["std"][:, :], m["var"][:, :], ACT.Sqrt).then_inc(s["std"], 1)


def norm_scales(v, m, s, G):
    wait(v, s["std"], G + 1)
    v.reciprocal(m["rstd"][:, :], m["std"][:, :]).then_inc(s["rstd"], 1)
    wait(v, s["rstd"], G + 1)
    v.scalar_tensor_tensor(out=m["shift"][:, :], in0=m["mv"][:, :, 0], scalar=-1.0, in1=m["rstd"][:, :],
                           op0=ALU.mult, op1=ALU.mult).then_inc(s["shift"], 1)


def norm_buffers(st, g):
    return [{"stats": st.sb(f"stats{u}", [P, GT, 6]), "mv": st.sb(f"mv{u}", [P, GT, 2]), "eps": g["eps1"],
             **{k: st.sb(f"{k}{u}", [P, GT]) for k in ("var", "std", "rstd", "shift")}} for u in range(2)]


def node_norm(nc, a, g, h0):
    with ExitStack() as ctx:
        st = Stage(nc, ctx, "node_norm")
        x, h = st.two("x", [P, GT, D]), st.two("h", [P, GT, D])
        m = norm_buffers(st, g)
        hT = [st.ps(f"hT{u}", (P, 1024)) for u in range(2)]
        x_in, h_out = st.sem2("x_in"), st.sem2("h_out")
        s = norm_steps(st, "n")
        h_ready, hT_ready, acc_ready = st.sem("h_ready"), st.sem("hT_ready"), st.sem("acc_ready")
        x_rows = a["x"].rearrange("(g t p) d -> g p t d", t=GT, p=P)
        h_rows = h0.rearrange("(g t p) d -> g p t d", t=GT, p=P)
        st.clear()
        block = ctx.enter_context(nc.Block())

        def pairs(eng, step):
            for u in range(2):
                step(u, 0, u)
            with eng.Fori(1, GROUPS // 2) as i:
                for u in range(2):
                    step(2 * i + u, i, u)

        @block.sync
        def _(sp):
            def step(G, i, u):
                wait(sp, h_ready, (G - 1) * GT)
                sp.dma_start(x[u][:, :, :], x_rows[bass.ds(G, 1)].rearrange("a p t d -> p (a t) d")).then_inc(x_in[u], 16)
            pairs(sp, step)

        @block.vector
        def _(v):
            def moments(G, i, u):
                wait(v, x_in[u], 16 * (i + 1))
                norm_moments(v, x[u], m[u], s, G)

            def scales(G, i, u):
                wait(v, h_ready, (G - 1) * GT)
                norm_scales(v, m[u], s, G)
            for f in (moments, scales):
                for u in range(2):
                    f(u, 0, u)
            with v.Fori(1, GROUPS // 2) as i:
                for f in (moments, scales):
                    for u in range(2):
                        f(2 * i + u, i, u)

        @block.scalar
        def _(act):
            def root(G, i, u):
                norm_root(act, m[u], s, G)

            def scale(G, i, u):
                wait(act, s["shift"], G + 1)
                wait(act, h_out[u], 16 * i)
                wait(act, hT_ready, G - 1)
                for t in range(GT):
                    act.activation(h[u][:, t, :], x[u][:, t, :], ACT.Relu, bias=m[u]["shift"][:, t:t + 1],
                                   scale=m[u]["rstd"][:, t:t + 1]).then_inc(h_ready, 1)

            def keep(G, i, u):
                wait(act, h_ready, (G + 1) * GT)
                act.dma_start(h_rows[bass.ds(G, 1)].rearrange("a p t d -> p (a t) d"), h[u][:, :, :]).then_inc(h_out[u], 16)
                wait(act, hT_ready, G + 1)
                act.activation(g["acc"][:, bass.ds(G * GN, GN)], hT[u][:, 0:GN], ACT.Copy,
                               scale=g["eps1"][:, 0:1]).then_inc(acc_ready, 1)
            def both(i, first):
                for f in (root, scale, keep):
                    for u in range(2):
                        f(2 * i + u if not first else u, i, u)
            both(0, True)
            with act.Fori(1, GROUPS // 2) as i:
                both(i, False)
            for u in range(2):
                act.wait_ge(h_out[u], 16 * (GROUPS // 2))
            act.wait_ge(acc_ready, GROUPS)

        @block.tensor
        def _(pe):
            def step(G, i, u):
                wait(pe, h_ready, (G + 1) * GT)
                wait(pe, acc_ready, G - 1)
                for t in range(GT):
                    mm = pe.transpose(hT[u][:, t * P:(t + 1) * P], h[u][:, t, :], g["ident"][:, :])
                mm.then_inc(hT_ready, 1)
            pairs(pe, step)


def edge_tables(nc, a, g, low_row):
    with ExitStack() as ctx:
        st = Stage(nc, ctx, "edge")
        by_block = st.sb("by_block", [PB, KB, BLOCK], I32)
        by_edge = st.sb("by_edge", [P, NBLK, SUB], I32)
        low, high = st.sb("low_p", [PB, KB]), st.sb("high_p", [PB, KB])
        wide, widest = st.sb("wide", [PB, KB]), st.sb("widest", [PB, 1])
        low_sb = st.sb("low_sb", [1, NBLK])
        lowT, wideT = st.ps("lowT", (P, 1024)), st.ps("wideT")
        dst_in, blocks_in = st.sem("dst_in"), st.sem("blocks_in")
        ends_ready, wide_ready, widest_ready = st.sem("ends_ready"), st.sem("wide_ready"), st.sem("widest_ready")
        rows_ready, tables_ready, low_out = st.sem("rows_ready"), st.sem("tables_ready"), st.sem("low_out")
        st.clear()
        block = ctx.enter_context(nc.Block())

        @block.sync
        def _(sp):
            sp.dma_start(by_block[:, :, :], a["dst_blocks"].rearrange("(k p) e -> p k e", p=PB)).then_inc(blocks_in, 16)
            sp.dma_start(by_edge[:, :, :], a["dst_cols"].rearrange("p (b s) -> p b s", s=SUB)).then_inc(dst_in, 16)
            sp.wait_ge(tables_ready, 4)
            sp.dma_start(low_row, low_sb[:, :]).then_inc(low_out, 16)
            sp.wait_ge(low_out, 16)

        @block.vector
        def _(v):
            v.wait_ge(blocks_in, 16)
            v.tensor_reduce(low[:, :], by_block[:, :, :], AX.X, ALU.min).then_inc(ends_ready, 1)
            v.tensor_reduce(high[:, :], by_block[:, :, :], AX.X, ALU.max).then_inc(ends_ready, 1)
            v.wait_ge(ends_ready, 2)
            v.tensor_tensor(wide[:, :], high[:, :], low[:, :], ALU.subtract).then_inc(wide_ready, 1)
            v.wait_ge(wide_ready, 1)
            v.tensor_reduce(widest[:, :], wide[:, :], AX.X, ALU.max).then_inc(widest_ready, 1)
            v.wait_ge(dst_in, 16)
            v.tensor_copy(g["dst"][:, :, :], by_edge[:, :, :]).then_inc(tables_ready, 1)
            v.wait_ge(rows_ready, 1)
            for half in range(2):
                n = min(KB - 4 * half, 4) * PB
                v.tensor_copy(low_sb[0:1, 4 * PB * half:4 * PB * half + n],
                              lowT[0:1, 512 * half:512 * half + n]).then_inc(tables_ready, 1)
            v.tensor_reduce(g["span"][0:1, 0:1], wideT[0:1, 0:PB], AX.X, ALU.max).then_inc(tables_ready, 1)
            v.wait_ge(tables_ready, 4)

        @block.tensor
        def _(pe):
            pe.wait_ge(widest_ready, 1)
            for k in range(KB):
                at = 512 * (k // 4) + PB * (k % 4)
                pe.matmul(lowT[0:1, at:at + PB], low[:, k:k + 1], g["ident"][0:PB, 0:PB], start=True, stop=True)
            pe.matmul(wideT[0:1, 0:PB], widest[:, 0:1], g["ident"][0:PB, 0:PB],
                      start=True, stop=True).then_inc(rows_ready, 1)


def first_windows(nc, g, low_row, name):
    with nc.semaphore(name) as copied, nc.Block() as block:
        @block.sync
        def _(sp):
            sp.dma_start(g["start"][:, :], low_row).then_inc(copied, 16)
            sp.wait_ge(copied, 16)


def next_windows(nc, g, st, s):
    bank = s["bank"]
    half = NBLK // 2
    with nc.Block() as block:
        @block.vector
        def _(v):
            v.tensor_scalar(g["capped"][:, :], g["start"][:, :], float(N), None, ALU.min).then_inc(s["capped"], 1)
            v.wait_ge(s["capped"], 1)
            v.tensor_copy(g["base"][:, :], g["capped"][:, :]).then_inc(s["tables"], 1)
            v.tensor_scalar(g["start"][:, :], g["start"][:, :], float(WIN), None, ALU.add).then_inc(s["tables"], 1)
            v.wait_ge(s["spread"], 2)
            for k in range(2):
                v.tensor_tensor(g["rel"][:, k * half:(k + 1) * half, :], g["dst"][:, k * half:(k + 1) * half, :],
                                bank[k][:, 0:half].unsqueeze(2).to_broadcast([P, half, SUB]),
                                ALU.subtract).then_inc(s["tables"], 1)
            v.wait_ge(s["tables"], 4)

        @block.tensor
        def _(pe):
            pe.wait_ge(s["capped"], 1)
            for k in range(2):
                pe.matmul(bank[k][:, 0:half], g["ones"][0:1, :], g["capped"][0:1, k * half:(k + 1) * half],
                          start=True, stop=True).then_inc(s["spread"], 1)


def onehot_op(v, g, out, c):
    rel = g["rel"][:, bass.ds(c * BPC, BPC), :].rearrange("p b s -> p (b s)")
    return v.tensor_tensor(out[:, :, :], g["iota"][:, :].unsqueeze(1).to_broadcast([P, COLS, WIN]),
                           rel.unsqueeze(2).to_broadcast([P, COLS, WIN]), ALU.is_equal)


def load_bases(eng, regs, g, c):
    eng.load(regs, g["base"][0:1, bass.ds(c * BPC, BPC)])


def window(eng, reg):
    return eng.snap(reg, min_val=0, max_val=N)


def hold(gp, g, held, c):
    wait(gp, held, c)
    gp.tensor_tensor(g["spare"][0:1, 0:1], g["ones"][0:1, 0:1], g["ones"][0:1, 0:1], ALU.mult).then_inc(held, 1)


def gather_chunk(gp, idx, rows, out, done, op=ALU.bypass):
    for k in range(COLS):
        gp.indirect_dma_start(out=out[:, k, :], out_offset=None, in_=rows[:, :], compute_op=op,
                              in_offset=bass.IndirectOffsetOnAxis(ap=idx[:, k:k + 1], axis=0)).then_inc(done, 16)


def gin_sweeps(nc, a, g, h0, ew, low, span):
    with ExitStack() as ctx:
        st = Stage(nc, ctx, "gin")
        wt = st.sb("wt_edge", [P, D])
        idx = st.two("idx", [P, COLS], I32)
        hs = st.two("hs", [P, COLS, D])
        hot = st.two("hot", [P, COLS, WIN])
        ev, ews = st.two("ev", [P, COLS, D]), st.two("ews", [P, COLS, D])
        evT = st.two("evT", [P, 512])
        sums = [st.ps(f"sums{j}") for j in range(2)]
        evT_ps = [st.ps(f"evT_ps{j}") for j in range(2)]
        ew_ps = [st.ps(f"ew_ps{j}") for j in range(2)]
        bank = [st.ps(f"wbank{j}") for j in range(2)]
        w = {"bank": bank, "capped": st.sem("w_capped"), "tables": st.sem("w_tables"), "spread": st.sem("w_spread")}
        setup, held = st.sem("setup"), st.sem("held")
        idx_in, gathered, ev_in, ew_out = st.sem2("idx_in"), st.sem2("gathered"), st.sem2("ev_in"), st.sem2("ew_out")
        hot_ready, sums_ready, added = st.sem("hot_ready"), st.sem("sums_ready"), st.sem("added")
        turned, evT_sb, product, ew_sb = st.sem("turned"), st.sem("evT_sb"), st.sem("product"), st.sem("ew_sb")
        src = a["src_chunks"]
        dve_regs = [nc.vector.alloc_register(f"gin_win{b}") for b in range(BPC)]
        with nc.Block() as block:
            @block.sync
            def _(sp):
                sp.dma_start(wt[:, :], a["Wt"][D:2 * D, :]).then_inc(setup, 16)
                sp.wait_ge(setup, 16)
        first_windows(nc, g, low, "copied_gin")
        with nc.Fori(0, span + 1, WIN):
            st.clear()
            next_windows(nc, g, st, w)
            with nc.Block() as block:
                @block.sync
                def _(sp):
                    def step(f, bk):
                        if not f:
                            return
                        c, h, j = f.c, f.h, f.j
                        wait(sp, gathered[j], 16 * COLS * h)
                        sp.dma_start(idx[j][:, :], src[bass.ds(c, 1)].rearrange("a p k -> p (a k)")).then_inc(idx_in[j], 16)
                        wait(sp, turned, QUADS * (c - 1))
                        if not f.last:
                            sp.dma_start(ev[j][:, :, :].rearrange("p (b s) d -> p b s d", s=SUB),
                                         a["edge_attr"][bass.ds(c * CHUNK, CHUNK), :].rearrange(
                                             "(b p s) d -> p b s d", p=P, s=SUB)).then_inc(ev_in[j], 16)
                            return
                        full = a["edge_attr"][c * CHUNK:c * CHUNK + TAIL_BLOCKS * BLOCK, :]
                        sp.dma_start(ev[j][:, 0:TAIL_BLOCKS * SUB, :].rearrange("p (b s) d -> p b s d", s=SUB),
                                     full.rearrange("(b p s) d -> p b s d", p=P, s=SUB)).then_inc(ev_in[j], 16)
                        part = a["edge_attr"][c * CHUNK + TAIL_BLOCKS * BLOCK:E, :]
                        sp.dma_start(ev[j][0:TAIL_PARTS, TAIL_BLOCKS * SUB:(TAIL_BLOCKS + 1) * SUB, :],
                                     part.rearrange("(p s) d -> p s d", s=SUB)).then_inc(ev_in[j], 16)
                    over_chunks(sp, step)

                @block.gpsimd
                def _(gp):
                    def step(f, bk):
                        if f:
                            wait(gp, idx_in[f.j], 16 * (f.h + 1))
                            wait(gp, sums_ready, f.c - 1)
                            hold(gp, g, held, f.c)
                            gather_chunk(gp, idx[f.j], h0, hs[f.j], gathered[f.j])
                    over_chunks(gp, step)

                @block.tensor
                def _(pe):
                    def turn_edges(f, q):
                        if q == 0:
                            wait(pe, ev_in[f.j], 16 * (f.h + 1) + (16 if f.last else 0))
                        wait(pe, evT_sb, QUADS * f.c + q - 1)
                        for k in range(4):
                            mm = pe.transpose(evT_ps[q % 2][:, k * P:(k + 1) * P], ev[f.j][:, 4 * q + k, :], g["ident"][:, :])
                        mm.then_inc(turned, 1)

                    def edge_product(f, q):
                        wait(pe, evT_sb, QUADS * f.c + q + 1)
                        wait(pe, ew_sb, QUADS * f.c + q - 1)
                        for k in range(4):
                            mm = pe.matmul(ew_ps[q % 2][:, k * P:(k + 1) * P], evT[q % 2][:, k * P:(k + 1) * P],
                                           wt[:, :], start=True, stop=True)
                        mm.then_inc(product, 1)

                    def add_rows(bk):
                        c, h, j = bk.c, bk.h, bk.j
                        wait(pe, gathered[j], 16 * COLS * (h + 1))
                        wait(pe, hot_ready, c + 1)
                        wait(pe, added, (c - 1) * BPC)
                        for b in range(BPC):
                            for k in range(b * SUB, (b + 1) * SUB):
                                mm = pe.matmul(sums[j][:, b * WIN:(b + 1) * WIN], hs[j][:, k, :], hot[j][:, k, :],
                                               start=(k % SUB == 0), stop=(k % SUB == SUB - 1))
                        mm.then_inc(sums_ready, 1)

                    def step(f, bk):
                        if f:
                            turn_edges(f, 0)
                            for q in range(1, QUADS):
                                turn_edges(f, q)
                                edge_product(f, q - 1)
                            edge_product(f, QUADS - 1)
                        if bk:
                            add_rows(bk)
                    over_chunks(pe, step)

                @block.scalar
                def _(act):
                    def step(f, bk):
                        def copy_product(q):
                            wait(act, product, QUADS * f.c + q + 1)
                            if q == 0:
                                wait(act, ew_out[f.j], 16 * f.h)
                            act.activation(ews[f.j][:, 4 * q:4 * q + 4, :].rearrange("p k d -> p (k d)"),
                                           ew_ps[q % 2][:, :], ACT.Copy).then_inc(ew_sb, 1)

                        if not f:
                            return
                        for q in range(QUADS):
                            wait(act, turned, QUADS * f.c + q + 1)
                            wait(act, product, QUADS * f.c + q - 1)
                            act.activation(evT[q % 2][:, :], evT_ps[q % 2][:, :], ACT.Copy).then_inc(evT_sb, 1)
                            if q:
                                copy_product(q - 1)
                        copy_product(QUADS - 1)
                        wait(act, ew_sb, QUADS * (f.c + 1))
                        act.dma_start(ew[bass.ds(f.c, 1)].rearrange("a p n -> p (a n)"),
                                      ews[f.j][:, :, :].rearrange("p k d -> p (k d)")).then_inc(ew_out[f.j], 16)
                    over_chunks(act, step)
                    for j in range(2):
                        act.wait_ge(ew_out[j], 16 * (NCH // 2))

                @block.vector
                def _(v):
                    def step(f, bk):
                        if f:
                            wait(v, sums_ready, f.c - 1)
                            onehot_op(v, g, hot[f.j], f.c).then_inc(hot_ready, 1)
                        if bk:
                            load_bases(v, dve_regs, g, bk.c)
                            for b in range(BPC):
                                at = window(v, dve_regs[b])
                                if b == 0:
                                    wait(v, sums_ready, bk.c + 1)
                                wait(v, added, bk.c * BPC + b)
                                v.tensor_tensor(g["acc"][:, bass.ds(at, WIN)], g["acc"][:, bass.ds(at, WIN)],
                                                sums[bk.j][:, b * WIN:(b + 1) * WIN], ALU.add).then_inc(added, 1)
                    over_chunks(v, step)
                    v.wait_ge(added, NCH * BPC)


def node_mid(nc, a, g, res, arow, qk, ck):
    with ExitStack() as ctx:
        st = Stage(nc, ctx, "node_mid")
        W = {k: st.sb("w_" + k, [P, D]) for k in ("W1", "W2", "Wt", "Wq", "WkT", "b2", "bt")}
        col = {k: st.sb("c_" + k, [P, 1]) for k in ("b1", "bq", "bk", "gamma", "beta")}
        tiles = {k: st.two("m_" + k, [P, GT, D]) for k in ("x", "u", "y", "x1", "h2", "r", "hn", "hT", "A", "q", "qk")}
        cb = st.two("m_c", [1, GN])
        m = norm_buffers(st, g)
        pa = [st.ps(f"pa{u}", (P, 1024)) for u in range(2)]
        pb = [st.ps(f"pb{u}", (P, 1024)) for u in range(2)]
        weights_in = st.sem("weights_in")
        x_in, r_out, a_out, q_out = st.sem2("x_in"), st.sem2("r_out"), st.sem2("a_out"), st.sem2("q_out")
        s1 = norm_steps(st, "s1")
        s2 = norm_steps(st, "s2")
        names = ("u_ps", "u_sb", "y_ps", "y_sb", "x1", "h2", "r", "hn", "t_ps", "hT", "a_ps", "a_sb",
                 "q_ps", "q_sb", "k_ps", "c_ps", "k_sb", "c_sb")
        s = {k: st.sem("m_" + k) for k in names}
        st.clear()
        block = ctx.enter_context(nc.Block())
        x_rows = a["x"].rearrange("(g t p) d -> g p t d", t=GT, p=P)
        r_rows = res.rearrange("(g t p) d -> g p t d", t=GT, p=P)
        a_rows = arow.rearrange("(g t p) d -> g p t d", t=GT, p=P)
        n_weights = 12
        flat = lambda t: t[:, :, :].rearrange("p t d -> p (t d)")
        one = lambda rows, G: rows[bass.ds(G, 1)].rearrange("a p t d -> p (a t) d")

        def pairs(eng, steps):
            for f in steps:
                for u in range(2):
                    f(u, 0, u)
            with eng.Fori(1, GROUPS // 2) as i:
                for f in steps:
                    for u in range(2):
                        f(2 * i + u, i, u)

        @block.sync
        def _(sp):
            for k in ("W1", "W2", "Wq", "WkT"):
                sp.dma_start(W[k][:, :], a[k]).then_inc(weights_in, 16)
            sp.dma_start(W["Wt"][:, :], a["Wt"][0:D, :]).then_inc(weights_in, 16)
            for k in ("b2", "bt"):
                sp.dma_start(W[k][:, :], a[k].rearrange("(a d) -> a d", a=1).to_broadcast([P, D])).then_inc(weights_in, 16)
            for k in ("b1", "bq", "bk", "gamma", "beta"):
                sp.dma_start(col[k][:, :], a[k].rearrange("(d a) -> d a", a=1)).then_inc(weights_in, 16)

            def load(G, i, u):
                wait(sp, s["x1"], G - 1)
                sp.dma_start(tiles["x"][u][:, :, :], one(x_rows, G)).then_inc(x_in[u], 16)

            def store_r(G, i, u):
                wait(sp, s["r"], G + 1)
                sp.dma_start(one(r_rows, G), tiles["r"][u][:, :, :]).then_inc(r_out[u], 16)

            def store_a(G, i, u):
                wait(sp, s["a_sb"], G + 1)
                sp.dma_start(one(a_rows, G), tiles["A"][u][:, :, :]).then_inc(a_out[u], 16)

            def store_q(G, i, u):
                wait(sp, s["k_sb"], G + 1)
                sp.dma_start(qk[:, bass.ds(G * GN, GN)], flat(tiles["qk"][u])).then_inc(q_out[u], 16)
                wait(sp, s["c_sb"], G + 1)
                sp.dma_start(ck[:, bass.ds(G * GN, GN)], cb[u][:, :]).then_inc(q_out[u], 16)
            pairs(sp, [load, store_r, store_a, store_q])
            for u in range(2):
                sp.wait_ge(r_out[u], 16 * (GROUPS // 2))
                sp.wait_ge(a_out[u], 16 * (GROUPS // 2))
                sp.wait_ge(q_out[u], 32 * (GROUPS // 2))

        @block.tensor
        def _(pe):
            pe.wait_ge(weights_in, 16 * n_weights)

            def halves(out, u, lhsT, rhs, sem):
                for h in range(2):
                    mm = pe.matmul(out[0:lhsT.shape[1], 512 * h:512 * h + HALF], lhsT, rhs(h), start=True, stop=True)
                mm.then_inc(sem, 1)

            def by_tile(out, lhs, rhs, sem):
                for t in range(GT):
                    mm = pe.matmul(out[:, t * P:(t + 1) * P], lhs[:, t, :], rhs[:, :], start=True, stop=True)
                mm.then_inc(sem, 1)

            def first(G, i, u):
                wait(pe, s["c_sb"], G - 1)
                halves(pa[u], u, W["W1"][:, :], lambda h: g["acc"][:, bass.ds(G * GN + h * HALF, HALF)], s["u_ps"])

            def second(G, i, u):
                wait(pe, s["u_sb"], G + 1)
                wait(pe, s["k_sb"], G - 1)
                by_tile(pb[u], tiles["u"][u], W["W2"], s["y_ps"])

            def turn(G, i, u):
                wait(pe, s["hn"], (G + 1) * GT)
                for t in range(GT):
                    mm = pe.transpose(pa[u][:, t * P:(t + 1) * P], tiles["hn"][u][:, t, :], g["ident"][:, :])
                mm.then_inc(s["t_ps"], 1)

            def by_source(G, i, u):
                wait(pe, s["hT"], G + 1)
                by_tile(pb[u], tiles["hT"][u], W["Wt"], s["a_ps"])
                hT = flat(tiles["hT"][u])
                halves(pa[u], u, W["Wq"][:, :], lambda h: hT[:, h * HALF:(h + 1) * HALF], s["q_ps"])

            def by_target(G, i, u):
                wait(pe, s["q_sb"], G + 1)
                wait(pe, s["a_sb"], G + 1)
                q = flat(tiles["q"][u])
                halves(pb[u], u, W["WkT"][:, :], lambda h: q[:, h * HALF:(h + 1) * HALF], s["k_ps"])
                halves(pa[u], u, col["bk"][:, 0:1], lambda h: q[:, h * HALF:(h + 1) * HALF], s["c_ps"])
            pairs(pe, [first, second, turn, by_source, by_target])

        two = lambda ps, m=P: ps[0:m, :].rearrange("p (h n) -> p h n", h=2)[:, :, 0:HALF]
        twos = lambda t: t.rearrange("p (h n) -> p h n", h=2)

        @block.scalar
        def _(act):
            act.wait_ge(weights_in, 16 * n_weights)

            def relu1(G, i, u):
                wait(act, s["u_ps"], G + 1)
                act.activation(twos(flat(tiles["u"][u])), two(pa[u]), ACT.Relu,
                               bias=col["b1"][:, 0:1]).then_inc(s["u_sb"], 1)

            def root1(G, i, u):
                norm_root(act, m[u], s1, G)

            def root2(G, i, u):
                norm_root(act, m[u], s2, G)

            def norm1(G, i, u):
                wait(act, s1["shift"], G + 1)
                for t in range(GT):
                    act.activation(tiles["h2"][u][:, t, :], tiles["x1"][u][:, t, :], ACT.Relu,
                                   bias=m[u]["shift"][:, t:t + 1], scale=m[u]["rstd"][:, t:t + 1]).then_inc(s["h2"], 1)

            def norm2(G, i, u):
                wait(act, s2["shift"], G + 1)
                for t in range(GT):
                    act.activation(tiles["hn"][u][:, t, :], tiles["h2"][u][:, t, :], ACT.Identity,
                                   bias=m[u]["shift"][:, t:t + 1], scale=m[u]["rstd"][:, t:t + 1]).then_inc(s["hn"], 1)

            def affine(G, i, u):
                wait(act, s["t_ps"], G + 1)
                act.activation(flat(tiles["hT"][u]), pa[u][:, 0:GN], ACT.Identity,
                               bias=col["beta"][:, 0:1], scale=col["gamma"][:, 0:1]).then_inc(s["hT"], 1)

            def query(G, i, u):
                wait(act, s["q_ps"], G + 1)
                act.activation(twos(flat(tiles["q"][u])), two(pa[u]), ACT.Identity,
                               bias=col["bq"][:, 0:1]).then_inc(s["q_sb"], 1)

            def key(G, i, u):
                wait(act, q_out[u], 32 * i)
                wait(act, s["k_ps"], G + 1)
                act.activation(twos(flat(tiles["qk"][u])), two(pb[u]), ACT.Copy,
                               scale=float(D) ** -0.5).then_inc(s["k_sb"], 1)
                wait(act, s["c_ps"], G + 1)
                act.activation(twos(cb[u][:, :]), two(pa[u], 1), ACT.Copy,
                               scale=float(D) ** -0.5).then_inc(s["c_sb"], 1)
            pairs(act, [relu1, root1, norm1, root2, norm2, affine, query, key])

        @block.vector
        def _(v):
            v.wait_ge(weights_in, 16 * n_weights)

            def residual(G, i, u):
                wait(v, s["y_ps"], G + 1)
                v.tensor_tensor(tiles["y"][u][:, :, :], pb[u][:, 0:GN].rearrange("p (t d) -> p t d", t=GT),
                                W["b2"][:, :].unsqueeze(1).to_broadcast([P, GT, D]), ALU.add).then_inc(s["y_sb"], 1)
                wait(v, x_in[u], 16 * (i + 1))
                wait(v, s["y_sb"], G + 1)
                v.scalar_tensor_tensor(out=flat(tiles["x1"][u]), in0=flat(tiles["y"][u]), scalar=0.0,
                                       in1=flat(tiles["x"][u]), op0=ALU.max, op1=ALU.add).then_inc(s["x1"], 1)
                wait(v, s["x1"], G + 1)
                norm_moments(v, tiles["x1"][u], m[u], s1, G)

            def scales1(G, i, u):
                wait(v, s["hn"], (G - 1) * GT)
                norm_scales(v, m[u], s1, G)

            def scales2(G, i, u):
                norm_scales(v, m[u], s2, G)

            def renorm(G, i, u):
                wait(v, s["h2"], (G + 1) * GT)
                norm_moments(v, tiles["h2"][u], m[u], s2, G)
                wait(v, r_out[u], 16 * i)
                v.tensor_tensor(tiles["r"][u][:, :, :], tiles["x1"][u][:, :, :], tiles["h2"][u][:, :, :],
                                ALU.add).then_inc(s["r"], 1)

            def sources(G, i, u):
                wait(v, a_out[u], 16 * i)
                wait(v, s["a_ps"], G + 1)
                v.tensor_tensor(tiles["A"][u][:, :, :], pb[u][:, 0:GN].rearrange("p (t d) -> p t d", t=GT),
                                W["bt"][:, :].unsqueeze(1).to_broadcast([P, GT, D]), ALU.add).then_inc(s["a_sb"], 1)
            pairs(v, [residual, scales1, renorm, scales2, sources])


def attention_sweeps(nc, a, g, arow, ew, qk, ck, low, span):
    with ExitStack() as ctx:
        st = Stage(nc, ctx, "attention")
        acc, rows = g["acc"], g["rows"]
        wgt = st.sb("wgt", [P, NBLK * SUB])
        idx = st.two("idx", [P, COLS], I32)
        t = [st.sb(f"t{k}", [P, COLS, D]) for k in range(4)]
        tT = st.two("tT", [P, 512])
        qw, cw = st.two("qw", [P, CW]), st.two("cw", [1, CW])
        hot, attn = st.two("hot", [P, COLS, WIN]), st.two("attn", [P, COLS])
        pen, prod = st.sb("pen", [P, COLS, WIN]), st.sb("prod", [P, COLS, WIN])
        xm = st.sb("xm", [P, CW])
        bm = st.sb("bm", [2 * WIN, BPC // 2])
        mold, mnew, mdiff = st.sb("mold", [1, CW]), st.sb("mnew", [1, CW]), st.sb("mdiff", [1, CW])
        fade = st.two("fade", [P, CW])
        mx, z, pr = st.sb("mx", [P, COLS]), st.sb("z", [P, COLS]), st.sb("pr", [P, COLS])
        e_hot = st.two("e_hot", [P, COLS, WIN])
        tT_ps = [st.ps(f"tT_ps{k}") for k in range(2)]
        sc_ps = st.ps("sc_q", (P, 1024))
        b0, b1 = st.ps("back0"), st.ps("back1")
        sum_ps, tot_ps = st.ps("sum_ps"), st.ps("tot_ps")
        w = {"bank": [b0, b1],
             "capped": st.sem("w_capped"), "tables": st.sem("w_tables"), "spread": st.sem("w_spread")}
        setup, held = st.sem("setup"), st.sem("held")
        idx_in, qw_in = st.sem2("idx_in"), st.sem2("qw_in")
        ew_in, gathered = ([st.sem(f"{x}_{k}") for k in range(4)] for x in ("ew_in", "gathered"))
        names = ("t_sb", "tT_ps", "tT_sb", "sc_q",
                 "hot", "pen", "prod", "score", "attn", "masked", "xm", "xm_ps", "bm", "bm_ps",
                 "mold", "mrow", "mnew", "mdiff", "mnew_ps", "mdiff_ps", "fade", "mx_in", "mx", "z", "pr", "e_hot",
                 "sums_ps", "faded", "added", "sfaded", "sadded")
        s = {k: st.sem("a_" + k) for k in names}
        src = a["src_chunks"]
        sp_regs = [nc.sync.alloc_register(f"att_sp{b}") for b in range(BPC)]
        mid_regs = [nc.vector.alloc_register(f"att_mid{b}") for b in range(BPC)]
        last_regs = [nc.vector.alloc_register(f"att_last{b}") for b in range(BPC)]
        half = COLS // 2
        HB = BPC // 2 * WIN * SUB

        with nc.Block() as block:
            @block.sync
            def _(sp):
                sp.dma_start(wgt[:, :], a["wgt_cols"]).then_inc(setup, 16)
                sp.wait_ge(setup, 16)

            @block.vector
            def _(v):
                v.memset(acc[:, :], 0.0).then_inc(s["added"], 1)
                v.memset(rows[0:1, :], -BIG).then_inc(s["added"], 1)
                v.memset(rows[32:33, :], 0.0).then_inc(s["added"], 1)
                v.wait_ge(s["added"], 3)
        first_windows(nc, g, low, "copied_att")

        with nc.Fori(0, span + 1, WIN):
            st.clear()
            next_windows(nc, g, st, w)
            with nc.Block() as block:
                @block.sync
                def _(sp):
                    def step(f, bk):
                        if not f:
                            return
                        c, h, j = f.c, f.h, f.j
                        k, uses = f.two_before
                        wait(sp, gathered[k], 16 * COLS * uses)
                        sp.dma_start(idx[j][:, :], src[bass.ds(c, 1)].rearrange("a p k -> p (a k)")).then_inc(idx_in[j], 16)
                        wait(sp, s["sums_ps"], c - 3)
                        sp.dma_start(t[f.k][:, :, :].rearrange("p k d -> p (k d)"),
                                     ew[bass.ds(c, 1)].rearrange("a p n -> p (a n)")).then_inc(ew_in[f.k], 16)
                        load_bases(sp, sp_regs, g, c)
                        wait(sp, s["sc_q"], QUADS * (c - 1))
                        for b in range(BPC):
                            at = window(sp, sp_regs[b])
                            sp.dma_start(qw[j][:, b * WIN:(b + 1) * WIN], qk[:, bass.ds(at, WIN)]).then_inc(qw_in[j], 16)
                            sp.dma_start(cw[j][:, b * WIN:(b + 1) * WIN], ck[:, bass.ds(at, WIN)]).then_inc(qw_in[j], 16)
                    over_chunks(sp, step)

                @block.gpsimd
                def _(gp):
                    def step(f, bk):
                        if f:
                            wait(gp, idx_in[f.j], 16 * (f.h + 1))
                            wait(gp, ew_in[f.k], 16 * (f.g + 1))
                            hold(gp, g, held, f.c)
                            gather_chunk(gp, idx[f.j], arow, t[f.k], gathered[f.k], ALU.add)
                    over_chunks(gp, step)

                @block.tensor
                def _(pe):
                    def turn_gelu(f, q):
                        c, h, j = f.c, f.h, f.j
                        wait(pe, s["t_sb"], QUADS * c + q + 1)
                        wait(pe, s["tT_sb"], QUADS * c + q - 1)
                        for k in range(4):
                            mm = pe.transpose(tT_ps[q % 2][:, k * P:(k + 1) * P], t[f.k][:, 4 * q + k, :], g["ident"][:, :])
                        mm.then_inc(s["tT_ps"], 1)

                    def scores(f, q):
                        c, h, j = f.c, f.h, f.j
                        at = 512 * (q // 2)
                        if q == 0:
                            wait(pe, qw_in[j], 16 * 2 * BPC * (h + 1))
                            wait(pe, s["prod"], c)
                        wait(pe, s["tT_sb"], QUADS * c + q + 1)
                        if q % 2 == 0:
                            nb = BPC // 2
                            bias = cw[j][0:1, (q // 2) * nb * WIN:(q // 2 + 1) * nb * WIN].rearrange(
                                "p (b n) -> p b n", n=WIN)
                            pe.matmul(sc_ps[:, at:at + HB].rearrange("p (b s n) -> p b s n", s=SUB, n=WIN),
                                      g["ones"][0:1, :], bcast_mid(bias, [1, nb, SUB, WIN]), start=True, stop=True,
                                      skip_group_check=True)
                        for k in range(4):
                            n = 4 * q + k
                            o = at + (n % half) * WIN
                            mm = pe.matmul(sc_ps[:, o:o + WIN], tT[q % 2][:, k * P:(k + 1) * P],
                                           qw[j][:, (n // SUB) * WIN:(n // SUB + 1) * WIN], start=False,
                                           stop=True, skip_group_check=True)
                        mm.then_inc(s["sc_q"], 1)

                    def turn_scores(bk):
                        c, h, j = bk.c, bk.h, bk.j
                        wait(pe, s["xm"], c + 1)
                        wait(pe, s["mx_in"], c)
                        for k in range(BPC // 2):
                            mm = pe.transpose(b0[0:2 * WIN, k * P:(k + 1) * P], xm[:, k * 2 * WIN:(k + 1) * 2 * WIN],
                                              g["ident"][:, :])
                        mm.then_inc(s["xm_ps"], 1)

                    def spread_maxima(bk):
                        c, h, j = bk.c, bk.h, bk.j
                        wait(pe, s["bm"], c + 1)
                        wait(pe, s["fade"], c)
                        for k in range(BPC // 2):
                            mm = pe.matmul(b1[0:1, k * 2 * WIN:(k + 1) * 2 * WIN], bm[:, k:k + 1],
                                           g["ident"][0:2 * WIN, 0:2 * WIN], start=True, stop=True)
                        mm.then_inc(s["bm_ps"], 1)

                    def spread_running(bk):
                        c, h, j = bk.c, bk.h, bk.j
                        wait(pe, s["mnew"], c + 1)
                        pe.matmul(b0[:, 0:CW], g["ones"][0:1, :], mnew[:, :], start=True, stop=True).then_inc(s["mnew_ps"], 1)
                        wait(pe, s["mdiff"], c + 1)
                        pe.matmul(b1[:, 0:CW], g["ones"][0:1, :], mdiff[:, :], start=True, stop=True).then_inc(s["mdiff_ps"], 1)

                    def sums(bk):
                        c, h, j = bk.c, bk.h, bk.j
                        wait(pe, s["e_hot"], c + 1)
                        wait(pe, s["added"], BPC * c)
                        wait(pe, s["sadded"], BPC * c)
                        for b in range(BPC):
                            for k in range(SUB):
                                pe.matmul(sum_ps[:, b * WIN:(b + 1) * WIN], t[bk.k][:, b * SUB + k, :], e_hot[j][:, b * SUB + k, :],
                                          start=(k == 0), stop=(k == SUB - 1))
                        e = e_hot[j][:, :, :].rearrange("p (b s) n -> p b s n", s=SUB)
                        for k in range(SUB):
                            mm = pe.matmul(tot_ps[:, 0:CW].rearrange("p (b n) -> p b n", n=WIN), g["ones"][:, :], e[:, :, k, :],
                                           start=(k == 0), stop=(k == SUB - 1))
                        mm.then_inc(s["sums_ps"], 1)

                    def step(f, mid, late, last):
                        if mid:
                            turn_scores(mid)
                            spread_maxima(mid)
                        if f:
                            for q in range(QUADS):
                                turn_gelu(f, q)
                                if q:
                                    scores(f, q - 1)
                            scores(f, QUADS - 1)
                        if mid:
                            spread_running(mid)
                        if late:
                            sums(late)
                    over_stages(pe, step)

                @block.scalar
                def _(act):
                    def gelu(f, q):
                        c, h, j = f.c, f.h, f.j
                        if q == 0:
                            wait(act, gathered[f.k], 16 * COLS * (f.g + 1))
                        x = t[f.k][:, 4 * q:4 * q + 4, :]
                        act.activation(x, x, ACT.Gelu).then_inc(s["t_sb"], 1)

                    def copy_tT(f, q):
                        c, h, j = f.c, f.h, f.j
                        wait(act, s["tT_ps"], QUADS * c + q + 1)
                        wait(act, s["sc_q"], QUADS * c + q - 1)
                        act.activation(tT[q % 2][:, :], tT_ps[q % 2][:, :], ACT.Copy).then_inc(s["tT_sb"], 1)

                    def exps(bk):
                        c, h, j = bk.c, bk.h, bk.j
                        wait(act, s["mdiff_ps"], c + 1)
                        wait(act, s["faded"], BPC * (c - 1))
                        wait(act, s["sfaded"], BPC * (c - 1))
                        act.activation(fade[j][:, :], b1[:, 0:CW], ACT.Exp).then_inc(s["fade"], 1)
                        wait(act, s["z"], c + 1)
                        act.activation(pr[:, :], z[:, :], ACT.Exp).then_inc(s["pr"], 1)

                    def step(f, bk, late, last):
                        if f:
                            gelu(f, 0)
                            gelu(f, 1)
                            copy_tT(f, 0)
                            gelu(f, 2)
                            copy_tT(f, 1)
                            gelu(f, 3)
                            copy_tT(f, 2)
                            copy_tT(f, 3)
                        if bk:
                            exps(bk)
                    over_stages(act, step)

                @block.vector
                def _(v):
                    by_b = lambda x: x.rearrange("p (b s) n -> p b s n", s=SUB)
                    win3 = lambda x: x.rearrange("p (b n) -> p b n", n=WIN)
                    along = lambda x: x.unsqueeze(2).to_broadcast([P, COLS, WIN])

                    def one_hot(f):
                        c, h, j = f.c, f.h, f.j
                        wait(v, s["e_hot"], c - 1)
                        onehot_op(v, g, hot[j], c).then_inc(s["hot"], 1)

                    def penalty(f):
                        c, h, j = f.c, f.h, f.j
                        wait(v, s["hot"], c + 1)
                        wait(v, s["xm"], c)
                        v.tensor_scalar(pen[:, :, :], hot[j][:, :, :], BIG, -BIG, ALU.mult, ALU.add).then_inc(s["pen"], 1)

                    def score(f):
                        c, h, j = f.c, f.h, f.j
                        wait(v, s["sc_q"], QUADS * (c + 1))
                        wait(v, s["mx"], c)
                        v.tensor_tensor(prod[:, :, :].rearrange("p (a k) n -> p a (k n)", a=2),
                                        sc_ps[:, :].rearrange("p (a n) -> p a n", a=2)[:, :, 0:HB],
                                        hot[j][:, :, :].rearrange("p (a k) n -> p a (k n)", a=2),
                                        ALU.mult).then_inc(s["prod"], 1)
                        wait(v, s["prod"], c + 1)
                        v.tensor_reduce(attn[j][:, :], prod[:, :, :], AX.X, ALU.add).then_inc(s["score"], 1)
                        wait(v, s["score"], c + 1)
                        v.tensor_tensor(attn[j][:, :], attn[j][:, :], wgt[:, bass.ds(c * COLS, COLS)],
                                        ALU.mult).then_inc(s["attn"], 1)
                        wait(v, s["attn"], c + 1)
                        wait(v, s["pen"], c + 1)
                        v.tensor_tensor(pen[:, :, :], pen[:, :, :], along(attn[j][:, :]), ALU.add).then_inc(s["masked"], 1)
                        wait(v, s["masked"], c + 1)
                        wait(v, s["xm_ps"], c)
                        x = by_b(pen[:, :, :])
                        v.tensor_tensor(win3(xm[:, :]), x[:, :, 0, :], x[:, :, 1, :], ALU.max).then_inc(s["xm"], 1)

                    def block_maxima(bk):
                        c, h, j = bk.c, bk.h, bk.j
                        wait(v, s["xm_ps"], c + 1)
                        wait(v, s["bm_ps"], c)
                        v.tensor_reduce(bm[:, :], b0[0:2 * WIN, :].rearrange("p (k e) -> p k e", e=P), AX.X,
                                        ALU.max).then_inc(s["bm"], 1)

                    def update_nodes(mid, last):
                        if mid:
                            load_bases(v, mid_regs, g, mid.c)
                        if last:
                            load_bases(v, last_regs, g, last.c)
                        for b in range(BPC):
                            cols = slice(b * WIN, (b + 1) * WIN)
                            if mid:
                                m = BPC * mid.c + b
                                at = window(v, mid_regs[b])
                                if b == 0:
                                    wait(v, s["bm_ps"], mid.c + 1)
                                top = rows[0:1, bass.ds(at, WIN)]
                                wait(v, s["mrow"], m)
                                if b == 0:
                                    wait(v, s["mdiff"], mid.c)
                                v.tensor_copy(mold[0:1, cols], top).then_inc(s["mold"], 1)
                            if last:
                                n = BPC * last.c + b
                                at = window(v, last_regs[b])
                                if b == 0:
                                    wait(v, s["sums_ps"], last.c + 1)
                                    wait(v, s["fade"], last.c + 1)
                                nodes, total = acc[:, bass.ds(at, WIN)], rows[32:33, bass.ds(at, WIN)]
                                wait(v, s["added"], n)
                                v.tensor_tensor(nodes, nodes, fade[last.j][:, cols], ALU.mult).then_inc(s["faded"], 1)
                                wait(v, s["sadded"], n)
                                v.tensor_tensor(total, total, fade[last.j][32:33, cols], ALU.mult).then_inc(s["sfaded"], 1)
                            if mid:
                                wait(v, s["mold"], m + 1)
                                v.tensor_tensor(top, mold[0:1, cols], b1[0:1, cols], ALU.max).then_inc(s["mrow"], 1)
                            if last:
                                wait(v, s["faded"], n + 1)
                                v.tensor_tensor(nodes, nodes, sum_ps[:, cols], ALU.add).then_inc(s["added"], 1)
                                wait(v, s["sfaded"], n + 1)
                                v.tensor_tensor(total, total, tot_ps[32:33, cols], ALU.add).then_inc(s["sadded"], 1)

                    def risen(bk):
                        c = bk.c
                        wait(v, s["mnew_ps"], c)
                        wait(v, s["mdiff_ps"], c)
                        v.tensor_tensor(mnew[:, :], mold[:, :], b1[0:1, 0:CW], ALU.max).then_inc(s["mnew"], 1)
                        wait(v, s["mnew"], c + 1)
                        v.tensor_tensor(mdiff[:, :], mold[:, :], mnew[:, :], ALU.subtract).then_inc(s["mdiff"], 1)

                    def below_maximum(bk):
                        c, h, j = bk.c, bk.h, bk.j
                        wait(v, s["mnew_ps"], c + 1)
                        wait(v, s["score"], c + 1)
                        v.tensor_tensor(by_b(prod[:, :, :]), by_b(hot[j][:, :, :]),
                                        bcast_mid(win3(b0[:, 0:CW]), [P, BPC, SUB, WIN]), ALU.mult).then_inc(s["mx_in"], 1)
                        wait(v, s["mx_in"], c + 1)
                        v.tensor_reduce(mx[:, :], prod[:, :, :], AX.X, ALU.add).then_inc(s["mx"], 1)
                        wait(v, s["mx"], c + 1)
                        wait(v, s["pr"], c)
                        v.tensor_tensor(z[:, :], attn[j][:, :], mx[:, :], ALU.subtract).then_inc(s["z"], 1)

                    def spread_e(bk):
                        c, h, j = bk.c, bk.h, bk.j
                        wait(v, s["pr"], c + 1)
                        wait(v, s["sums_ps"], c - 1)
                        v.tensor_tensor(e_hot[j][:, :, :], hot[j][:, :, :], along(pr[:, :]), ALU.mult).then_inc(s["e_hot"], 1)

                    def step(f, mid, late, last):
                        if mid:
                            block_maxima(mid)
                        if f:
                            one_hot(f)
                            penalty(f)
                        update_nodes(mid, last)
                        if mid:
                            risen(mid)
                            below_maximum(mid)
                        if f:
                            score(f)
                        if mid:
                            spread_e(mid)
                    over_stages(v, step)
                    v.wait_ge(s["added"], NCH * BPC)
                    v.wait_ge(s["sadded"], NCH * BPC)


def node_end(nc, a, g, res):
    with ExitStack() as ctx:
        st = Stage(nc, ctx, "node_end")
        wv, bv = st.sb("wv", [P, D]), st.sb("bv_row", [1, D])
        tc, gl, rr, oo = (st.two("e_" + k, [P, GT, D]) for k in ("tc", "gl", "rr", "oo"))
        sr = st.two("e_s", [1, GN])
        den, rden = st.two("e_den", [P, GT]), st.two("e_rden", [P, GT])
        pv = [st.ps(f"pv{u}", (P, 1024)) for u in range(2)]
        pd = [st.ps(f"pd{u}") for u in range(2)]
        names = ("tc", "sr", "pv", "den", "rden", "gl", "oo")
        s = {k: st.sem("e_" + k) for k in names}
        weights_in, r_in, o_out = st.sem("ew_in"), st.sem2("er_in"), st.sem2("eo_out")
        r_rows = res.rearrange("(g t p) d -> g p t d", t=GT, p=P)
        o_rows = a["out"].rearrange("(g t p) d -> g p t d", t=GT, p=P)
        one = lambda rows, G: rows[bass.ds(G, 1)].rearrange("a p t d -> p (a t) d")
        st.clear()
        block = ctx.enter_context(nc.Block())

        def pairs(eng, steps):
            for f in steps:
                for u in range(2):
                    f(u, 0, u)
            with eng.Fori(1, GROUPS // 2) as i:
                for f in steps:
                    for u in range(2):
                        f(2 * i + u, i, u)

        @block.sync
        def _(sp):
            sp.dma_start(wv[:, :], a["Wv"]).then_inc(weights_in, 16)
            sp.dma_start(bv[:, :], a["bv"].rearrange("(a d) -> a d", a=1)).then_inc(weights_in, 16)

            def load(G, i, u):
                wait(sp, s["oo"], G - 1)
                sp.dma_start(rr[u][:, :, :], one(r_rows, G)).then_inc(r_in[u], 16)

            def store(G, i, u):
                wait(sp, s["oo"], G + 1)
                sp.dma_start(one(o_rows, G), oo[u][:, :, :]).then_inc(o_out[u], 16)
            pairs(sp, [load, store])
            for u in range(2):
                sp.wait_ge(o_out[u], 16 * (GROUPS // 2))

        @block.scalar
        def _(act):
            def take(G, i, u):
                wait(act, s["pv"], G - 1)
                act.activation(tc[u][:, :, :].rearrange("p t d -> p (t d)"), g["acc"][:, bass.ds(G * GN, GN)],
                               ACT.Copy).then_inc(s["tc"], 1)
                act.activation(sr[u][0:1, :], g["rows"][32:33, bass.ds(G * GN, GN)], ACT.Copy).then_inc(s["sr"], 1)

            def gelu(G, i, u):
                wait(act, s["pv"], G + 1)
                wait(act, s["rden"], G + 1)
                wait(act, s["oo"], G - 1)
                for t in range(GT):
                    act.activation(gl[u][:, t, :], pv[u][:, t * P:(t + 1) * P], ACT.Gelu,
                                   scale=rden[u][:, t:t + 1]).then_inc(s["gl"], 1)
            pairs(act, [take, gelu])

        @block.tensor
        def _(pe):
            pe.wait_ge(weights_in, 32)

            def products(G, i, u):
                wait(pe, s["tc"], G + 1)
                wait(pe, s["sr"], G + 1)
                wait(pe, s["gl"], (G - 1) * GT)
                for t in range(GT):
                    out, sums = pv[u][:, t * P:(t + 1) * P], sr[u][0:1, t * P:(t + 1) * P]
                    pe.matmul(out, tc[u][:, t, :], wv[:, :], start=True, stop=False)
                    pe.matmul(out, sums, bv[:, :], start=False, stop=True)
                for t in range(GT):
                    mm = pe.matmul(pd[u][:, t:t + 1], sr[u][0:1, t * P:(t + 1) * P], g["ones"][0:1, 0:1],
                                   start=True, stop=True)
                mm.then_inc(s["pv"], 1)
            pairs(pe, [products])

        @block.vector
        def _(v):
            def inverse(G, i, u):
                wait(v, s["gl"], (G - 1) * GT)
                wait(v, s["pv"], G + 1)
                v.tensor_scalar(den[u][:, :], pd[u][:, 0:GT], SM_EPS, None, ALU.add).then_inc(s["den"], 1)
                wait(v, s["den"], G + 1)
                v.reciprocal(rden[u][:, :], den[u][:, :]).then_inc(s["rden"], 1)

            def finish(G, i, u):
                wait(v, s["gl"], (G + 1) * GT)
                wait(v, r_in[u], 16 * (i + 1))
                wait(v, o_out[u], 16 * i)
                v.tensor_tensor(oo[u][:, :, :], gl[u][:, :, :], rr[u][:, :, :], ALU.add).then_inc(s["oo"], 1)
            pairs(v, [inverse, finish])


def kernel(x, src, dst, edge_attr_128, edge_weight1, L0_gnn_eps, L0_gnn_W1, L0_gnn_b1, L0_gnn_W2, L0_gnn_b2,
           L1_gnn_gamma, L1_gnn_beta, L1_gnn_Wt, L1_gnn_bt, L1_gnn_Wq, L1_gnn_bq, L1_gnn_Wk, L1_gnn_bk,
           L1_gnn_Wv, L1_gnn_bv):
    import concourse.bacc as bacc
    from concourse.bass_utils import run_bass_kernel_spmd

    pad = NCH * CHUNK - E

    def chunked(v, fill):
        v = np.concatenate([np.asarray(v).reshape(-1), np.full(pad, fill, np.asarray(v).dtype)])
        return v.reshape(NCH, BPC, P, SUB).transpose(0, 2, 1, 3)

    dst_pad = np.concatenate([np.asarray(dst), np.full(pad, N, np.asarray(dst).dtype)])
    cols = lambda v: np.ascontiguousarray(v.transpose(1, 0, 2, 3).reshape(P, NBLK * SUB))
    arrays = {
        "x": np.pad(np.asarray(x), ((0, NP - N), (0, 0))),
        "src_chunks": np.ascontiguousarray(chunked(src, 0).reshape(NCH, P, COLS)),
        "dst_cols": cols(chunked(dst, N)),
        "dst_blocks": dst_pad.reshape(NBLK, BLOCK),
        "wgt_cols": cols(chunked(edge_weight1, 0)),
        "edge_attr": np.asarray(edge_attr_128),
        "eps": np.asarray(L0_gnn_eps).reshape(1, 1),
        "W1": L0_gnn_W1, "b1": L0_gnn_b1, "W2": L0_gnn_W2, "b2": L0_gnn_b2,
        "gamma": L1_gnn_gamma, "beta": L1_gnn_beta, "Wt": L1_gnn_Wt, "bt": L1_gnn_bt,
        "Wq": L1_gnn_Wq, "bq": L1_gnn_bq, "WkT": np.ascontiguousarray(np.asarray(L1_gnn_Wk).T), "bk": L1_gnn_bk,
        "Wv": L1_gnn_Wv, "bv": L1_gnn_bv,
    }
    arrays = {k: np.ascontiguousarray(v) for k, v in arrays.items()}
    nc = bacc.Bacc("TRN2", target_bir_lowering=False, num_devices=1)
    a = {k: nc.dram_tensor("in_" + k, list(v.shape), mybir.dt.from_np(v.dtype), kind="ExternalInput").ap()
         for k, v in arrays.items()}
    a["out"] = nc.dram_tensor("out_rows", [NP, D], F32, kind="ExternalOutput").ap()
    build_gnn(nc, a)
    r = run_bass_kernel_spmd(nc, [{"in_" + k: v for k, v in arrays.items()}], core_ids=[0])
    return r.results[0]["out_rows"][:N]
```

```python
from contextlib import ExitStack

import numpy as np

import concourse.bass as bass
from concourse import mybir
from concourse.alu_op_type import AluOpType as ALU

F32 = mybir.dt.float32
I32 = mybir.dt.int32
BF16 = mybir.dt.bfloat16
ACT = mybir.ActivationFunctionType
AX = mybir.AxisListType

P = 128
D = 128
N = 12500
E = 200000
WIN = 40
SUB = 2
BLOCK = P * SUB
BPC = 8
CHUNK = BPC * BLOCK
COLS = BPC * SUB
NCH = -(-E // CHUNK)
NBLK = NCH * BPC
QUADS = COLS // 4
CW = BPC * WIN
SPAN = 264
BIG = 1e30
FAR = 1e38
TILES = -(-(N + WIN) // P)
NP = TILES * P
PARTS = 4
WIDE = 96
QSPAN = SPAN - WIN + WIDE
NW = -(-(N + QSPAN) // P) * P
GT = 7
GROUPS = TILES // GT
GN = GT * P
HALF = GN // 2
PB = 112
KB = NBLK // PB
LN_EPS = 1e-5
SM_EPS = 1e-16
PEEL = 4
TAIL = E - (NCH - 1) * CHUNK
TAIL_BLOCKS = TAIL // BLOCK
TAIL_PARTS = (TAIL - TAIL_BLOCKS * BLOCK) // SUB
assert TILES % (2 * GT) == 0 and NBLK % PB == 0 and NCH % 4 == 2 and TAIL % SUB == 0 and HALF <= 512


def wait(eng, sem, value):
    if isinstance(value, int) and value <= 0:
        return
    eng.wait_ge(sem, value)


class Chunk:

    def __init__(self, base, n):
        self.j, self.k = n % 2, n % 4
        self.c = n if base is None else 4 * base + n
        self.h = n // 2 if base is None else 2 * base + n // 2
        self.g = n // 4 if base is None else base + n // 4
        self.last = base is None and n == NCH - 1
        self.two_before = (n - 2) % 4, (n - 2) // 4 + 1 if base is None else base + (n - 2) // 4 + 1


def over_chunks(eng, step):
    step(Chunk(None, 0), None)
    for n in range(1, PEEL):
        step(Chunk(None, n), Chunk(None, n - 1))
    with eng.Fori(0, (NCH - PEEL - 2) // 4) as i:
        for n in range(PEEL, PEEL + 4):
            step(Chunk(i, n), Chunk(i, n - 1))
    for n in range(NCH - 2, NCH):
        step(Chunk(None, n), Chunk(None, n - 1))
    step(None, Chunk(None, NCH - 1))


def over_stages(eng, step):
    def at(base, n):
        step(*(Chunk(base, n - k) if base is not None or 0 <= n - k < NCH else None for k in range(4)))

    for n in range(PEEL):
        at(None, n)
    with eng.Fori(0, (NCH - PEEL - 2) // 4) as i:
        for n in range(PEEL, PEEL + 4):
            at(i, n)
    for n in range(NCH - 2, NCH + 3):
        at(None, n)


def bcast_mid(ap, shape):
    return ap.unsqueeze(2).to_broadcast(shape)


def build_gnn(nc, a):
    with ExitStack() as ctx:
        def sb(name, shape, dt=F32):
            return ctx.enter_context(nc.sbuf_tensor(name, shape, dt))

        h0 = nc.dram_tensor("h0_rows", [NP, D], F32, kind="Internal").ap()
        res = nc.dram_tensor("residual_rows", [NP, D], F32, kind="Internal").ap()
        arow = nc.dram_tensor("source_rows", [NP, D], F32, kind="Internal").ap()
        qk = nc.dram_tensor("qk_cols", [D, NW], F32, kind="Internal").ap()
        ck = nc.dram_tensor("qk_bias_cols", [1, NW], F32, kind="Internal").ap()
        fades = nc.dram_tensor("fades", [2, SPAN], F32, kind="Internal").ap()
        ew = nc.dram_tensor("edge_products", [NCH, P, COLS * D], F32, kind="Internal").ap()
        first = nc.dram_tensor("first_starts", [1, NBLK + NCH], F32, kind="Internal").ap()

        g = {
            "acc": sb("acc", [P, NW]),
            "ident": sb("ident", [P, P]),
            "ones": sb("ones", [P, P]),
            "iota": sb("iota", [P, WIN]),
            "dst": sb("dst", [P, NBLK, SUB]),
            "rel": sb("rel", [P, NBLK, SUB]),
            "start": sb("start", [1, NBLK + NCH]),
            "capped": sb("capped", [1, NBLK + NCH]),
            "base": sb("base", [1, NBLK + NCH], I32),
            "offset": sb("offset", [1, NBLK], I32),
            "span": sb("span", [1, 1], I32),
            "eps1": sb("eps1", [P, 1]),
            "spare": sb("spare", [1, 1]),
        }
        constants(nc, a, g)
        node_norm(nc, a, g, h0)
        edge_tables(nc, a, g, first)
        span = nc.values_load(g["span"][0:1, 0:1], min_val=0, max_val=N)
        gin_sweeps(nc, a, g, h0, ew, first, span)
        node_mid(nc, a, g, res, arow, qk, ck)
        with nc.sbuf_tensor("rows", [33, NW], F32) as rows:
            g["rows"] = rows
            attention_sweeps(nc, a, g, arow, ew, qk, ck, fades, first, span)
            node_end(nc, a, g, res)


class Stage:

    def __init__(self, nc, ctx, name):
        self.nc, self.ctx, self.name, self.sems = nc, ctx, name, []

    def sb(self, name, shape, dt=F32):
        return self.ctx.enter_context(self.nc.sbuf_tensor(f"{self.name}_{name}", shape, dt))

    def two(self, name, shape, dt=F32):
        return [self.sb(f"{name}{j}", shape, dt) for j in range(2)]

    def ps(self, name, shape=(P, 512)):
        return self.ctx.enter_context(self.nc.psum_tensor(f"{self.name}_{name}", list(shape), F32))

    def sem(self, name):
        s = self.ctx.enter_context(self.nc.semaphore(f"{self.name}_{name}"))
        self.sems.append(s)
        return s

    def sem2(self, name):
        return [self.sem(f"{name}_{j}") for j in range(2)]

    def clear(self, gathers=False):
        self.nc.all_engine_barrier()
        if gathers:
            self.nc.gpsimd.dma_reset()
            self.nc.all_engine_barrier()
        for s in self.sems:
            self.nc.sync.sem_clear(s)
        self.nc.all_engine_barrier()


def constants(nc, a, g):
    with ExitStack() as ctx:
        st = Stage(nc, ctx, "constants")
        iota_i = st.sb("iota_i", [P, WIN], I32)
        zeroed, identity_ready, iota_ready = st.sem("zeroed"), st.sem("identity_ready"), st.sem("iota_ready")
        eps_in, ones_ready, float_ready = st.sem("eps_in"), st.sem("ones_ready"), st.sem("float_ready")
        block = ctx.enter_context(nc.Block())

        @block.sync
        def _(sp):
            sp.dma_start(g["eps1"][:, :], a["eps"].to_broadcast([P, 1])).then_inc(eps_in, 16)

        @block.gpsimd
        def _(gp):
            gp.memset(g["ident"][:, :], 0.0).then_inc(zeroed, 1)
            gp.iota(iota_i[:, :], pattern=[[1, WIN]], base=0, channel_multiplier=0).then_inc(iota_ready, 1)
            gp.wait_ge(zeroed, 1)
            gp.affine_select(out=g["ident"][:, :], in_=g["ident"][:, :], compare_op=ALU.not_equal, fill=1.0,
                             base=0, pattern=[[-1, P]], channel_multiplier=1).then_inc(identity_ready, 1)
            gp.wait_ge(identity_ready, 1)

        @block.vector
        def _(v):
            v.memset(g["ones"][:, :], 1.0).then_inc(ones_ready, 1)
            v.wait_ge(iota_ready, 1)
            v.tensor_copy(g["iota"][:, :], iota_i[:, :]).then_inc(float_ready, 1)
            v.wait_ge(eps_in, 16)
            v.tensor_scalar(g["eps1"][:, :], g["eps1"][:, :], 1.0, None, ALU.add).then_inc(float_ready, 1)
            v.wait_ge(float_ready, 2)
            v.wait_ge(ones_ready, 1)


NORM_STEPS = ("stats", "held", "means", "var", "std", "rstd", "shift")


def norm_steps(st, name):
    return {**{k: st.sem(f"{name}_{k}") for k in NORM_STEPS}, "spare": st.sb(name + "_spare", [1, 1])}


def norm_moments(v, x, m, s, G):
    for t in range(GT):
        v.bn_stats(m["stats"][:, t, :], x[:, t, :]).then_inc(s["stats"], 1)
    wait(v, s["stats"], (G + 1) * GT)
    wait(v, s["held"], G)
    v.tensor_tensor(s["spare"][:, :], m["eps"][0:1, 0:1], m["eps"][0:1, 0:1], ALU.mult).then_inc(s["held"], 1)
    for t in range(GT):
        v.bn_aggr(m["mv"][:, t, :], m["stats"][:, t, :]).then_inc(s["means"], 1)
    wait(v, s["means"], (G + 1) * GT)
    v.tensor_scalar(m["var"][:, :], m["mv"][:, :, 1], LN_EPS, None, ALU.add).then_inc(s["var"], 1)


def norm_root(act, m, s, G):
    wait(act, s["var"], G + 1)
    wait(act, s["rstd"], G - 1)
    act.activation(m["std"][:, :], m["var"][:, :], ACT.Sqrt).then_inc(s["std"], 1)


def norm_scales(v, m, s, G):
    wait(v, s["std"], G + 1)
    v.reciprocal(m["rstd"][:, :], m["std"][:, :]).then_inc(s["rstd"], 1)
    wait(v, s["rstd"], G + 1)
    v.scalar_tensor_tensor(out=m["shift"][:, :], in0=m["mv"][:, :, 0], scalar=-1.0, in1=m["rstd"][:, :],
                           op0=ALU.mult, op1=ALU.mult).then_inc(s["shift"], 1)


def norm_buffers(st, g):
    return [{"stats": st.sb(f"stats{u}", [P, GT, 6]), "mv": st.sb(f"mv{u}", [P, GT, 2]), "eps": g["eps1"],
             **{k: st.sb(f"{k}{u}", [P, GT]) for k in ("var", "std", "rstd", "shift")}} for u in range(2)]


def node_norm(nc, a, g, h0):
    with ExitStack() as ctx:
        st = Stage(nc, ctx, "node_norm")
        x, h = st.two("x", [P, GT, D]), st.two("h", [P, GT, D])
        m = norm_buffers(st, g)
        hT = [st.ps(f"hT{u}", (P, 1024)) for u in range(2)]
        x_in, h_out = st.sem2("x_in"), st.sem2("h_out")
        s = norm_steps(st, "n")
        h_ready, hT_ready, acc_ready = st.sem("h_ready"), st.sem("hT_ready"), st.sem("acc_ready")
        x_rows = a["x"].rearrange("(g t p) d -> g p t d", t=GT, p=P)
        h_rows = h0.rearrange("(g t p) d -> g p t d", t=GT, p=P)
        st.clear()
        block = ctx.enter_context(nc.Block())

        def pairs(eng, step):
            for u in range(2):
                step(u, 0, u)
            with eng.Fori(1, GROUPS // 2) as i:
                for u in range(2):
                    step(2 * i + u, i, u)

        @block.sync
        def _(sp):
            def step(G, i, u):
                wait(sp, h_ready, (G - 1) * GT)
                sp.dma_start(x[u][:, :, :], x_rows[bass.ds(G, 1)].rearrange("a p t d -> p (a t) d")).then_inc(x_in[u], 16)
            pairs(sp, step)

        @block.vector
        def _(v):
            def moments(G, i, u):
                wait(v, x_in[u], 16 * (i + 1))
                norm_moments(v, x[u], m[u], s, G)

            def scales(G, i, u):
                wait(v, h_ready, (G - 1) * GT)
                norm_scales(v, m[u], s, G)
            for f in (moments, scales):
                for u in range(2):
                    f(u, 0, u)
            with v.Fori(1, GROUPS // 2) as i:
                for f in (moments, scales):
                    for u in range(2):
                        f(2 * i + u, i, u)

        @block.scalar
        def _(act):
            def root(G, i, u):
                norm_root(act, m[u], s, G)

            def scale(G, i, u):
                wait(act, s["shift"], G + 1)
                wait(act, h_out[u], 16 * i)
                wait(act, hT_ready, G - 1)
                for t in range(GT):
                    act.activation(h[u][:, t, :], x[u][:, t, :], ACT.Relu, bias=m[u]["shift"][:, t:t + 1],
                                   scale=m[u]["rstd"][:, t:t + 1]).then_inc(h_ready, 1)

            def keep(G, i, u):
                wait(act, h_ready, (G + 1) * GT)
                act.dma_start(h_rows[bass.ds(G, 1)].rearrange("a p t d -> p (a t) d"), h[u][:, :, :]).then_inc(h_out[u], 16)
                wait(act, hT_ready, G + 1)
                act.activation(g["acc"][:, bass.ds(G * GN, GN)], hT[u][:, 0:GN], ACT.Copy,
                               scale=g["eps1"][:, 0:1]).then_inc(acc_ready, 1)
            def both(i, first):
                for f in (root, scale, keep):
                    for u in range(2):
                        f(2 * i + u if not first else u, i, u)
            both(0, True)
            with act.Fori(1, GROUPS // 2) as i:
                both(i, False)
            for u in range(2):
                act.wait_ge(h_out[u], 16 * (GROUPS // 2))
            act.wait_ge(acc_ready, GROUPS)

        @block.tensor
        def _(pe):
            def step(G, i, u):
                wait(pe, h_ready, (G + 1) * GT)
                wait(pe, acc_ready, G - 1)
                for t in range(GT):
                    mm = pe.transpose(hT[u][:, t * P:(t + 1) * P], h[u][:, t, :], g["ident"][:, :])
                mm.then_inc(hT_ready, 1)
            pairs(pe, step)


def edge_tables(nc, a, g, first):
    with ExitStack() as ctx:
        st = Stage(nc, ctx, "edge")
        by_block = st.sb("by_block", [PB, KB, BLOCK], I32)
        by_edge = st.sb("by_edge", [P, NBLK, SUB], I32)
        low, high = st.sb("low_p", [PB, KB]), st.sb("high_p", [PB, KB])
        low_row, high_row, wide = (st.sb(x, [1, NBLK]) for x in ("low_row", "high_row", "wide"))
        chunk_low, latest = st.sb("chunk_low", [1, NCH]), st.sb("latest", [1, NCH])
        start = g["start"]
        low_ps, high_ps = st.ps("low_ps", (P, 1024)), st.ps("high_ps", (P, 1024))
        dst_in, blocks_in = st.sem("dst_in"), st.sem("blocks_in")
        low_ready, high_ready, low_turned = st.sem("low_ready"), st.sem("high_ready"), st.sem("low_turned")
        high_turned, copied, chunks_ready = st.sem("high_turned"), st.sem("copied"), st.sem("chunks_ready")
        latest_ready, start_ready, tables_ready = st.sem("latest_ready"), st.sem("start_ready"), st.sem("tables_ready")
        start_out = st.sem("start_out")
        by_chunk = lambda x: x.rearrange("p (c b) -> p c b", b=BPC)
        st.clear()
        block = ctx.enter_context(nc.Block())

        @block.sync
        def _(sp):
            sp.dma_start(by_block[:, :, :], a["dst_blocks"].rearrange("(k p) e -> p k e", p=PB)).then_inc(blocks_in, 16)
            sp.dma_start(by_edge[:, :, :], a["dst_cols"].rearrange("p (b s) -> p b s", s=SUB)).then_inc(dst_in, 16)
            sp.wait_ge(start_ready, 2)
            sp.dma_start(first, start[:, :]).then_inc(start_out, 16)
            sp.wait_ge(start_out, 16)

        @block.vector
        def _(v):
            v.wait_ge(blocks_in, 16)
            v.tensor_reduce(low[:, :], by_block[:, :, :], AX.X, ALU.min).then_inc(low_ready, 1)
            v.tensor_reduce(high[:, :], by_block[:, :, :], AX.X, ALU.max).then_inc(high_ready, 1)
            v.wait_ge(dst_in, 16)
            v.tensor_copy(g["dst"][:, :, :], by_edge[:, :, :]).then_inc(tables_ready, 1)
            v.wait_ge(low_turned, 1)
            v.wait_ge(high_turned, 1)
            for half in range(2):
                at, n = 4 * PB * half, min(KB - 4 * half, 4) * PB
                v.tensor_copy(low_row[0:1, at:at + n], low_ps[0:1, 512 * half:512 * half + n]).then_inc(copied, 1)
                v.tensor_copy(high_row[0:1, at:at + n], high_ps[0:1, 512 * half:512 * half + n]).then_inc(copied, 1)
            v.wait_ge(copied, 4)
            v.tensor_reduce(chunk_low[:, :], by_chunk(low_row[:, :]), AX.X, ALU.min).then_inc(chunks_ready, 1)
            v.wait_ge(chunks_ready, 1)
            v.tensor_scalar(latest[:, :], chunk_low[:, :], float(SPAN - WIN), None, ALU.add).then_inc(latest_ready, 1)
            v.tensor_copy(start[0:1, NBLK:NBLK + NCH], chunk_low[:, :]).then_inc(start_ready, 1)
            v.wait_ge(latest_ready, 1)
            v.tensor_tensor(by_chunk(start[0:1, 0:NBLK]), by_chunk(low_row[:, :]),
                            latest[:, :].unsqueeze(2).to_broadcast([1, NCH, BPC]), ALU.min).then_inc(start_ready, 1)
            v.wait_ge(start_ready, 2)
            v.tensor_tensor(wide[:, :], high_row[:, :], start[0:1, 0:NBLK], ALU.subtract).then_inc(tables_ready, 1)
            v.wait_ge(tables_ready, 2)
            v.tensor_reduce(g["span"][0:1, 0:1], wide[:, :], AX.X, ALU.max).then_inc(tables_ready, 1)
            v.wait_ge(tables_ready, 3)

        @block.tensor
        def _(pe):
            def turn(column, out, ready, turned):
                pe.wait_ge(ready, 1)
                for k in range(KB):
                    at = 512 * (k // 4) + PB * (k % 4)
                    mm = pe.matmul(out[0:1, at:at + PB], column[:, k:k + 1], g["ident"][0:PB, 0:PB], start=True, stop=True)
                mm.then_inc(turned, 1)
            turn(low, low_ps, low_ready, low_turned)
            turn(high, high_ps, high_ready, high_turned)


def next_windows(nc, g, st, s):
    bank = s["bank"]
    half = NBLK // 2
    with nc.Block() as block:
        @block.vector
        def _(v):
            v.tensor_scalar(g["capped"][:, :], g["start"][:, :], float(N), None, ALU.min).then_inc(s["capped"], 1)
            v.wait_ge(s["capped"], 1)
            v.tensor_copy(g["base"][:, :], g["capped"][:, :]).then_inc(s["tables"], 1)
            v.tensor_tensor(g["offset"][:, :].rearrange("p (c b) -> p c b", b=BPC),
                            g["capped"][0:1, 0:NBLK].rearrange("p (c b) -> p c b", b=BPC),
                            g["capped"][0:1, NBLK:NBLK + NCH].unsqueeze(2).to_broadcast([1, NCH, BPC]),
                            ALU.subtract).then_inc(s["tables"], 1)
            v.tensor_scalar(g["start"][:, :], g["start"][:, :], float(WIN), None, ALU.add).then_inc(s["tables"], 1)
            v.wait_ge(s["spread"], 2)
            for k in range(2):
                v.tensor_tensor(g["rel"][:, k * half:(k + 1) * half, :], g["dst"][:, k * half:(k + 1) * half, :],
                                bank[k][:, 0:half].unsqueeze(2).to_broadcast([P, half, SUB]),
                                ALU.subtract).then_inc(s["tables"], 1)
            v.wait_ge(s["tables"], 5)

        @block.tensor
        def _(pe):
            pe.wait_ge(s["capped"], 1)
            for k in range(2):
                pe.matmul(bank[k][:, 0:half], g["ones"][0:1, :], g["capped"][0:1, k * half:(k + 1) * half],
                          start=True, stop=True).then_inc(s["spread"], 1)


def onehot_op(v, g, out, c, op=ALU.is_equal):
    rel = g["rel"][:, bass.ds(c * BPC, BPC), :].rearrange("p b s -> p (b s)")
    return v.tensor_tensor(out[:, :, :], g["iota"][:, :].unsqueeze(1).to_broadcast([P, COLS, WIN]),
                           rel.unsqueeze(2).to_broadcast([P, COLS, WIN]), op)


def load_bases(eng, regs, g, c):
    eng.load(regs, g["base"][0:1, bass.ds(c * BPC, BPC)])


def load_span(eng, reg, g, c):
    eng.load([reg], g["base"][0:1, bass.ds(NBLK + c, 1)])


def load_offsets(eng, regs, g, c):
    eng.load(regs, g["offset"][0:1, bass.ds(c * BPC, BPC)])


def window(eng, reg):
    return eng.snap(reg, min_val=0, max_val=N)


def inside(eng, reg):
    return eng.snap(reg, min_val=0, max_val=SPAN - WIN)


def hold(gp, g, held, c):
    wait(gp, held, c)
    gp.tensor_tensor(g["spare"][0:1, 0:1], g["ones"][0:1, 0:1], g["ones"][0:1, 0:1], ALU.mult).then_inc(held, 1)


def gather_chunk(gp, idx, rows, out, done, op=ALU.bypass, cols=range(COLS)):
    for k in cols:
        gp.indirect_dma_start(out=out[:, k, :], out_offset=None, in_=rows[:, :], compute_op=op,
                              in_offset=bass.IndirectOffsetOnAxis(ap=idx[:, k:k + 1], axis=0)).then_inc(done, 16)


def gin_sweeps(nc, a, g, h0, ew, first, span):
    with ExitStack() as ctx:
        st = Stage(nc, ctx, "gin")
        wt = st.sb("wt_edge", [P, D])
        idx = st.two("idx", [P, COLS], I32)
        hs = st.two("hs", [P, COLS, D])
        hot = st.two("hot", [P, COLS, WIN])
        ev, ews = st.two("ev", [P, COLS, D]), st.two("ews", [P, COLS, D])
        evT = st.two("evT", [P, 512])
        sums = [st.ps(f"sums{j}") for j in range(2)]
        evT_ps = [st.ps(f"evT_ps{j}") for j in range(2)]
        ew_ps = [st.ps(f"ew_ps{j}") for j in range(2)]
        bank = [st.ps(f"wbank{j}") for j in range(2)]
        w = {"bank": bank, "capped": st.sem("w_capped"), "tables": st.sem("w_tables"), "spread": st.sem("w_spread")}
        setup, held = st.sem("setup"), st.sem("held")
        idx_in, gathered, ev_in, ew_out = st.sem2("idx_in"), st.sem2("gathered"), st.sem2("ev_in"), st.sem2("ew_out")
        hot_ready, sums_ready, added = st.sem("hot_ready"), st.sem("sums_ready"), st.sem("added")
        turned, evT_sb, product, ew_sb = st.sem("turned"), st.sem("evT_sb"), st.sem("product"), st.sem("ew_sb")
        src = a["src_chunks"]
        dve_regs = [nc.vector.alloc_register(f"gin_win{b}") for b in range(BPC)]
        with nc.Block() as block:
            @block.sync
            def _(sp):
                sp.dma_start(wt[:, :], a["Wt"][D:2 * D, :]).then_inc(setup, 16)
                sp.dma_start(g["start"][:, :], first).then_inc(setup, 16)
                sp.wait_ge(setup, 32)
        with nc.Fori(0, span + 1, WIN):
            st.clear(gathers=True)
            next_windows(nc, g, st, w)
            with nc.Block() as block:
                @block.sync
                def _(sp):
                    def step(f, bk):
                        if not f:
                            return
                        c, h, j = f.c, f.h, f.j
                        wait(sp, gathered[j], 16 * COLS * h)
                        sp.dma_start(idx[j][:, :], src[bass.ds(c, 1)].rearrange("a p k -> p (a k)")).then_inc(idx_in[j], 16)
                        wait(sp, turned, QUADS * (c - 1))
                        if not f.last:
                            sp.dma_start(ev[j][:, :, :].rearrange("p (b s) d -> p b s d", s=SUB),
                                         a["edge_attr"][bass.ds(c * CHUNK, CHUNK), :].rearrange(
                                             "(b p s) d -> p b s d", p=P, s=SUB)).then_inc(ev_in[j], 16)
                            return
                        full = a["edge_attr"][c * CHUNK:c * CHUNK + TAIL_BLOCKS * BLOCK, :]
                        sp.dma_start(ev[j][:, 0:TAIL_BLOCKS * SUB, :].rearrange("p (b s) d -> p b s d", s=SUB),
                                     full.rearrange("(b p s) d -> p b s d", p=P, s=SUB)).then_inc(ev_in[j], 16)
                        part = a["edge_attr"][c * CHUNK + TAIL_BLOCKS * BLOCK:E, :]
                        sp.dma_start(ev[j][0:TAIL_PARTS, TAIL_BLOCKS * SUB:(TAIL_BLOCKS + 1) * SUB, :],
                                     part.rearrange("(p s) d -> p s d", s=SUB)).then_inc(ev_in[j], 16)
                    over_chunks(sp, step)

                @block.gpsimd
                def _(gp):
                    def step(f, bk):
                        if f:
                            wait(gp, idx_in[f.j], 16 * (f.h + 1))
                            wait(gp, sums_ready, f.c - 1)
                            hold(gp, g, held, f.c)
                            gather_chunk(gp, idx[f.j], h0, hs[f.j], gathered[f.j])
                    over_chunks(gp, step)

                @block.tensor
                def _(pe):
                    def turn_edges(f, q):
                        if q == 0:
                            wait(pe, ev_in[f.j], 16 * (f.h + 1) + (16 if f.last else 0))
                        wait(pe, evT_sb, QUADS * f.c + q - 1)
                        for k in range(4):
                            mm = pe.transpose(evT_ps[q % 2][:, k * P:(k + 1) * P], ev[f.j][:, 4 * q + k, :], g["ident"][:, :])
                        mm.then_inc(turned, 1)

                    def edge_product(f, q):
                        wait(pe, evT_sb, QUADS * f.c + q + 1)
                        wait(pe, ew_sb, QUADS * f.c + q - 1)
                        for k in range(4):
                            mm = pe.matmul(ew_ps[q % 2][:, k * P:(k + 1) * P], evT[q % 2][:, k * P:(k + 1) * P],
                                           wt[:, :], start=True, stop=True)
                        mm.then_inc(product, 1)

                    def add_rows(bk):
                        c, h, j = bk.c, bk.h, bk.j
                        wait(pe, gathered[j], 16 * COLS * (h + 1))
                        wait(pe, hot_ready, c + 1)
                        wait(pe, added, (c - 1) * BPC)
                        for b in range(BPC):
                            for k in range(b * SUB, (b + 1) * SUB):
                                mm = pe.matmul(sums[j][:, b * WIN:(b + 1) * WIN], hs[j][:, k, :], hot[j][:, k, :],
                                               start=(k % SUB == 0), stop=(k % SUB == SUB - 1))
                        mm.then_inc(sums_ready, 1)

                    def step(f, bk):
                        if f:
                            turn_edges(f, 0)
                            for q in range(1, QUADS):
                                turn_edges(f, q)
                                edge_product(f, q - 1)
                            edge_product(f, QUADS - 1)
                        if bk:
                            add_rows(bk)
                    over_chunks(pe, step)

                @block.scalar
                def _(act):
                    def step(f, bk):
                        def copy_product(q):
                            wait(act, product, QUADS * f.c + q + 1)
                            if q == 0:
                                wait(act, ew_out[f.j], 16 * f.h)
                            act.activation(ews[f.j][:, 4 * q:4 * q + 4, :].rearrange("p k d -> p (k d)"),
                                           ew_ps[q % 2][:, :], ACT.Copy).then_inc(ew_sb, 1)

                        if not f:
                            return
                        for q in range(QUADS):
                            wait(act, turned, QUADS * f.c + q + 1)
                            wait(act, product, QUADS * f.c + q - 1)
                            act.activation(evT[q % 2][:, :], evT_ps[q % 2][:, :], ACT.Copy).then_inc(evT_sb, 1)
                            if q:
                                copy_product(q - 1)
                        copy_product(QUADS - 1)
                        wait(act, ew_sb, QUADS * (f.c + 1))
                        act.dma_start(ew[bass.ds(f.c, 1)].rearrange("a p n -> p (a n)"),
                                      ews[f.j][:, :, :].rearrange("p k d -> p (k d)")).then_inc(ew_out[f.j], 16)
                    over_chunks(act, step)
                    for j in range(2):
                        act.wait_ge(ew_out[j], 16 * (NCH // 2))

                @block.vector
                def _(v):
                    def step(f, bk):
                        if f:
                            wait(v, sums_ready, f.c - 1)
                            onehot_op(v, g, hot[f.j], f.c).then_inc(hot_ready, 1)
                        if bk:
                            load_bases(v, dve_regs, g, bk.c)
                            for b in range(BPC):
                                at = window(v, dve_regs[b])
                                if b == 0:
                                    wait(v, sums_ready, bk.c + 1)
                                wait(v, added, bk.c * BPC + b)
                                v.tensor_tensor(g["acc"][:, bass.ds(at, WIN)], g["acc"][:, bass.ds(at, WIN)],
                                                sums[bk.j][:, b * WIN:(b + 1) * WIN], ALU.add).then_inc(added, 1)
                    over_chunks(v, step)
                    v.wait_ge(added, NCH * BPC)


def node_mid(nc, a, g, res, arow, qk, ck):
    with ExitStack() as ctx:
        st = Stage(nc, ctx, "node_mid")
        W = {k: st.sb("w_" + k, [P, D]) for k in ("W1", "W2", "Wt", "Wq", "WkT", "b2", "bt")}
        col = {k: st.sb("c_" + k, [P, 1]) for k in ("b1", "bq", "bk", "gamma", "beta")}
        tiles = {k: st.two("m_" + k, [P, GT, D]) for k in ("x", "u", "y", "x1", "h2", "r", "hn", "hT", "A", "q", "qk")}
        cb = st.two("m_c", [1, GN])
        m = norm_buffers(st, g)
        pa = [st.ps(f"pa{u}", (P, 1024)) for u in range(2)]
        pb = [st.ps(f"pb{u}", (P, 1024)) for u in range(2)]
        weights_in = st.sem("weights_in")
        x_in, r_out, a_out, q_out = st.sem2("x_in"), st.sem2("r_out"), st.sem2("a_out"), st.sem2("q_out")
        s1 = norm_steps(st, "s1")
        s2 = norm_steps(st, "s2")
        names = ("u_ps", "u_sb", "y_ps", "y_sb", "x1", "h2", "r", "hn", "t_ps", "hT", "a_ps", "a_sb",
                 "q_ps", "q_sb", "k_ps", "c_ps", "k_sb", "c_sb")
        s = {k: st.sem("m_" + k) for k in names}
        st.clear()
        block = ctx.enter_context(nc.Block())
        x_rows = a["x"].rearrange("(g t p) d -> g p t d", t=GT, p=P)
        r_rows = res.rearrange("(g t p) d -> g p t d", t=GT, p=P)
        a_rows = arow.rearrange("(g t p) d -> g p t d", t=GT, p=P)
        n_weights = 12
        flat = lambda t: t[:, :, :].rearrange("p t d -> p (t d)")
        one = lambda rows, G: rows[bass.ds(G, 1)].rearrange("a p t d -> p (a t) d")

        def pairs(eng, steps, behind):
            def both(f, i):
                for u in range(2):
                    f(2 * i + u, i, u)

            def slot(i):
                for f in steps:
                    both(f, i - 1 if f in behind else i)
            for f in steps:
                if f not in behind:
                    both(f, 0)
            slot(1)
            with eng.Fori(2, GROUPS // 2) as i:
                slot(i)
            for f in steps:
                if f in behind:
                    both(f, GROUPS // 2 - 1)

        def next_pair(G):
            return min(G + 3, GROUPS) if isinstance(G, int) else G + 3

        @block.sync
        def _(sp):
            for k in ("W1", "W2", "Wq", "WkT"):
                sp.dma_start(W[k][:, :], a[k]).then_inc(weights_in, 16)
            sp.dma_start(W["Wt"][:, :], a["Wt"][0:D, :]).then_inc(weights_in, 16)
            for k in ("b2", "bt"):
                sp.dma_start(W[k][:, :], a[k].rearrange("(a d) -> a d", a=1).to_broadcast([P, D])).then_inc(weights_in, 16)
            for k in ("b1", "bq", "bk", "gamma", "beta"):
                sp.dma_start(col[k][:, :], a[k].rearrange("(d a) -> d a", a=1)).then_inc(weights_in, 16)

            def load(G, i, u):
                wait(sp, s["x1"], G - 1)
                sp.dma_start(tiles["x"][u][:, :, :], one(x_rows, G)).then_inc(x_in[u], 16)

            def store_r(G, i, u):
                wait(sp, s["r"], G + 1)
                sp.dma_start(one(r_rows, G), tiles["r"][u][:, :, :]).then_inc(r_out[u], 16)

            def store_a(G, i, u):
                wait(sp, s["a_sb"], G + 1)
                sp.dma_start(one(a_rows, G), tiles["A"][u][:, :, :]).then_inc(a_out[u], 16)

            def store_q(G, i, u):
                wait(sp, s["k_sb"], G + 1)
                sp.dma_start(qk[:, bass.ds(G * GN, GN)], flat(tiles["qk"][u])).then_inc(q_out[u], 16)
                wait(sp, s["c_sb"], G + 1)
                sp.dma_start(ck[:, bass.ds(G * GN, GN)], cb[u][:, :]).then_inc(q_out[u], 16)
            pairs(sp, [load, store_a, store_q, store_r], [store_a, store_q])
            for u in range(2):
                sp.wait_ge(r_out[u], 16 * (GROUPS // 2))
                sp.wait_ge(a_out[u], 16 * (GROUPS // 2))
                sp.wait_ge(q_out[u], 32 * (GROUPS // 2))

        @block.tensor
        def _(pe):
            pe.wait_ge(weights_in, 16 * n_weights)

            def halves(out, u, lhsT, rhs, sem):
                for h in range(2):
                    mm = pe.matmul(out[0:lhsT.shape[1], 512 * h:512 * h + HALF], lhsT, rhs(h), start=True, stop=True)
                mm.then_inc(sem, 1)

            def by_tile(out, lhs, rhs, sem):
                for t in range(GT):
                    mm = pe.matmul(out[:, t * P:(t + 1) * P], lhs[:, t, :], rhs[:, :], start=True, stop=True)
                mm.then_inc(sem, 1)

            def first(G, i, u):
                wait(pe, s["c_sb"], G - 3)
                halves(pa[u], u, W["W1"][:, :], lambda h: g["acc"][:, bass.ds(G * GN + h * HALF, HALF)], s["u_ps"])

            def second(G, i, u):
                wait(pe, s["u_sb"], G + 1)
                wait(pe, s["k_sb"], G - 3)
                by_tile(pb[u], tiles["u"][u], W["W2"], s["y_ps"])

            def turn(G, i, u):
                wait(pe, s["hn"], (G + 1) * GT)
                wait(pe, s["u_sb"], next_pair(G))
                wait(pe, s["c_sb"], G - 1)
                for t in range(GT):
                    mm = pe.transpose(pa[u][:, t * P:(t + 1) * P], tiles["hn"][u][:, t, :], g["ident"][:, :])
                mm.then_inc(s["t_ps"], 1)

            def by_source(G, i, u):
                wait(pe, s["hT"], G + 1)
                wait(pe, s["y_sb"], next_pair(G))
                wait(pe, s["k_sb"], G - 1)
                by_tile(pb[u], tiles["hT"][u], W["Wt"], s["a_ps"])
                hT = flat(tiles["hT"][u])
                halves(pa[u], u, W["Wq"][:, :], lambda h: hT[:, h * HALF:(h + 1) * HALF], s["q_ps"])

            def by_target(G, i, u):
                wait(pe, s["q_sb"], G + 1)
                wait(pe, s["a_sb"], G + 1)
                q = flat(tiles["q"][u])
                halves(pb[u], u, W["WkT"][:, :], lambda h: q[:, h * HALF:(h + 1) * HALF], s["k_ps"])
                halves(pa[u], u, col["bk"][:, 0:1], lambda h: q[:, h * HALF:(h + 1) * HALF], s["c_ps"])
            pairs(pe, [first, second, turn, by_source, by_target], [turn, by_source, by_target])

        two = lambda ps, m=P: ps[0:m, :].rearrange("p (h n) -> p h n", h=2)[:, :, 0:HALF]
        twos = lambda t: t.rearrange("p (h n) -> p h n", h=2)

        @block.scalar
        def _(act):
            act.wait_ge(weights_in, 16 * n_weights)

            def relu1(G, i, u):
                wait(act, s["u_ps"], G + 1)
                act.activation(twos(flat(tiles["u"][u])), two(pa[u]), ACT.Relu,
                               bias=col["b1"][:, 0:1]).then_inc(s["u_sb"], 1)

            def root1(G, i, u):
                norm_root(act, m[u], s1, G)

            def root2(G, i, u):
                norm_root(act, m[u], s2, G)

            def norm1(G, i, u):
                wait(act, s1["shift"], G + 1)
                for t in range(GT):
                    act.activation(tiles["h2"][u][:, t, :], tiles["x1"][u][:, t, :], ACT.Relu,
                                   bias=m[u]["shift"][:, t:t + 1], scale=m[u]["rstd"][:, t:t + 1]).then_inc(s["h2"], 1)

            def norm2(G, i, u):
                wait(act, s2["shift"], G + 1)
                wait(act, s["t_ps"], G - 1)
                for t in range(GT):
                    act.activation(tiles["hn"][u][:, t, :], tiles["h2"][u][:, t, :], ACT.Identity,
                                   bias=m[u]["shift"][:, t:t + 1], scale=m[u]["rstd"][:, t:t + 1]).then_inc(s["hn"], 1)

            def affine(G, i, u):
                wait(act, s["t_ps"], G + 1)
                act.activation(flat(tiles["hT"][u]), pa[u][:, 0:GN], ACT.Identity,
                               bias=col["beta"][:, 0:1], scale=col["gamma"][:, 0:1]).then_inc(s["hT"], 1)

            def query(G, i, u):
                wait(act, s["q_ps"], G + 1)
                act.activation(twos(flat(tiles["q"][u])), two(pa[u]), ACT.Identity,
                               bias=col["bq"][:, 0:1]).then_inc(s["q_sb"], 1)

            def key(G, i, u):
                wait(act, q_out[u], 32 * i)
                wait(act, s["k_ps"], G + 1)
                act.activation(twos(flat(tiles["qk"][u])), two(pb[u]), ACT.Copy,
                               scale=float(D) ** -0.5).then_inc(s["k_sb"], 1)
                wait(act, s["c_ps"], G + 1)
                act.activation(twos(cb[u][:, :]), two(pa[u], 1), ACT.Copy,
                               scale=float(D) ** -0.5).then_inc(s["c_sb"], 1)
            pairs(act, [relu1, affine, root1, norm1, query, root2, norm2, key], [affine, query, key])

        @block.vector
        def _(v):
            v.wait_ge(weights_in, 16 * n_weights)

            def residual(G, i, u):
                wait(v, s["y_ps"], G + 1)
                v.tensor_tensor(tiles["y"][u][:, :, :], pb[u][:, 0:GN].rearrange("p (t d) -> p t d", t=GT),
                                W["b2"][:, :].unsqueeze(1).to_broadcast([P, GT, D]), ALU.add).then_inc(s["y_sb"], 1)
                wait(v, x_in[u], 16 * (i + 1))
                wait(v, s["y_sb"], G + 1)
                v.scalar_tensor_tensor(out=flat(tiles["x1"][u]), in0=flat(tiles["y"][u]), scalar=0.0,
                                       in1=flat(tiles["x"][u]), op0=ALU.max, op1=ALU.add).then_inc(s["x1"], 1)
                wait(v, s["x1"], G + 1)
                norm_moments(v, tiles["x1"][u], m[u], s1, G)

            def scales1(G, i, u):
                wait(v, s["hn"], (G - 1) * GT)
                norm_scales(v, m[u], s1, G)

            def scales2(G, i, u):
                norm_scales(v, m[u], s2, G)

            def renorm(G, i, u):
                wait(v, s["h2"], (G + 1) * GT)
                norm_moments(v, tiles["h2"][u], m[u], s2, G)
                wait(v, r_out[u], 16 * i)
                v.tensor_tensor(tiles["r"][u][:, :, :], tiles["x1"][u][:, :, :], tiles["h2"][u][:, :, :],
                                ALU.add).then_inc(s["r"], 1)

            def sources(G, i, u):
                wait(v, a_out[u], 16 * i)
                wait(v, s["a_ps"], G + 1)
                v.tensor_tensor(tiles["A"][u][:, :, :], pb[u][:, 0:GN].rearrange("p (t d) -> p t d", t=GT),
                                W["bt"][:, :].unsqueeze(1).to_broadcast([P, GT, D]), ALU.add).then_inc(s["a_sb"], 1)
            pairs(v, [residual, scales1, sources, renorm, scales2], [sources])


def attention_sweeps(nc, a, g, arow, ew, qk, ck, fades, first, span):
    with ExitStack() as ctx:
        st = Stage(nc, ctx, "attention")
        acc, rows = g["acc"], g["rows"]
        wgt = st.sb("wgt", [P, NBLK * SUB])
        idx = st.two("idx", [P, COLS], I32)
        t = [st.sb(f"t{k}", [P, COLS, D]) for k in range(4)]
        tT = st.two("tT", [P, 512])
        qw, cw = st.two("qw", [P, QSPAN]), st.two("cw", [P, SPAN])
        zeros = st.sb("zeros", [1, QSPAN], BF16)
        miss, attn = st.sb("miss", [P, COLS, WIN]), st.sb("attn", [P, COLS])
        biased, below = st.sb("biased", [P, COLS, WIN]), st.sb("below", [P, COLS, WIN])
        masked = st.two("masked", [P, COLS, WIN])
        xm = st.sb("xm", [P, CW])
        bm = st.sb("bm", [2 * WIN, BPC // 2])
        mnew, mdiff = st.sb("mnew", [1, SPAN]), st.sb("mdiff", [1, SPAN])
        fade_row, fade = st.two("fade_row", [1, SPAN]), st.two("fade", [P, SPAN])
        e_hot = st.two("e_hot", [P, COLS, WIDE])
        tT_ps = [st.ps(f"tT_ps{k}") for k in range(2)]
        sc_ps = st.ps("sc_q", (P, 1024))
        xm_bank, row_bank = st.ps("xm_bank"), st.ps("row_bank")
        sum_ps, tot_ps = st.ps("sum_ps"), st.ps("tot_ps")
        w = {"bank": [xm_bank, row_bank],
             "capped": st.sem("w_capped"), "tables": st.sem("w_tables"), "spread": st.sem("w_spread")}
        setup, held = st.sem("setup"), st.sem("held")
        idx_in, qw_in, fade_in, fade_out = (st.sem2(x) for x in ("idx_in", "qw_in", "fade_in", "fade_out"))
        gathered = [st.sem(f"gathered_{k}") for k in range(4)]
        ew_in = [[st.sem(f"ew_in_{k}_{r}") for r in range(PARTS)] for k in range(4)]
        names = ("t_sb", "tT_ps", "tT_sb", "sc_q", "miss", "biased", "prod", "score", "attn", "masked", "xm", "xm_ps",
                 "bm", "bm_ps", "mold", "raised", "mnew_ps", "mdiff", "kept", "fade", "below", "e_hot",
                 "t_used", "sums_ps", "faded", "added", "sfaded", "sadded")
        s = {k: st.sem("a_" + k) for k in names}
        src = a["src_chunks"]
        sp_reg, last_reg, mid_reg = (e.alloc_register(x) for e, x in (
            (nc.sync, "att_sp"), (nc.vector, "att_last"), (nc.vector, "att_mid")))
        block_regs = [nc.vector.alloc_register(f"att_block{b}") for b in range(BPC)]
        pe_regs = [[nc.tensor.alloc_register(f"att_pe{k}_{b}") for b in range(BPC)] for k in range(4)]
        pc = COLS // PARTS
        half = COLS // 2

        with nc.Block() as block:
            @block.sync
            def _(sp):
                sp.dma_start(wgt[:, :], a["wgt_cols"]).then_inc(setup, 16)
                sp.dma_start(g["start"][:, :], first).then_inc(setup, 16)
                sp.wait_ge(s["added"], 1)
                sp.dma_start(qk[:, NP:NW], acc[:, 0:NW - NP]).then_inc(setup, 16)
                sp.dma_start(ck[:, NP:NW], acc[0:1, 0:NW - NP]).then_inc(setup, 16)
                sp.wait_ge(setup, 64)

            @block.vector
            def _(v):
                v.memset(acc[:, :], 0.0).then_inc(s["added"], 1)
                v.memset(rows[0:1, 0:NW // 2], -BIG).then_inc(s["added"], 1)
                v.memset(zeros[:, :], 0.0).then_inc(s["added"], 1)
                v.wait_ge(s["added"], 3)

            @block.gpsimd
            def _(gp):
                gp.memset(rows[32:33, :], 0.0).then_inc(s["sadded"], 1)
                for j in range(2):
                    gp.wait_ge(s["sadded"], j + 1)
                    gp.memset(e_hot[j][:, :, :], 0.0).then_inc(s["sadded"], 1)
                gp.wait_ge(s["sadded"], 3)
                gp.memset(rows[0:1, NW // 2:NW], -BIG).then_inc(s["sadded"], 1)
                gp.wait_ge(s["sadded"], 4)

        with nc.Fori(0, span + 1, WIN):
            st.clear(gathers=True)
            next_windows(nc, g, st, w)
            with nc.Block() as block:
                @block.sync
                def _(sp):
                    def loads(f):
                        c, h, j = f.c, f.h, f.j
                        load_span(sp, sp_reg, g, c)
                        k, uses = f.two_before
                        wait(sp, gathered[k], 16 * COLS * uses)
                        sp.dma_start(idx[j][:, :], src[bass.ds(c, 1)].rearrange("a p k -> p (a k)")).then_inc(idx_in[j], 16)
                        for r in range(PARTS):
                            wait(sp, s["t_used"], PARTS * (c - 4) + r + 1)
                            sp.dma_start(t[f.k][:, r * pc:(r + 1) * pc, :].rearrange("p k d -> p (k d)"),
                                         ew[bass.ds(c, 1), :, r * pc * D:(r + 1) * pc * D].rearrange(
                                             "a p n -> p (a n)")).then_inc(ew_in[f.k][r], 16)
                        wait(sp, s["sc_q"], QUADS * (c - 1))
                        at = window(sp, sp_reg)
                        sp.dma_start(qw[j][:, :], qk[:, bass.ds(at, QSPAN)]).then_inc(qw_in[j], 16)
                        wait(sp, s["biased"], BPC * (c - 1))
                        at = window(sp, sp_reg)
                        sp.dma_start(cw[j][:, :], ck[:, bass.ds(at, SPAN)].to_broadcast([P, SPAN])).then_inc(qw_in[j], 16)

                    def spread_fade(bk):
                        c, h, j = bk.c, bk.h, bk.j
                        wait(sp, fade_out[j], 16 * (h + 1))
                        sp.dma_start(fade[j][:, :], fades[j:j + 1, :].to_broadcast([P, SPAN])).then_inc(fade_in[j], 16)

                    def step(f, mid, late, last):
                        if f:
                            loads(f)
                        if last:
                            spread_fade(last)
                    over_stages(sp, step)

                @block.gpsimd
                def _(gp):
                    def step(f, bk):
                        if f:
                            wait(gp, idx_in[f.j], 16 * (f.h + 1))
                            for r in range(PARTS):
                                wait(gp, ew_in[f.k][r], 16 * (f.g + 1))
                                hold(gp, g, held, PARTS * f.c + r)
                                gather_chunk(gp, idx[f.j], arow, t[f.k], gathered[f.k], ALU.add,
                                             range(r * pc, (r + 1) * pc))
                    over_chunks(gp, step)

                @block.tensor
                def _(pe):
                    def turn_gelu(f, q):
                        c, h, j = f.c, f.h, f.j
                        wait(pe, s["t_sb"], QUADS * c + q + 1)
                        wait(pe, s["tT_sb"], QUADS * c + q - 1)
                        for k in range(4):
                            mm = pe.transpose(tT_ps[q % 2][:, k * P:(k + 1) * P], t[f.k][:, 4 * q + k, :], g["ident"][:, :])
                        mm.then_inc(s["tT_ps"], 1)

                    def scores(f, q):
                        c, h, j = f.c, f.h, f.j
                        if q == 0:
                            wait(pe, qw_in[j], 32 * (h + 1))
                            wait(pe, s["biased"], BPC * c)
                        wait(pe, s["tT_sb"], QUADS * c + q + 1)
                        for n in range(4 * q, 4 * q + 4):
                            if n % SUB == 0:
                                off = inside(pe, pe_regs[f.k][n // SUB])
                            o = 512 * (n // half) + (n % half) * WIN
                            mm = pe.matmul(sc_ps[:, o:o + WIDE], tT[q % 2][:, (n % 4) * P:(n % 4 + 1) * P],
                                           qw[j][:, bass.ds(off, WIDE)], start=True, stop=True)
                        mm.then_inc(s["sc_q"], 1)

                    def turn_scores(bk):
                        c = bk.c
                        wait(pe, s["xm"], c + 1)
                        wait(pe, s["bm"], c)
                        for k in range(BPC // 2):
                            mm = pe.transpose(xm_bank[0:2 * WIN, k * P:(k + 1) * P], xm[:, k * 2 * WIN:(k + 1) * 2 * WIN],
                                              g["ident"][:, :])
                        mm.then_inc(s["xm_ps"], 1)

                    def spread_maxima(bk):
                        c = bk.c
                        wait(pe, s["bm"], c + 1)
                        wait(pe, s["below"], BPC * c)
                        for k in range(BPC // 2):
                            mm = pe.matmul(row_bank[0:1, k * 2 * WIN:(k + 1) * 2 * WIN], bm[:, k:k + 1],
                                           g["ident"][0:2 * WIN, 0:2 * WIN], start=True, stop=True)
                        mm.then_inc(s["bm_ps"], 1)

                    def spread_running(bk):
                        wait(pe, s["raised"], BPC * (bk.c + 1))
                        pe.matmul(row_bank[:, 0:SPAN], g["ones"][0:1, :], mnew[:, :], start=True, stop=True).then_inc(s["mnew_ps"], 1)

                    def sums(bk):
                        c, h, j = bk.c, bk.h, bk.j
                        wait(pe, s["e_hot"], c + 1)
                        wait(pe, s["added"], c)
                        wait(pe, s["sadded"], c)
                        pe.matmul(sum_ps[:, 0:QSPAN], zeros[0:1, 0:P], zeros[:, :], start=True, stop=True, skip_group_check=True)
                        pe.matmul(tot_ps[0:33, 0:SPAN], zeros[0:1, 0:33], zeros[:, 0:SPAN], start=True, stop=True, skip_group_check=True)
                        for b in range(BPC):
                            off = inside(pe, pe_regs[bk.k][b])
                            for k in range(b * SUB, (b + 1) * SUB):
                                mm = pe.matmul(sum_ps[:, bass.ds(off, WIDE)], t[bk.k][:, k, :], e_hot[j][:, k, :],
                                               start=False, stop=True, skip_group_check=True)
                            if (b + 1) % (BPC // PARTS) == 0:
                                mm.then_inc(s["t_used"], 1)
                        for b in range(BPC):
                            off = inside(pe, pe_regs[bk.k][b])
                            for k in range(b * SUB, (b + 1) * SUB):
                                mm = pe.matmul(tot_ps[0:33, bass.ds(off, WIN)], g["ones"][:, 0:33], e_hot[j][:, k, 0:WIN],
                                               start=False, stop=True, skip_group_check=True)
                        mm.then_inc(s["sums_ps"], 1)

                    def step(f, mid, late, last):
                        if f:
                            load_offsets(pe, pe_regs[f.k], g, f.c)
                            turn_gelu(f, 0)
                        if mid:
                            turn_scores(mid)
                        if f:
                            turn_gelu(f, 1)
                            scores(f, 0)
                        if mid:
                            spread_maxima(mid)
                        if f:
                            turn_gelu(f, 2)
                            scores(f, 1)
                            turn_gelu(f, 3)
                            scores(f, 2)
                            scores(f, 3)
                        if mid:
                            spread_running(mid)
                        if late:
                            sums(late)
                    over_stages(pe, step)

                @block.scalar
                def _(act):
                    def gelu(f, q):
                        if q == 0:
                            wait(act, gathered[f.k], 16 * COLS * (f.g + 1))
                        x = t[f.k][:, 4 * q:4 * q + 4, :]
                        act.activation(x, x, ACT.Gelu).then_inc(s["t_sb"], 1)

                    def copy_tT(f, q):
                        wait(act, s["tT_ps"], QUADS * f.c + q + 1)
                        wait(act, s["sc_q"], QUADS * f.c + q - 1)
                        act.activation(tT[q % 2][:, :], tT_ps[q % 2][:, :], ACT.Copy).then_inc(s["tT_sb"], 1)

                    def exps(bk):
                        c, h, j = bk.c, bk.h, bk.j
                        wait(act, s["mdiff"], c + 1)
                        wait(act, fade_out[j], 16 * h)
                        act.activation(fade_row[j][:, :], mdiff[:, :], ACT.Exp).then_inc(s["fade"], 1)
                        wait(act, s["below"], BPC * (c + 1))
                        wait(act, s["sums_ps"], c - 1)
                        act.activation(e_hot[j][:, :, 0:WIN], below[:, :, :], ACT.Exp).then_inc(s["e_hot"], 1)
                        wait(act, s["fade"], c + 1)
                        wait(act, fade_in[j], 16 * h)
                        wait(act, s["sadded"], c - 1)
                        act.dma_start(fades[j:j + 1, :], fade_row[j][:, :]).then_inc(fade_out[j], 16)

                    def step(f, mid, late, last):
                        if f:
                            gelu(f, 0)
                            gelu(f, 1)
                            copy_tT(f, 0)
                            gelu(f, 2)
                            copy_tT(f, 1)
                            gelu(f, 3)
                            copy_tT(f, 2)
                            copy_tT(f, 3)
                        if mid:
                            exps(mid)
                    over_stages(act, step)

                @block.vector
                def _(v):
                    by_b = lambda x: x.rearrange("p (b s) n -> p b s n", s=SUB)
                    win3 = lambda x: x.rearrange("p (b n) -> p b n", n=WIN)

                    def misses(f):
                        wait(v, s["masked"], f.c)
                        onehot_op(v, g, miss, f.c, ALU.not_equal).then_inc(s["miss"], 1)

                    def score(f):
                        c, h, j = f.c, f.h, f.j
                        load_offsets(v, block_regs, g, c)
                        for b in range(BPC):
                            off = inside(v, block_regs[b])
                            if b == 0:
                                wait(v, qw_in[j], 32 * (h + 1))
                                wait(v, s["score"], c)
                            if b % (BPC // 2) == 0:
                                wait(v, s["sc_q"], QUADS * c + (QUADS // 2 if b == 0 else QUADS))
                            cols, o = slice(b * SUB, (b + 1) * SUB), 512 * (b * SUB // half) + b * SUB % half * WIN
                            v.tensor_tensor(biased[:, cols, :], sc_ps[:, o:o + SUB * WIN].rearrange("p (s n) -> p s n", s=SUB),
                                            cw[j][:, bass.ds(off, WIN)].unsqueeze(1).to_broadcast([P, SUB, WIN]),
                                            ALU.add).then_inc(s["biased"], 1)
                        wait(v, s["miss"], c + 1)
                        wait(v, s["biased"], BPC * (c + 1))
                        v.scalar_tensor_tensor(biased[:, :, :], miss[:, :, :], 0.0, biased[:, :, :],
                                               ALU.is_equal, ALU.mult).then_inc(s["prod"], 1)
                        wait(v, s["prod"], c + 1)
                        v.tensor_reduce(attn[:, :], biased[:, :, :], AX.X, ALU.add).then_inc(s["score"], 1)
                        wait(v, s["score"], c + 1)
                        v.tensor_tensor(attn[:, :], attn[:, :], wgt[:, bass.ds(c * COLS, COLS)],
                                        ALU.mult).then_inc(s["attn"], 1)
                        wait(v, s["attn"], c + 1)
                        wait(v, s["below"], BPC * (c - 1))
                        v.scalar_tensor_tensor(masked[j][:, :, :], miss[:, :, :], -FAR,
                                               attn[:, :].unsqueeze(2).to_broadcast([P, COLS, WIN]),
                                               ALU.mult, ALU.add).then_inc(s["masked"], 1)
                        wait(v, s["masked"], c + 1)
                        wait(v, s["xm_ps"], c)
                        x = by_b(masked[j][:, :, :])
                        v.tensor_tensor(win3(xm[:, :]), x[:, :, 0, :], x[:, :, 1, :], ALU.max).then_inc(s["xm"], 1)

                    def add_sums(last):
                        c, h, j = last.c, last.h, last.j
                        load_span(v, last_reg, g, c)
                        at = window(v, last_reg)
                        nodes, total = acc[:, bass.ds(at, SPAN)], rows[32:33, bass.ds(at, SPAN)]
                        wait(v, fade_in[j], 16 * (h + 1))
                        wait(v, s["added"], c)
                        v.tensor_tensor(nodes, nodes, fade[j][:, :], ALU.mult).then_inc(s["faded"], 1)
                        wait(v, s["sadded"], c)
                        v.tensor_tensor(total, total, fade[j][32:33, :], ALU.mult).then_inc(s["sfaded"], 1)
                        wait(v, s["sums_ps"], c + 1)
                        wait(v, s["faded"], c + 1)
                        v.tensor_tensor(nodes, nodes, sum_ps[:, 0:SPAN], ALU.add).then_inc(s["added"], 1)
                        wait(v, s["sfaded"], c + 1)
                        v.tensor_tensor(total, total, tot_ps[32:33, 0:SPAN], ALU.add).then_inc(s["sadded"], 1)

                    def block_maxima(bk):
                        c = bk.c
                        wait(v, s["xm_ps"], c + 1)
                        wait(v, s["bm_ps"], c)
                        v.tensor_reduce(bm[:, :], xm_bank[0:2 * WIN, :].rearrange("p (k e) -> p k e", e=P), AX.X,
                                        ALU.max).then_inc(s["bm"], 1)

                    def raise_maxima(bk):
                        c = bk.c
                        load_span(v, mid_reg, g, c)
                        top = rows[0:1, bass.ds(window(v, mid_reg), SPAN)]
                        load_offsets(v, block_regs, g, c)
                        wait(v, s["kept"], c)
                        wait(v, s["mnew_ps"], c)
                        v.tensor_tensor(mnew[:, :], top, top, ALU.max).then_inc(s["mold"], 1)
                        for b in range(BPC):
                            some = mnew[0:1, bass.ds(inside(v, block_regs[b]), WIN)]
                            if b == 0:
                                wait(v, s["mold"], c + 1)
                                wait(v, s["bm_ps"], c + 1)
                            wait(v, s["raised"], BPC * c + b)
                            v.tensor_tensor(some, some, row_bank[0:1, b * WIN:(b + 1) * WIN], ALU.max).then_inc(s["raised"], 1)
                        wait(v, s["raised"], BPC * (c + 1))
                        wait(v, s["fade"], c)
                        v.tensor_tensor(mdiff[:, :], top, mnew[:, :], ALU.subtract).then_inc(s["mdiff"], 1)
                        wait(v, s["mdiff"], c + 1)
                        v.tensor_tensor(top, top, mnew[:, :], ALU.max).then_inc(s["kept"], 1)

                    def below_maxima(bk):
                        c, h, j = bk.c, bk.h, bk.j
                        for b in range(BPC):
                            off = inside(v, block_regs[b])
                            if b == 0:
                                wait(v, s["mnew_ps"], c + 1)
                                wait(v, s["e_hot"], c)
                            cols = slice(b * SUB, (b + 1) * SUB)
                            v.tensor_tensor(below[:, cols, :], masked[j][:, cols, :],
                                            row_bank[:, bass.ds(off, WIN)].unsqueeze(1).to_broadcast([P, SUB, WIN]),
                                            ALU.subtract).then_inc(s["below"], 1)

                    def step(f, mid, late, last):
                        if last:
                            add_sums(last)
                        if f:
                            misses(f)
                        if mid:
                            block_maxima(mid)
                            raise_maxima(mid)
                            below_maxima(mid)
                        if f:
                            score(f)
                    over_stages(v, step)
                    v.wait_ge(s["added"], NCH)
                    v.wait_ge(s["sadded"], NCH)
                    v.wait_ge(s["kept"], NCH)


def node_end(nc, a, g, res):
    with ExitStack() as ctx:
        st = Stage(nc, ctx, "node_end")
        wv, bv = st.sb("wv", [P, D]), st.sb("bv_rows", [P, D])
        tc, gl, rr, oo = (st.two("e_" + k, [P, GT, D]) for k in ("tc", "gl", "rr", "oo"))
        sr = st.two("e_s", [1, GN])
        num = st.two("e_num", [P, GT, D])
        total, den, rden = st.two("e_total", [P, GT]), st.two("e_den", [P, GT]), st.two("e_rden", [P, GT])
        pv = [st.ps(f"pv{u}", (P, 1024)) for u in range(2)]
        pd = [st.ps(f"pd{u}") for u in range(2)]
        names = ("tc", "sr", "pv", "total", "den", "rden", "num", "gl", "oo")
        s = {k: st.sem("e_" + k) for k in names}
        weights_in, r_in, o_out = st.sem("ew_in"), st.sem2("er_in"), st.sem2("eo_out")
        r_rows = res.rearrange("(g t p) d -> g p t d", t=GT, p=P)
        o_rows = a["out"].rearrange("(g t p) d -> g p t d", t=GT, p=P)
        one = lambda rows, G: rows[bass.ds(G, 1)].rearrange("a p t d -> p (a t) d")
        st.clear()
        block = ctx.enter_context(nc.Block())

        def pairs(eng, steps):
            for f in steps:
                for u in range(2):
                    f(u, 0, u)
            with eng.Fori(1, GROUPS // 2) as i:
                for f in steps:
                    for u in range(2):
                        f(2 * i + u, i, u)

        @block.sync
        def _(sp):
            sp.dma_start(wv[:, :], a["Wv"]).then_inc(weights_in, 16)
            sp.dma_start(bv[:, :], a["bv"].rearrange("(a d) -> a d", a=1).to_broadcast([P, D])).then_inc(weights_in, 16)

            def load(G, i, u):
                wait(sp, s["oo"], G - 1)
                sp.dma_start(rr[u][:, :, :], one(r_rows, G)).then_inc(r_in[u], 16)

            def store(G, i, u):
                wait(sp, s["oo"], G + 1)
                sp.dma_start(one(o_rows, G), oo[u][:, :, :]).then_inc(o_out[u], 16)
            pairs(sp, [load, store])
            for u in range(2):
                sp.wait_ge(o_out[u], 16 * (GROUPS // 2))

        @block.scalar
        def _(act):
            def take(G, i, u):
                wait(act, s["pv"], G - 1)
                act.activation(tc[u][:, :, :].rearrange("p t d -> p (t d)"), g["acc"][:, bass.ds(G * GN, GN)],
                               ACT.Copy).then_inc(s["tc"], 1)
                act.activation(sr[u][0:1, :], g["rows"][32:33, bass.ds(G * GN, GN)], ACT.Copy).then_inc(s["sr"], 1)

            def gelu(G, i, u):
                wait(act, s["num"], (G + 1) * GT)
                wait(act, s["rden"], G + 1)
                wait(act, s["oo"], G - 1)
                for t in range(GT):
                    act.activation(gl[u][:, t, :], num[u][:, t, :], ACT.Gelu,
                                   scale=rden[u][:, t:t + 1]).then_inc(s["gl"], 1)
            pairs(act, [take, gelu])

        @block.tensor
        def _(pe):
            pe.wait_ge(weights_in, 32)

            def products(G, i, u):
                wait(pe, s["tc"], G + 1)
                wait(pe, s["sr"], G + 1)
                wait(pe, s["num"], (G - 1) * GT)
                wait(pe, s["total"], G - 1)
                for t in range(GT):
                    pe.matmul(pv[u][:, t * P:(t + 1) * P], tc[u][:, t, :], wv[:, :], start=True, stop=True)
                for t in range(GT):
                    mm = pe.matmul(pd[u][:, t:t + 1], sr[u][0:1, t * P:(t + 1) * P], g["ones"][0:1, 0:1],
                                   start=True, stop=True)
                mm.then_inc(s["pv"], 1)
            pairs(pe, [products])

        @block.vector
        def _(v):
            def inverse(G, i, u):
                wait(v, s["gl"], (G - 1) * GT)
                wait(v, s["pv"], G + 1)
                wait(v, s["num"], (G - 1) * GT)
                v.tensor_copy(total[u][:, :], pd[u][:, 0:GT]).then_inc(s["total"], 1)
                wait(v, s["total"], G + 1)
                v.tensor_scalar(den[u][:, :], total[u][:, :], SM_EPS, None, ALU.add).then_inc(s["den"], 1)
                wait(v, s["den"], G + 1)
                v.reciprocal(rden[u][:, :], den[u][:, :]).then_inc(s["rden"], 1)

            def bias(G, i, u):
                for t in range(GT):
                    v.scalar_tensor_tensor(num[u][:, t, :], bv[:, :], total[u][:, t:t + 1], pv[u][:, t * P:(t + 1) * P],
                                           ALU.mult, ALU.add).then_inc(s["num"], 1)

            def finish(G, i, u):
                wait(v, s["gl"], (G + 1) * GT)
                wait(v, r_in[u], 16 * (i + 1))
                wait(v, o_out[u], 16 * i)
                v.tensor_tensor(oo[u][:, :, :], gl[u][:, :, :], rr[u][:, :, :], ALU.add).then_inc(s["oo"], 1)
            v.wait_ge(weights_in, 32)
            pairs(v, [inverse, bias, finish])


def kernel(x, src, dst, edge_attr_128, edge_weight1, L0_gnn_eps, L0_gnn_W1, L0_gnn_b1, L0_gnn_W2, L0_gnn_b2,
           L1_gnn_gamma, L1_gnn_beta, L1_gnn_Wt, L1_gnn_bt, L1_gnn_Wq, L1_gnn_bq, L1_gnn_Wk, L1_gnn_bk,
           L1_gnn_Wv, L1_gnn_bv):
    import concourse.bacc as bacc
    from concourse.bass_utils import run_bass_kernel_spmd

    pad = NCH * CHUNK - E

    def chunked(v, fill):
        v = np.concatenate([np.asarray(v).reshape(-1), np.full(pad, fill, np.asarray(v).dtype)])
        return v.reshape(NCH, BPC, P, SUB).transpose(0, 2, 1, 3)

    dst_pad = np.concatenate([np.asarray(dst), np.full(pad, N, np.asarray(dst).dtype)])
    cols = lambda v: np.ascontiguousarray(v.transpose(1, 0, 2, 3).reshape(P, NBLK * SUB))
    arrays = {
        "x": np.pad(np.asarray(x), ((0, NP - N), (0, 0))),
        "src_chunks": np.ascontiguousarray(chunked(src, 0).reshape(NCH, P, COLS)),
        "dst_cols": cols(chunked(dst, N)),
        "dst_blocks": dst_pad.reshape(NBLK, BLOCK),
        "wgt_cols": cols(chunked(edge_weight1, 0)),
        "edge_attr": np.asarray(edge_attr_128),
        "eps": np.asarray(L0_gnn_eps).reshape(1, 1),
        "W1": L0_gnn_W1, "b1": L0_gnn_b1, "W2": L0_gnn_W2, "b2": L0_gnn_b2,
        "gamma": L1_gnn_gamma, "beta": L1_gnn_beta, "Wt": L1_gnn_Wt, "bt": L1_gnn_bt,
        "Wq": L1_gnn_Wq, "bq": L1_gnn_bq, "WkT": np.ascontiguousarray(np.asarray(L1_gnn_Wk).T), "bk": L1_gnn_bk,
        "Wv": L1_gnn_Wv, "bv": L1_gnn_bv,
    }
    arrays = {k: np.ascontiguousarray(v) for k, v in arrays.items()}
    nc = bacc.Bacc("TRN2", target_bir_lowering=False, num_devices=1)
    a = {k: nc.dram_tensor("in_" + k, list(v.shape), mybir.dt.from_np(v.dtype), kind="ExternalInput").ap()
         for k, v in arrays.items()}
    a["out"] = nc.dram_tensor("out_rows", [NP, D], F32, kind="ExternalOutput").ap()
    build_gnn(nc, a)
    r = run_bass_kernel_spmd(nc, [{"in_" + k: v for k, v in arrays.items()}], core_ids=[0])
    return r.results[0]["out_rows"][:N]
```
